# Optimizing a Trainium2 kernel written in Bass

```python
import numpy as np
import jax
import jax.numpy as jnp

def _softmax(x, axis=-1):
    return jax.nn.softmax(x, axis=axis)

def _gelu(x):
    return jax.nn.gelu(x, approximate=True)

def _silu(x):
    return jax.nn.silu(x)

def _sigmoid(x):
    return jax.nn.sigmoid(x)

def _layernorm(x, axis=-1, eps=1e-05):
    m = jnp.mean(x, axis=axis, keepdims=True)
    v = jnp.var(x, axis=axis, keepdims=True)
    return (x - m) / jnp.sqrt(v + eps)

def _scatter_add(tgt, idx, src, axis=0):
    return tgt.at[idx].add(src)

def _segment_sum(src, seg, n):
    return jax.ops.segment_sum(src, seg, n)
kernel_name = 'mk_xattn_seq_d2_seqx_r8_9898d8'

def setup_inputs(seed: int=0):
    np.random.seed(seed)
    _w = jnp.asarray

    def _rec_inputs():
        import jax
        import jax.numpy as jnp
        _rk = jax.random.key(seed)
        x = -0.0001548 + 1 * jax.random.normal(jax.random.fold_in(_rk, 1), (8, 256, 160), jnp.float32)
        _lenS = 256 - jax.random.randint(jax.random.fold_in(_rk, 7), (8,), 0, max(1, 256 // 4) + 1, jnp.int32)
        _lenS2 = 256 - jax.random.randint(jax.random.fold_in(_rk, 8), (8,), 0, max(1, 256 // 4) + 1, jnp.int32)
        _ctx_768P = jax.random.normal(jax.random.fold_in(_rk, 11), (8, 16, 96), jnp.float32)
        _ctx_768c = jax.random.dirichlet(jax.random.fold_in(_rk, 511), 0.3 * jnp.ones((16,), jnp.float32), (8, 256))
        _ctx_768t = jnp.einsum('bsk,bkd->bsd', _ctx_768c, _ctx_768P)
        _ctx_768t = _ctx_768t * jax.lax.rsqrt(jnp.mean(jnp.square(_ctx_768t)) + 1e-12) * 0.953939
        ctx_768 = 0.000651243 + 0.998673 * (_ctx_768t + 0.3 * jax.random.normal(jax.random.fold_in(_rk, 611), (8, 256, 96), jnp.float32))
        return (x, ctx_768)
    x, ctx_768 = _rec_inputs()

    def _L0_xattn_setup():
        import jax, jax.numpy as jnp
        import numpy as np
        DIM, HEADS, DHEAD, CTX_DIM, DFF = (160, 20, 64, 96, 640)
        EPS = 1e-05
        SCALE = DHEAD ** (-0.5)

        def layer_norm(x, g, b):
            mu = jnp.mean(x, axis=-1, keepdims=True)
            var = jnp.mean(jnp.square(x - mu), axis=-1, keepdims=True)
            return (x - mu) * jax.lax.rsqrt(var + EPS) * g + b

        def cross_attention(x, ctx, wq, wk, wv, wo, bo):
            B, N, _ = x.shape
            M = ctx.shape[1]
            q = jnp.einsum('bne,ef->bnf', x, wq).reshape(B, N, HEADS, DHEAD).transpose(0, 2, 1, 3)
            k = jnp.einsum('bme,ef->bmf', ctx, wk).reshape(B, M, HEADS, DHEAD).transpose(0, 2, 1, 3)
            v = jnp.einsum('bme,ef->bmf', ctx, wv).reshape(B, M, HEADS, DHEAD).transpose(0, 2, 1, 3)
            scores = jnp.einsum('bhnd,bhmd->bhnm', q, k) * SCALE
            attn = jax.nn.softmax(scores, axis=-1)
            out = jnp.einsum('bhnm,bhmd->bhnd', attn, v)
            out = out.transpose(0, 2, 1, 3).reshape(B, N, HEADS * DHEAD)
            return jnp.einsum('bnf,fe->bne', out, wo) + bo

        def geglu_ff(x, w1, b1, w2, b2):
            h = jnp.einsum('bne,ef->bnf', x, w1) + b1
            a, gate = (h[..., :DFF], h[..., DFF:])
            h = a * jax.nn.gelu(gate)
            return jnp.einsum('bnf,fe->bne', h, w2) + b2

        def block_forward(x, context, g1, be1, wq1, wk1, wv1, wo1, bo1, g2, be2, wq2, wk2, wv2, wo2, bo2, g3, be3, w_ff1, b_ff1, w_ff2, b_ff2):
            x = cross_attention(layer_norm(x, g1, be1), layer_norm(x, g1, be1), wq1, wk1, wv1, wo1, bo1) + x
            x = cross_attention(layer_norm(x, g2, be2), context, wq2, wk2, wv2, wo2, bo2) + x
            return geglu_ff(layer_norm(x, g3, be3), w_ff1, b_ff1, w_ff2, b_ff2) + x
        key = jax.random.key(seed)
        ks = jax.random.split(key, 20)
        s = 0.02
        inner = HEADS * DHEAD
        return {'x': jax.random.normal(ks[0], (4, 128, DIM), jnp.float32), 'context': jax.random.normal(ks[1], (4, 77, CTX_DIM), jnp.float32), 'g1': jnp.ones((DIM,), jnp.float32), 'be1': jnp.zeros((DIM,), jnp.float32), 'wq1': jax.random.normal(ks[2], (DIM, inner), jnp.float32) * s, 'wk1': jax.random.normal(ks[3], (DIM, inner), jnp.float32) * s, 'wv1': jax.random.normal(ks[4], (DIM, inner), jnp.float32) * s, 'wo1': jax.random.normal(ks[5], (inner, DIM), jnp.float32) * s, 'bo1': jnp.zeros((DIM,), jnp.float32), 'g2': jnp.ones((DIM,), jnp.float32), 'be2': jnp.zeros((DIM,), jnp.float32), 'wq2': jax.random.normal(ks[6], (DIM, inner), jnp.float32) * s, 'wk2': jax.random.normal(ks[7], (CTX_DIM, inner), jnp.float32) * s, 'wv2': jax.random.normal(ks[8], (CTX_DIM, inner), jnp.float32) * s, 'wo2': jax.random.normal(ks[9], (inner, DIM), jnp.float32) * s, 'bo2': jnp.zeros((DIM,), jnp.float32), 'g3': jnp.ones((DIM,), jnp.float32), 'be3': jnp.zeros((DIM,), jnp.float32), 'w_ff1': jax.random.normal(ks[10], (DIM, 2 * DFF), jnp.float32) * s, 'b_ff1': jnp.zeros((2 * DFF,), jnp.float32), 'w_ff2': jax.random.normal(ks[11], (DFF, DIM), jnp.float32) * s, 'b_ff2': jnp.zeros((DIM,), jnp.float32)}
    _L0_xattn_all = _L0_xattn_setup()
    _L0_xattn_in = {k: v for k, v in _L0_xattn_all.items() if k in ('g1', 'be1', 'wq1', 'wk1', 'wv1', 'wo1', 'bo1', 'g2', 'be2', 'wq2', 'wk2', 'wv2', 'wo2', 'bo2', 'g3', 'be3', 'w_ff1', 'b_ff1', 'w_ff2', 'b_ff2')}
    del _L0_xattn_all

    def _L1_xattn_setup():
        import jax, jax.numpy as jnp
        import numpy as np
        HEADS = 8
        NUM_TOKENS = 4
        CROSS_ATTENTION_DIM = 96

        def _mha(q, k, v, heads=HEADS):
            B, Sq, H = q.shape
            Sk = k.shape[1]
            d = H // heads
            qh = q.reshape(B, Sq, heads, d).transpose(0, 2, 1, 3)
            kh = k.reshape(B, Sk, heads, d).transpose(0, 2, 1, 3)
            vh = v.reshape(B, Sk, heads, d).transpose(0, 2, 1, 3)
            scores = jnp.einsum('bhqd,bhkd->bhqk', qh, kh) * jnp.asarray(d, q.dtype) ** (-0.5)
            probs = jax.nn.softmax(scores, axis=-1)
            out = jnp.einsum('bhqk,bhkd->bhqd', probs, vh)
            return out.transpose(0, 2, 1, 3).reshape(B, Sq, H)
        key = jax.random.key(seed)
        ks = jax.random.split(key, 10)
        B, S, H, CAD, T = (4, 128, 160, CROSS_ATTENTION_DIM, NUM_TOKENS)
        sc = 0.02
        return {'hidden_states': jax.random.normal(ks[0], (B, S, H), jnp.float32), 'encoder_hidden_states': jax.random.normal(ks[1], (B, 77 + T, CAD), jnp.float32), 'Wq': jax.random.normal(ks[2], (H, H), jnp.float32) * sc, 'Wk': jax.random.normal(ks[3], (CAD, H), jnp.float32) * sc, 'Wv': jax.random.normal(ks[4], (CAD, H), jnp.float32) * sc, 'Wq_ca': jax.random.normal(ks[5], (T, H), jnp.float32) * sc, 'Wk_ca': jax.random.normal(ks[6], (CAD, H), jnp.float32) * sc, 'Wv_ca': jax.random.normal(ks[7], (CAD, H), jnp.float32) * sc, 'Wout': jax.random.normal(ks[8], (H, H), jnp.float32) * sc, 'b_out': jnp.zeros((H,), jnp.float32)}
    _L1_xattn_all = _L1_xattn_setup()
    _L1_xattn_in = {k: v for k, v in _L1_xattn_all.items() if k in ('Wq', 'Wk', 'Wv', 'Wq_ca', 'Wk_ca', 'Wv_ca', 'Wout', 'b_out')}
    del _L1_xattn_all
    return {'x': x, 'ctx_768': ctx_768, 'L0_xattn_g1': _L0_xattn_in['g1'], 'L0_xattn_be1': _L0_xattn_in['be1'], 'L0_xattn_wq1': _L0_xattn_in['wq1'], 'L0_xattn_wk1': _L0_xattn_in['wk1'], 'L0_xattn_wv1': _L0_xattn_in['wv1'], 'L0_xattn_wo1': _L0_xattn_in['wo1'], 'L0_xattn_bo1': _L0_xattn_in['bo1'], 'L0_xattn_g2': _L0_xattn_in['g2'], 'L0_xattn_be2': _L0_xattn_in['be2'], 'L0_xattn_wq2': _L0_xattn_in['wq2'], 'L0_xattn_wk2': _L0_xattn_in['wk2'], 'L0_xattn_wv2': _L0_xattn_in['wv2'], 'L0_xattn_wo2': _L0_xattn_in['wo2'], 'L0_xattn_bo2': _L0_xattn_in['bo2'], 'L0_xattn_g3': _L0_xattn_in['g3'], 'L0_xattn_be3': _L0_xattn_in['be3'], 'L0_xattn_w_ff1': _L0_xattn_in['w_ff1'], 'L0_xattn_b_ff1': _L0_xattn_in['b_ff1'], 'L0_xattn_w_ff2': _L0_xattn_in['w_ff2'], 'L0_xattn_b_ff2': _L0_xattn_in['b_ff2'], 'L1_xattn_Wq': _L1_xattn_in['Wq'], 'L1_xattn_Wk': _L1_xattn_in['Wk'], 'L1_xattn_Wv': _L1_xattn_in['Wv'], 'L1_xattn_Wq_ca': _L1_xattn_in['Wq_ca'], 'L1_xattn_Wk_ca': _L1_xattn_in['Wk_ca'], 'L1_xattn_Wv_ca': _L1_xattn_in['Wv_ca'], 'L1_xattn_Wout': _L1_xattn_in['Wout'], 'L1_xattn_b_out': _L1_xattn_in['b_out']}

def reference(x, ctx_768, L0_xattn_g1, L0_xattn_be1, L0_xattn_wq1, L0_xattn_wk1, L0_xattn_wv1, L0_xattn_wo1, L0_xattn_bo1, L0_xattn_g2, L0_xattn_be2, L0_xattn_wq2, L0_xattn_wk2, L0_xattn_wv2, L0_xattn_wo2, L0_xattn_bo2, L0_xattn_g3, L0_xattn_be3, L0_xattn_w_ff1, L0_xattn_b_ff1, L0_xattn_w_ff2, L0_xattn_b_ff2, L1_xattn_Wq, L1_xattn_Wk, L1_xattn_Wv, L1_xattn_Wq_ca, L1_xattn_Wk_ca, L1_xattn_Wv_ca, L1_xattn_Wout, L1_xattn_b_out):
    import jax
    import jax.numpy as jnp

    def _L0_xattn_ref(x, context, g1, be1, wq1, wk1, wv1, wo1, bo1, g2, be2, wq2, wk2, wv2, wo2, bo2, g3, be3, w_ff1, b_ff1, w_ff2, b_ff2):
        import jax, jax.numpy as jnp
        import numpy as np
        DIM, HEADS, DHEAD, CTX_DIM, DFF = (160, 20, 64, 96, 640)
        EPS = 1e-05
        SCALE = DHEAD ** (-0.5)

        def layer_norm(x, g, b):
            mu = jnp.mean(x, axis=-1, keepdims=True)
            var = jnp.mean(jnp.square(x - mu), axis=-1, keepdims=True)
            return (x - mu) * jax.lax.rsqrt(var + EPS) * g + b

        def cross_attention(x, ctx, wq, wk, wv, wo, bo):
            B, N, _ = x.shape
            M = ctx.shape[1]
            q = jnp.einsum('bne,ef->bnf', x, wq).reshape(B, N, HEADS, DHEAD).transpose(0, 2, 1, 3)
            k = jnp.einsum('bme,ef->bmf', ctx, wk).reshape(B, M, HEADS, DHEAD).transpose(0, 2, 1, 3)
            v = jnp.einsum('bme,ef->bmf', ctx, wv).reshape(B, M, HEADS, DHEAD).transpose(0, 2, 1, 3)
            scores = jnp.einsum('bhnd,bhmd->bhnm', q, k) * SCALE
            attn = jax.nn.softmax(scores, axis=-1)
            out = jnp.einsum('bhnm,bhmd->bhnd', attn, v)
            out = out.transpose(0, 2, 1, 3).reshape(B, N, HEADS * DHEAD)
            return jnp.einsum('bnf,fe->bne', out, wo) + bo

        def geglu_ff(x, w1, b1, w2, b2):
            h = jnp.einsum('bne,ef->bnf', x, w1) + b1
            a, gate = (h[..., :DFF], h[..., DFF:])
            h = a * jax.nn.gelu(gate)
            return jnp.einsum('bnf,fe->bne', h, w2) + b2

        def block_forward(x, context, g1, be1, wq1, wk1, wv1, wo1, bo1, g2, be2, wq2, wk2, wv2, wo2, bo2, g3, be3, w_ff1, b_ff1, w_ff2, b_ff2):
            x = cross_attention(layer_norm(x, g1, be1), layer_norm(x, g1, be1), wq1, wk1, wv1, wo1, bo1) + x
            x = cross_attention(layer_norm(x, g2, be2), context, wq2, wk2, wv2, wo2, bo2) + x
            return geglu_ff(layer_norm(x, g3, be3), w_ff1, b_ff1, w_ff2, b_ff2) + x
        return block_forward(x, context, g1, be1, wq1, wk1, wv1, wo1, bo1, g2, be2, wq2, wk2, wv2, wo2, bo2, g3, be3, w_ff1, b_ff1, w_ff2, b_ff2)

    def _L1_xattn_ref(hidden_states, encoder_hidden_states, Wq, Wk, Wv, Wq_ca, Wk_ca, Wv_ca, Wout, b_out):
        import jax, jax.numpy as jnp
        import numpy as np
        HEADS = 8
        NUM_TOKENS = 4
        CROSS_ATTENTION_DIM = 96

        def _mha(q, k, v, heads=HEADS):
            B, Sq, H = q.shape
            Sk = k.shape[1]
            d = H // heads
            qh = q.reshape(B, Sq, heads, d).transpose(0, 2, 1, 3)
            kh = k.reshape(B, Sk, heads, d).transpose(0, 2, 1, 3)
            vh = v.reshape(B, Sk, heads, d).transpose(0, 2, 1, 3)
            scores = jnp.einsum('bhqd,bhkd->bhqk', qh, kh) * jnp.asarray(d, q.dtype) ** (-0.5)
            probs = jax.nn.softmax(scores, axis=-1)
            out = jnp.einsum('bhqk,bhkd->bhqd', probs, vh)
            return out.transpose(0, 2, 1, 3).reshape(B, Sq, H)
        residual = hidden_states
        unet_size = residual.shape[1]
        end_pos = encoder_hidden_states.shape[1] - NUM_TOKENS
        enc = encoder_hidden_states[:, :end_pos, :]
        ca = encoder_hidden_states[:, end_pos:, :]
        query = hidden_states @ Wq
        keyt = enc @ Wk
        valt = enc @ Wv
        hs = _mha(query, keyt, valt)
        ca_q1 = jnp.einsum('btc,th->bch', ca, Wq_ca)
        indices = np.linspace(0, CROSS_ATTENTION_DIM - 1, unet_size).astype(np.int64)
        ca_q1 = ca_q1[:, indices, :]
        ca_hs1 = _mha(ca_q1, residual, residual)
        ca_q2 = ca_hs1 @ Wq
        ca_k2 = ca @ Wk_ca
        ca_v2 = ca @ Wv_ca
        ca_hs2 = _mha(ca_q2, ca_k2, ca_v2)
        out = hs + ca_hs2
        out = out @ Wout + b_out
        out = out + residual
        return out
    x = _L0_xattn_ref(x, ctx_768, L0_xattn_g1, L0_xattn_be1, L0_xattn_wq1, L0_xattn_wk1, L0_xattn_wv1, L0_xattn_wo1, L0_xattn_bo1, L0_xattn_g2, L0_xattn_be2, L0_xattn_wq2, L0_xattn_wk2, L0_xattn_wv2, L0_xattn_wo2, L0_xattn_bo2, L0_xattn_g3, L0_xattn_be3, L0_xattn_w_ff1, L0_xattn_b_ff1, L0_xattn_w_ff2, L0_xattn_b_ff2)
    x = _L1_xattn_ref(x, ctx_768, L1_xattn_Wq, L1_xattn_Wk, L1_xattn_Wv, L1_xattn_Wq_ca, L1_xattn_Wk_ca, L1_xattn_Wv_ca, L1_xattn_Wout, L1_xattn_b_out)
    return x

_drawn_inputs = setup_inputs


def setup_inputs(seed=0):
    import zlib

    import numpy as np

    out = dict(_drawn_inputs(seed))
    spreads = {'L0_xattn_g1': (1.0, 0.6),
     'L0_xattn_be1': (0.0, 0.452),
     'L0_xattn_bo1': (0.0, 0.1),
     'L0_xattn_g2': (1.0, 0.6),
     'L0_xattn_be2': (0.0, 0.8),
     'L0_xattn_bo2': (0.0, 0.1),
     'L0_xattn_g3': (1.0, 0.6),
     'L0_xattn_be3': (0.0, 0.8),
     'L0_xattn_b_ff1': (0.0, 0.8),
     'L0_xattn_b_ff2': (0.0, 0.1),
     'L1_xattn_b_out': (0.0, 0.1)}
    factors = {'L0_xattn_wq1': 8.0,
     'L0_xattn_wk1': 8.0,
     'L0_xattn_wq2': 8.0,
     'L0_xattn_wk2': 8.0,
     'L0_xattn_w_ff1': 2.751,
     'L0_xattn_w_ff2': 2.726,
     'L1_xattn_Wq': 8.0,
     'L1_xattn_Wk': 8.0,
     'L1_xattn_Wq_ca': 8.0,
     'L1_xattn_Wk_ca': 8.0}
    for name, (base, spread) in spreads.items():
        noise = np.random.default_rng([zlib.crc32(name.encode()), seed]).standard_normal(out[name].shape)
        drawn = base * np.exp(spread * noise) if base else spread * noise
        out[name] = jnp.asarray(drawn.astype(out[name].dtype))
    for name, factor in factors.items():
        out[name] = (out[name] * factor).astype(out[name].dtype)
    return out
```

```python
from contextlib import ExitStack

import numpy as np

import concourse.bass as bass
from concourse import mybir

ALU = mybir.AluOpType
ACT = mybir.ActivationFunctionType
AX = mybir.AxisListType
F32 = mybir.dt.float32
F32R = mybir.dt.float32r

BATCH, TOK, DIM, CTX = 8, 256, 160, 96
HEADS, DH = 20, 64
INNER = HEADS * DH
DFF = 640
HEADS2, DH2, NCA = 8, 20, 4
P = 128
REM = DIM - P
STACK = 3 * REM
TT = TOK // P
PAIRS = HEADS // 2
CHUNKS = INNER // 256
FT = DFF // P
PADH = 32
QUADS = HEADS2 // 4
PADW = HEADS2 * PADH
KEYS2 = TOK - NCA
EPS = 1e-5
GELU_C = 0.7978845608028654
GELU_A = 0.044715

UNITS = ([("self", h) for h in range(HEADS)] + [("cross", h) for h in range(HEADS)]
         + [("ca", h) for h in range(HEADS2)] + [("enc", h) for h in range(HEADS2)])
NU = len(UNITS)
FIRST = {"self": 0, "cross": HEADS, "ca": 2 * HEADS, "enc": 2 * HEADS + HEADS2}
RING = 4
RINGT = 8
LAG_T = 2
LAG_V = 3
LAG_O = 4

PER = dict(scores_ready=NU, exp_done=NU, max_ready=NU, recip_ready=NU, norm_ready=NU, tr_ready=NU,
           pT_ready=NU, pv_ready=2 * PAIRS + 2 * QUADS, o_ready=2 * PAIRS + 2 * QUADS,
           wo_done=2 * PAIRS, y_ready=2, y_taken=4,
           pa_ready=PAIRS + 2 * CHUNKS + FT + 7, pa_taken=PAIRS + 2 * CHUNKS + FT + 7,
           pb_ready=2 * CHUNKS + FT + 7, pb_taken=2 * CHUNKS + FT + 7,
           hi_ready=4, lo_ready=4, stats_ready=3, rstd_ready=3, xn_ready=3, res_ready=4,
           xaff_ready=4, ff_cube=FT, ff_u=FT, ff_tanh=FT, ff_h=FT, s2_exp=1, k2v2=2,
           out_ready=1, v2_done=1)


def unit_queries(kind):
    return CTX if kind == "ca" else TOK


def unit_keys(kind):
    return KEYS2 if kind == "enc" else TOK


def group_of(u):
    if u < 2 * HEADS:
        return u // 2
    return 2 * PAIRS + (u - 2 * HEADS) // 4


def groups_units(g):
    if g < 2 * PAIRS:
        return [2 * g, 2 * g + 1]
    first = 2 * HEADS + 4 * (g - 2 * PAIRS)
    return list(range(first, first + 4))


def build(nc, x, ctx, w_main, w_rem, w_ctx, w_o, w_f2, wq_p, wk_p, wv_p, wqca_p, wkca_p, wvca_p,
          wout_p, cols, rows, expand, mask_k, mask_v, out):
    es = ExitStack()
    with es:
        def sb(name, shape, dt=F32):
            return es.enter_context(nc.sbuf_tensor(name, shape, dt))

        sems = {}

        def sem(name):
            sems[name] = es.enter_context(nc.semaphore(name))
            return sems[name]

        NW = 5
        W_Q1, W_K1, W_V1, W_Q2, W_F1 = range(NW)
        w_hi = sb("w_hi", [P, NW, INNER], F32R)
        w_lo = sb("w_lo", [P, NW, INNER], F32R)
        w_st = sb("w_st", [STACK, NW, INNER], F32R)
        wc_hi = sb("wc_hi", [CTX, 2, INNER], F32R)
        wc_lo = sb("wc_lo", [CTX, 2, INNER], F32R)
        wo = sb("wo", [P, 2 * PAIRS, DIM])
        wf2 = sb("wf2", [P, FT, DIM])
        wq2p = sb("wq2p", [P, QUADS, PADW])
        wk2p = sb("wk2p", [CTX, PADW])
        wv2p = sb("wv2p", [CTX, PADW])
        wqca = sb("wqca", [NCA, PADW])
        wkca = sb("wkca", [CTX, PADW])
        wvca = sb("wvca", [CTX, PADW])
        woutp = sb("woutp", [P, QUADS, DIM])
        col = sb("col", [P, 12 + 2 * FT])
        row = sb("row", [P, 4, DIM])
        ex = sb("ex", [CTX, TOK])
        mk = sb("mk", [P, 4, NCA])
        mv = sb("mv", [HEADS2 * NCA, PADW])
        ident = sb("ident", [P, P])
        eps_c = sb("eps_c", [P, TT])
        half_c = sb("half_c", [P, TT])

        x_in = sb("x_in", [P, TT, DIM])
        ctx_in = sb("ctx_in", [P, TT, CTX])
        ca_in = sb("ca_in", [NCA, CTX])
        x_cur = sb("x_cur", [P, TT, DIM])
        x_res = sb("x_res", [P, TT, DIM])
        stats = sb("stats", [P, TT, 6])
        mv_ln = sb("mv_ln", [P, TT, 2])
        wait_pad = sb("wait_pad", [P, 1])
        var_e = sb("var_e", [P, TT])
        rstd = sb("rstd", [P, TT])
        xn = sb("xn", [P, TT, P + STACK])
        xaff = sb("xaff", [P, 2, TOK])
        x_hi = sb("x_hi", [P, TOK], F32R)
        x_lo = sb("x_lo", [P, TOK], F32R)
        x_st = sb("x_st", [STACK, TOK], F32R)
        cT = sb("cT", [CTX, TOK])
        ca_rep = sb("ca_rep", [CTX, HEADS2, NCA])
        cT_hi = sb("cT_hi", [CTX, TOK], F32R)
        cT_lo = sb("cT_lo", [CTX, TOK], F32R)
        qk_buf = sb("qk_buf", [P, PAIRS * 2 * TOK])
        val_buf = sb("val_buf", [P, TT * INNER])
        qk = qk_buf[:].rearrange("p (j s t) -> p j s t", j=PAIRS, s=2)
        val = val_buf[:].rearrange("p (t n) -> p t n", t=TT)
        prob = sb("prob", [P, RING, 2 * TOK])
        pT = sb("pT", [P, RINGT, TT, TOK])
        nmax = sb("nmax", [P, RINGT, TT])
        rsum = sb("rsum", [P, RINGT, TT])
        rinv = sb("rinv", [P, RINGT, TT])
        oT = sb("oT", [P, 2, TOK])
        f_g, f_w, f_a = (qk_buf[:, n * DFF * TT:(n + 1) * DFF * TT].rearrange("p (j t) -> p j t", j=FT) for n in range(3))
        val_at = [0]

        def over_val(parts, groups, width):
            at = val_at[0]
            val_at[0] += groups * width
            return val_buf[0:parts, at:at + groups * width].rearrange("p (g t) -> p g t", g=groups)

        x3T, q2T, hsT = (over_val(P, QUADS, TOK) for _ in range(3))
        hs1T, cq2T, c2T = (over_val(P, QUADS, CTX) for _ in range(3))
        c2w = over_val(CTX, 1, DIM)[:, 0, :]
        x3p = sb("x3p", [P, TT, PADW])
        k2T = sb("k2T", [P, QUADS, TOK])
        v2p = sb("v2p", [P, TT, PADW])
        cq1T = sb("cq1T", [P, QUADS, CTX])
        k2bd = sb("k2bd", [P, QUADS, 4, NCA])
        v2bd = sb("v2bd", [HEADS2 * NCA, PADW])
        s2 = sb("s2", [CTX, HEADS2, NCA])
        s2m = sb("s2m", [CTX, HEADS2])
        s2s = sb("s2s", [CTX, HEADS2])
        s2r = sb("s2r", [CTX, HEADS2])
        p2T = sb("p2T", [HEADS2 * NCA, CTX])
        o_sb = sb("o_sb", [P, TT, DIM])
        stage_m = [qk_buf[:, n * INNER:(n + 1) * INNER] for n in range(2)]
        stage_r = [qk_buf[0:STACK, 2 * INNER:3 * INNER], val_buf[0:STACK, 0:INNER]]

        def bank(name):
            return es.enter_context(nc.psum_tensor(name, [P, 512], F32))

        s_bank = [bank("s_bank0"), bank("s_bank1")]
        t_bank = [bank("t_bank0"), bank("t_bank1")]
        o_bank, y_bank, pa, pb = bank("o_bank"), bank("y_bank"), bank("pa"), bank("pb")

        for name in PER:
            sem(name)
        w_loaded = [[es.enter_context(nc.semaphore(f"w_loaded{i}")) for i in range(2)]][0]
        wc_loaded = sem("wc_loaded")
        small_loaded = sem("small_loaded")
        w_hi_ready, w_lo_ready = sem("w_hi_ready"), sem("w_lo_ready")
        x_loaded, ctx_loaded, out_stored = sem("x_loaded"), sem("ctx_loaded"), sem("out_stored")
        ident_ready, l1_scaled = sem("ident_ready"), sem("l1_scaled")
        dve_step, act_step, pool_step = sem("dve_step"), sem("act_step"), sem("pool_step")

        NSMALL = 14

        def wait_n(eng, name, b, n):
            per = PER[name]
            if isinstance(b, int) and b * per + n <= 0:
                return
            eng.wait_ge(sems[name], b * per + n)

        def batches(eng, one):
            one(0)
            with eng.Fori(1, BATCH) as b:
                one(b)

        block = es.enter_context(nc.Block())

        @block.sync
        def _(sp):
            with nc.allow_non_contiguous_dma(reason="vectors and padded heads"):
                for dst, src in ((col[:], cols), (row[:], rows.to_broadcast([P, 4, DIM])),
                                 (wf2[:], w_f2.rearrange("(j p) e -> p j e", p=P)),
                                 (wq2p[:], wq_p), (wk2p[:], wk_p), (wv2p[:], wv_p), (wqca[:], wqca_p),
                                 (wkca[:], wkca_p), (wvca[:], wvca_p), (woutp[:], wout_p), (ex[:], expand),
                                 (mk[:], mask_k), (mv[:], mask_v)):
                    sp.dma_start(dst, src).then_inc(small_loaded, 16)
                sp.dma_start(wo[:], w_o.rearrange("a (j p) e -> p (a j) e", p=P)).then_inc(small_loaded, 16)

            def one(b):
                if not isinstance(b, int):
                    sp.wait_ge(sems["xn_ready"], 3 * b - 2)
                    sp.wait_ge(sems["res_ready"], 4 * b - 3)
                sp.dma_start(x_in[:], x[b].rearrange("(t p) e -> p t e", p=P)).then_inc(x_loaded, 16)
                if not isinstance(b, int):
                    sp.wait_ge(sems["pb_ready"], PER["pb_ready"] * (b - 1) + 1)
                    sp.wait_ge(sems["pa_ready"], PER["pa_ready"] * (b - 1) + 2)
                sp.dma_start(ctx_in[:], ctx[b].rearrange("(t p) e -> p t e", p=P)).then_inc(ctx_loaded, 16)
                sp.dma_start(ca_in[:], ctx[b, KEYS2:TOK, :]).then_inc(ctx_loaded, 16)
                if not isinstance(b, int):
                    sp.wait_ge(sems["out_ready"], b)
                    sp.dma_start(out[b - 1].rearrange("(t p) e -> p t e", p=P), o_sb[:]).then_inc(out_stored, 16)
            batches(sp, one)
            sp.wait_ge(sems["out_ready"], BATCH)
            sp.dma_start(out[BATCH - 1].rearrange("(t p) e -> p t e", p=P), o_sb[:]).then_inc(out_stored, 16)
            sp.wait_ge(out_stored, 16 * BATCH)

        @block.gpsimd
        def _(pool):
            pool.memset(ident[:], 0.0).then_inc(ident_ready, 1)
            pool.memset(half_c[:], -0.5).then_inc(ident_ready, 1)
            pool.memset(x3p[:], 0.0).then_inc(ident_ready, 1)
            pool.memset(eps_c[:], EPS).then_inc(ident_ready, 1)
            pool.wait_ge(ident_ready, 4)
            pool.affine_select(out=ident[:], in_=ident[:], compare_op=ALU.not_equal, fill=1.0, base=0,
                               pattern=[[-1, P]], channel_multiplier=1).then_inc(ident_ready, 1)
            pool.wait_ge(small_loaded, 16 * NSMALL)

            def normalise(b, u):
                kind, _ = UNITS[u]
                q, k = unit_queries(kind), unit_keys(kind)
                wait_n(pool, "recip_ready", b, u + 1)
                if kind == "ca":
                    p = prob[0:q, u % RING, 0:k]
                    r = rinv[0:q, u % RINGT, 0:1].to_broadcast([q, k])
                else:
                    p = prob[:, u % RING, 0:2 * k].rearrange("p (t k) -> p t k", t=2)
                    r = rinv[:, u % RINGT, :].rearrange("p (t o) -> p t o", o=1).to_broadcast([P, 2, k])
                pool.tensor_tensor(p, p, r, ALU.mult).then_inc(sems["norm_ready"], 1)

            def rstd_of(b, k):
                wait_n(pool, "stats_ready", b, k + 1)
                pool.tensor_tensor(var_e[:], mv_ln[:, :, 1], eps_c[:], ALU.add).then_inc(pool_step, 1)
                pool.wait_ge(pool_step, 3 * b + k + 1)
                pool.tensor_tensor(rstd[:], var_e[:], half_c[:], ALU.pow).then_inc(sems["rstd_ready"], 1)

            def residual(b, k):
                if k == 0:
                    pool.wait_ge(x_loaded, 16 * b + 16)
                    wait_n(pool, "y_taken", b, 0)
                    pool.tensor_tensor(x_res[:], x_in[:], row[:, 0, :].rearrange("p (o e) -> p o e", o=1).to_broadcast([P, TT, DIM]),
                                       ALU.add).then_inc(sems["res_ready"], 1)
                elif k < 3:
                    wait_n(pool, "y_taken", b, k)
                    pool.tensor_tensor(x_res[:], x_cur[:], row[:, k, :].rearrange("p (o e) -> p o e", o=1).to_broadcast([P, TT, DIM]),
                                       ALU.add).then_inc(sems["res_ready"], 1)
                else:
                    wait_n(pool, "y_taken", b, 3)
                    for t in range(TT):
                        last = pool.tensor_tensor(
                            x_res[:, t, :].rearrange("p (h d) -> p h d", d=DH2),
                            x3p[:, t, :].rearrange("p (h d) -> p h d", d=PADH)[:, :, 0:DH2],
                            row[:, 3, :].rearrange("p (h d) -> p h d", d=DH2), ALU.add)
                    last.then_inc(sems["res_ready"], 1)

            def one(b):
                rstd_of(b, 0)
                residual(b, 0)
                for u in range(0, HEADS):
                    normalise(b, u)
                rstd_of(b, 1)
                residual(b, 1)
                for u in range(HEADS, 2 * HEADS):
                    normalise(b, u)
                rstd_of(b, 2)
                residual(b, 2)
                for j in range(FT):
                    wait_n(pool, "pa_taken", b, 2 + PAIRS + 2 * CHUNKS + j + 1)
                    pool.tensor_tensor(f_w[:, j, :], f_w[:, j, :], f_g[:, j, :], ALU.mult).then_inc(sems["ff_cube"], 1)
                residual(b, 3)
                for u in range(2 * HEADS, NU):
                    normalise(b, u)
            batches(pool, one)

        @block.scalar
        def _(act):
            def load_w(i):
                if i >= 2:
                    act.wait_ge(w_lo_ready, 2 * (i - 1))
                act.dma_start(stage_m[i % 2], w_main[i]).then_inc(w_loaded[i % 2], 16)
                act.dma_start(stage_r[i % 2], w_rem[i]).then_inc(w_loaded[i % 2], 16)

            load_w(0)
            load_w(1)
            act.dma_start(pT[0:CTX, :, :, :].rearrange("p r t k -> p (r t k)")[:, 0:INNER], w_ctx[0]).then_inc(wc_loaded, 16)
            act.dma_start(pT[0:CTX, :, :, :].rearrange("p r t k -> p (r t k)")[:, INNER:2 * INNER], w_ctx[1]).then_inc(wc_loaded, 16)
            for i in range(NW):
                act.wait_ge(w_loaded[i % 2], 32 * (i // 2 + 1))
                sc = DH ** -0.5 if i in (W_Q1, W_Q2) else 1.0
                act.activation(w_hi[:, i, :], stage_m[i % 2], ACT.Copy, scale=sc).then_inc(w_hi_ready, 1)
                act.activation(w_st[:, i, :], stage_r[i % 2], ACT.Copy, scale=sc).then_inc(w_hi_ready, 1)
                if i + 2 < NW:
                    load_w(i + 2)
            act.wait_ge(wc_loaded, 32)
            act.activation(wc_hi[:].rearrange("p a n -> p (a n)"),
                           pT[0:CTX, :, :, :].rearrange("p r t k -> p (r t k)")[:, 0:2 * INNER], ACT.Copy).then_inc(w_hi_ready, 1)
            act.wait_ge(small_loaded, 16 * NSMALL)
            act.activation(wq2p[:], wq2p[:], ACT.Copy, scale=DH2 ** -0.5).then_inc(l1_scaled, 1)
            act.activation(wqca[:], wqca[:], ACT.Copy, scale=DH2 ** -0.5).then_inc(l1_scaled, 1)
            act.wait_ge(w_lo_ready, 2 * NW + 1)

            def exps(b, u):
                kind, _ = UNITS[u]
                q, k = unit_queries(kind), unit_keys(kind)
                wait_n(act, "max_ready", b, u + 1)
                wait_n(act, "tr_ready", b, u + 1 - RING)
                tiles = 1 if kind == "ca" else 2
                for t in range(tiles):
                    last = act.activation(prob[0:min(q, P), u % RING, t * k:t * k + k],
                                          s_bank[u % 2][0:min(q, P), t * TOK:t * TOK + k], ACT.Exp,
                                          bias=nmax[0:min(q, P), u % RINGT, t:t + 1],
                                          accum_out=rsum[0:min(q, P), u % RINGT, t:t + 1])
                last.then_inc(sems["exp_done"], 1)

            def take_pT(b, u):
                kind, _ = UNITS[u]
                q, k = unit_queries(kind), unit_keys(kind)
                wait_n(act, "tr_ready", b, u + 1)
                prev = u - RINGT
                wait_n(act, "pv_ready", b, group_of(prev) + 1 if prev >= 0
                       else group_of(prev + NU) + 1 - PER["pv_ready"])
                src = t_bank[u % 2][:, 0:2 * q].rearrange("p (t q) -> p t q", t=2)
                if k == TOK:
                    act.activation(pT[:, u % RINGT, :, 0:q], src, ACT.Copy).then_inc(sems["pT_ready"], 1)
                else:
                    act.activation(pT[:, u % RINGT, 0, 0:q], src[:, 0, :], ACT.Copy)
                    act.activation(pT[0:k - P, u % RINGT, 1, 0:q], src[0:k - P, 1, :], ACT.Copy)\
                       .then_inc(sems["pT_ready"], 1)

            def take_pa(b, n, dst, src):
                wait_n(act, "pa_ready", b, n + 1)
                act.activation(dst, src, ACT.Copy).then_inc(sems["pa_taken"], 1)

            def high_halves(b, k):
                wait_n(act, "xaff_ready", b, k + 1)
                act.activation(x_hi[:], xaff[:, 0, :], ACT.Copy)
                act.activation(x_st[:], xaff[0:STACK, 1, :], ACT.Copy).then_inc(sems["hi_ready"], 1)

            def attention(b, first, n, extra):
                for s in range(n + LAG_T):
                    if s < n:
                        exps(b, first + s)
                    if s >= LAG_T:
                        take_pT(b, first + s - LAG_T)
                    if s in extra:
                        extra[s]()

            def one(b):
                pa_n = [0]

                def take(dst, src):
                    take_pa(b, pa_n[0], dst, src)
                    pa_n[0] += 1

                flat = pa[:, :]
                wait_n(act, "xaff_ready", b, 1)
                act.activation(cT_hi[:], cT[:], ACT.Copy).then_inc(sems["hi_ready"], 1)
                take(k2T[:].rearrange("p g t -> p (g t)"), flat)
                take(cq1T[:].rearrange("p g t -> p (g t)"), flat[:, 0:QUADS * CTX])
                high_halves(b, 1)
                qk_flat = [qk[:, j, :, :].rearrange("p s t -> p (s t)") for j in range(PAIRS)]
                take(qk_flat[0], flat)
                attention(b, 0, HEADS, {2 * j: (lambda j=j: take(qk_flat[j + 1], flat)) for j in range(PAIRS - 1)})
                for c in range(CHUNKS):
                    take(qk[:, 2 * c:2 * c + 2, 1, :], flat.rearrange("p (j t) -> p j t", j=2))
                high_halves(b, 2)
                take(qk[:, 0:2, 0, :], flat.rearrange("p (j t) -> p j t", j=2))
                attention(b, HEADS, HEADS, {4 * c: (lambda c=c: take(qk[:, 2 * c + 2:2 * c + 4, 0, :],
                                                                       flat.rearrange("p (j t) -> p j t", j=2)))
                                            for c in range(CHUNKS - 1)})
                high_halves(b, 3)
                for j in range(FT + 2):
                    if j < FT:
                        wait_n(act, "pa_ready", b, pa_n[0] + 1)
                        bias = col[:, 12 + FT + j:13 + FT + j]
                        act.activation(f_g[:, j, :], flat[:, 0:TOK], ACT.Identity, bias=bias)
                        act.activation(f_w[:, j, :], flat[:, 0:TOK], ACT.Square, bias=bias)\
                           .then_inc(sems["pa_taken"], 1)
                        pa_n[0] += 1
                    if j >= 2:
                        i = j - 2
                        wait_n(act, "ff_u", b, i + 1)
                        act.activation(f_w[:, i, :], f_w[:, i, :], ACT.Tanh, scale=GELU_C).then_inc(sems["ff_tanh"], 1)
                take(q2T.rearrange("p g t -> p (g t)"), flat)

                def chain_cq2():
                    take(cq2T.rearrange("p g t -> p (g t)"), flat[:, 0:QUADS * CTX])

                def chain_exp():
                    wait_n(act, "s2_exp", b, 1)
                    act.activation(s2[:], s2[:], ACT.Exp).then_inc(sems["v2_done"], 1)

                def chain_p2T():
                    take(p2T[:], pa[0:HEADS2 * NCA, 0:CTX])

                def chain_c2T():
                    take(c2T.rearrange("p g t -> p (g t)"), flat[:, 0:QUADS * CTX])

                def chain_c2w():
                    take(c2w, pa[0:CTX, 0:DIM])
                attention(b, 2 * HEADS, 2 * HEADS2, {12: chain_cq2, 13: chain_exp, 14: chain_p2T, 15: chain_c2T,
                                                     16: chain_c2w})
                assert pa_n[0] == PER["pa_ready"], pa_n
            batches(act, one)

        @block.vector
        def _(dve):
            for i in range(NW):
                sc = DH ** -0.5 if i in (W_Q1, W_Q2) else 1.0
                dve.wait_ge(w_hi_ready, 2 * i + 2)
                dve.scalar_tensor_tensor(out=w_lo[:, i, :], in0=stage_m[i % 2], scalar=sc,
                                         in1=w_hi[:, i, :].bitcast(F32), op0=ALU.mult, op1=ALU.subtract)\
                   .then_inc(w_lo_ready, 1)
                lo = slice(REM, 2 * REM)
                dve.scalar_tensor_tensor(out=w_st[lo, i, :], in0=stage_r[i % 2][lo], scalar=sc,
                                         in1=w_st[lo, i, :].bitcast(F32), op0=ALU.mult, op1=ALU.subtract)\
                   .then_inc(w_lo_ready, 1)
            dve.wait_ge(w_hi_ready, 2 * NW + 1)
            dve.tensor_tensor(wc_lo[:].rearrange("p a n -> p (a n)"),
                              pT[0:CTX, :, :, :].rearrange("p r t k -> p (r t k)")[:, 0:2 * INNER],
                              wc_hi[:].rearrange("p a n -> p (a n)").bitcast(F32), ALU.subtract).then_inc(w_lo_ready, 1)
            dve.wait_ge(small_loaded, 16 * NSMALL)
            dve.wait_ge(ident_ready, 5)

            step = [0]
            STEPS = 13 + FT

            def own(b, ins):
                step[0] += 1
                ins.then_inc(dve_step, 1)
                dve.wait_ge(dve_step, b * STEPS + step[0])

            def maxima(b, u):
                kind, _ = UNITS[u]
                q, k = unit_queries(kind), unit_keys(kind)
                wait_n(dve, "scores_ready", b, u + 1)
                if kind == "ca":
                    dve.tensor_reduce(nmax[0:q, u % RINGT, 0:1], s_bank[u % 2][0:q, 0:k], AX.X, ALU.max,
                                      negate=True).then_inc(sems["max_ready"], 1)
                else:
                    dve.tensor_reduce(nmax[:, u % RINGT, :],
                                      s_bank[u % 2][:, :].rearrange("p (t k) -> p t k", t=2)[:, :, 0:k],
                                      AX.X, ALU.max, negate=True).then_inc(sems["max_ready"], 1)

            def inverse(b, u):
                q = min(unit_queries(UNITS[u][0]), P)
                t = 1 if UNITS[u][0] == "ca" else TT
                wait_n(dve, "exp_done", b, u + 1)
                dve.reciprocal(rinv[0:q, u % RINGT, 0:t], rsum[0:q, u % RINGT, 0:t]).then_inc(sems["recip_ready"], 1)

            def take_o(b, g):
                kind = UNITS[groups_units(g)[0]][0]
                wait_n(dve, "pv_ready", b, g + 1)
                if kind in ("self", "cross"):
                    wait_n(dve, "wo_done", b, g - 1)
                    dve.tensor_copy(oT[:, g % 2, :], o_bank[:, 0:TOK]).then_inc(sems["o_ready"], 1)
                elif kind == "ca":
                    dve.tensor_copy(hs1T[:, (g - 2 * PAIRS) % QUADS, :], o_bank[:, 0:CTX]).then_inc(sems["o_ready"], 1)
                else:
                    dve.tensor_copy(hsT[:, (g - 2 * PAIRS) % QUADS, :], o_bank[:, 0:TOK]).then_inc(sems["o_ready"], 1)

            def layer_norm(b, k, src):
                for t in range(TT):
                    last = dve.bn_stats(stats[:, t, :], src[:, t, :])
                own(b, last)
                dve.memset(wait_pad[:], 0.0)
                for t in range(TT):
                    last = dve.bn_aggr(mv_ln[:, t, :], stats[:, t, :])
                last.then_inc(sems["stats_ready"], 1)
                wait_n(dve, "rstd_ready", b, k + 1)
                for t in range(TT):
                    dve.tensor_scalar(xn[:, t, 0:P], src[:, t, 0:P], mv_ln[:, t, 0:1], rstd[:, t:t + 1],
                                      ALU.subtract, ALU.mult)
                    last = dve.tensor_scalar(
                        xn[:, t, P:P + STACK].rearrange("p (c r) -> p c r", c=3),
                        src[:, t, P:DIM].rearrange("p (o r) -> p o r", o=1).to_broadcast([P, 3, REM]),
                        mv_ln[:, t, 0:1], rstd[:, t:t + 1], ALU.subtract, ALU.mult)
                last.then_inc(sems["xn_ready"], 1)

            def affine_and_low(b, k, n_pb):
                wait_n(dve, "pb_ready", b, n_pb + 1)
                dve.tensor_scalar(xaff[:, 0, :], pb[:, 0:TOK], col[:, 4 * k:4 * k + 1], col[:, 4 * k + 1:4 * k + 2],
                                  ALU.mult, ALU.add)
                own(b, dve.tensor_scalar(xaff[0:STACK, 1, :], pb[0:STACK, TOK:2 * TOK], col[0:STACK, 4 * k + 2:4 * k + 3],
                                         col[0:STACK, 4 * k + 3:4 * k + 4], ALU.mult, ALU.add))
                dve.sem_inc(sems["xaff_ready"], 1)
                dve.sem_inc(sems["pb_taken"], 1)
                wait_n(dve, "hi_ready", b, k + 2)
                dve.tensor_tensor(x_lo[:], xaff[:, 0, :], x_hi[:].bitcast(F32), ALU.subtract)
                lo = slice(2 * REM, 3 * REM)
                dve.tensor_tensor(x_st[lo, :], xaff[lo, 1, :], x_st[lo, :].bitcast(F32), ALU.subtract)\
                   .then_inc(sems["lo_ready"], 1)

            def attention(b, first, n, extra):
                for s in range(n + LAG_V):
                    if s < n:
                        maxima(b, first + s)
                    if s in extra:
                        extra[s]()
                    if 1 <= s <= n:
                        inverse(b, first + s - 1)
                    last = first + s - LAG_V
                    if s >= LAG_V and groups_units(group_of(last))[-1] == last:
                        take_o(b, group_of(last))

            def take_y(b, n):
                if n < 2:
                    wait_n(dve, "wo_done", b, PAIRS * (n + 1))
                else:
                    wait_n(dve, "y_ready", b, n - 1)
                wait_n(dve, "res_ready", b, n + 1)

            def one(b):
                step[0] = 0
                pb_n = [0]

                def take(dst, src):
                    wait_n(dve, "pb_ready", b, pb_n[0] + 1)
                    dve.tensor_copy(dst, src).then_inc(sems["pb_taken"], 1)
                    pb_n[0] += 1

                wait_n(dve, "pb_ready", b, pb_n[0] + 1)
                dve.tensor_copy(ca_rep[:], pb[0:CTX, KEYS2:TOK].rearrange("p (o c) -> p o c", o=1)
                                .to_broadcast([CTX, HEADS2, NCA]))
                own(b, dve.tensor_copy(cT[:], pb[0:CTX, 0:TOK]))
                dve.sem_inc(sems["xaff_ready"], 1)
                dve.sem_inc(sems["pb_taken"], 1)
                pb_n[0] += 1
                dve.wait_ge(x_loaded, 16 * b + 16)
                layer_norm(b, 0, x_in)
                wait_n(dve, "hi_ready", b, 1)
                dve.tensor_tensor(cT_lo[:], cT[:], cT_hi[:].bitcast(F32), ALU.subtract).then_inc(sems["lo_ready"], 1)
                affine_and_low(b, 0, pb_n[0])
                pb_n[0] += 1
                take(v2p[:].rearrange("p t n -> p (t n)"), pb[:, :])
                wait_n(dve, "pb_ready", b, pb_n[0] + 1)
                for g in range(QUADS):
                    dve.tensor_tensor(k2bd[:, g, :, :],
                                      pb[:, g * NCA:(g + 1) * NCA].rearrange("p (o c) -> p o c", o=1).to_broadcast([P, 4, NCA]),
                                      mk[:], ALU.mult)
                dve.tensor_tensor(v2bd[:], pb[0:HEADS2 * NCA, 64:64 + PADW], mv[:], ALU.mult).then_inc(sems["pb_taken"], 1)
                pb_n[0] += 1

                attention(b, 0, HEADS, {4 * c + 1: (lambda c=c: take(val[:, :, 256 * c:256 * c + 256],
                                                                   pb[:, :].rearrange("p (t n) -> p t n", t=2)))
                                        for c in range(CHUNKS)})
                for c in range(CHUNKS):
                    take(val[:, :, 256 * c:256 * c + 256], pb[:, :].rearrange("p (t n) -> p t n", t=2))
                take_y(b, 0)
                own(b, dve.tensor_tensor(x_cur[:].rearrange("p t e -> p (t e)"), y_bank[:, 0:TT * DIM],
                                         x_res[:].rearrange("p t e -> p (t e)"), ALU.add))
                dve.sem_inc(sems["y_taken"], 1)
                layer_norm(b, 1, x_cur)
                affine_and_low(b, 1, pb_n[0])
                pb_n[0] += 1
                attention(b, HEADS, HEADS, {})
                take_y(b, 1)
                own(b, dve.tensor_tensor(x_cur[:].rearrange("p t e -> p (t e)"), y_bank[:, 0:TT * DIM],
                                         x_res[:].rearrange("p t e -> p (t e)"), ALU.add))
                dve.sem_inc(sems["y_taken"], 1)
                layer_norm(b, 2, x_cur)
                affine_and_low(b, 2, pb_n[0])
                pb_n[0] += 1

                for j in range(FT + 3):
                    if j < FT:
                        wait_n(dve, "pb_ready", b, pb_n[0] + 1)
                        dve.tensor_scalar(f_a[:, j, :], pb[:, 0:TOK], col[:, 12 + j:13 + j], None, ALU.add)\
                           .then_inc(sems["pb_taken"], 1)
                        pb_n[0] += 1
                    if 1 <= j <= FT:
                        i = j - 1
                        wait_n(dve, "ff_cube", b, i + 1)
                        dve.scalar_tensor_tensor(out=f_w[:, i, :], in0=f_w[:, i, :], scalar=GELU_A, in1=f_g[:, i, :],
                                                 op0=ALU.mult, op1=ALU.add).then_inc(sems["ff_u"], 1)
                    if j >= 3:
                        i = j - 3
                        wait_n(dve, "ff_tanh", b, i + 1)
                        own(b, dve.scalar_tensor_tensor(out=f_w[:, i, :], in0=f_w[:, i, :], scalar=1.0, in1=f_g[:, i, :],
                                                        op0=ALU.add, op1=ALU.mult))
                        dve.tensor_tensor(f_a[:, i, :], f_w[:, i, :], f_a[:, i, :], ALU.mult).then_inc(sems["ff_h"], 1)
                take_y(b, 2)
                for t in range(TT):
                    last = dve.scalar_tensor_tensor(
                        out=x3p[:, t, :].rearrange("p (h d) -> p h d", d=PADH)[:, :, 0:DH2],
                        in0=y_bank[:, t * DIM:(t + 1) * DIM].rearrange("p (h d) -> p h d", d=DH2), scalar=0.5,
                        in1=x_res[:, t, :].rearrange("p (h d) -> p h d", d=DH2), op0=ALU.mult, op1=ALU.add)
                last.then_inc(sems["y_taken"], 1)
                take(x3T.rearrange("p g t -> p (g t)"), pb[:, :])

                def chain_softmax():
                    wait_n(dve, "k2v2", b, 1)
                    s3 = y_bank[0:CTX, 0:HEADS2 * NCA].rearrange("p (h c) -> p h c", c=NCA)
                    own(b, dve.tensor_reduce(s2m[:], s3, AX.X, ALU.max))
                    dve.tensor_tensor(s2[:], s3, s2m[:].rearrange("p (h o) -> p h o", o=1).to_broadcast([CTX, HEADS2, NCA]),
                                      ALU.subtract).then_inc(sems["s2_exp"], 1)

                def chain_norm():
                    wait_n(dve, "v2_done", b, 1)
                    own(b, dve.tensor_reduce(s2s[:], s2[:], AX.X, ALU.add))
                    own(b, dve.reciprocal(s2r[:], s2s[:]))
                    dve.tensor_tensor(s2[:], s2[:], s2r[:].rearrange("p (h o) -> p h o", o=1).to_broadcast([CTX, HEADS2, NCA]),
                                      ALU.mult).then_inc(sems["k2v2"], 1)
                attention(b, 2 * HEADS, 2 * HEADS2, {13: chain_softmax, 14: chain_norm})
                take_y(b, 3)
                if not isinstance(b, int):
                    dve.wait_ge(out_stored, 16 * b)
                own(b, dve.tensor_tensor(o_sb[:].rearrange("p t e -> p (t e)"), y_bank[:, 0:TT * DIM],
                                         x_res[:].rearrange("p t e -> p (t e)"), ALU.add))
                dve.sem_inc(sems["y_taken"], 1)
                dve.sem_inc(sems["out_ready"], 1)
                assert pb_n[0] == PER["pb_ready"], pb_n
                assert step[0] == STEPS, step
            batches(dve, one)

        @block.tensor
        def _(pe):
            pe.wait_ge(ident_ready, 5)

            def split_product(out_ap, w_i, wcols, x_is_weight, tok=slice(0, TOK)):
                pairs = [(w_hi[:, w_i, wcols], x_hi[:, tok]), (w_lo[:, w_i, wcols], x_hi[:, tok]),
                         (w_hi[:, w_i, wcols], x_lo[:, tok]), (w_st[:, w_i, wcols], x_st[:, tok])]
                for n, (w, a) in enumerate(pairs):
                    l, r = (a, w) if x_is_weight else (w, a)
                    last = pe.matmul(out_ap, l, r, start=(n == 0), stop=(n == 3))
                return last

            def split_ctx(out_ap, w_i, wcols, x_is_weight, tok=slice(0, TOK)):
                pairs = [(wc_hi[:, w_i, wcols], cT_hi[:, tok]), (wc_lo[:, w_i, wcols], cT_hi[:, tok]),
                         (wc_hi[:, w_i, wcols], cT_lo[:, tok])]
                for n, (w, a) in enumerate(pairs):
                    l, r = (a, w) if x_is_weight else (w, a)
                    last = pe.matmul(out_ap, l, r, start=(n == 0), stop=(n == 2))
                return last

            def one(b):
                pa_n, pb_n = [0], [0]

                def use_pa():
                    wait_n(pe, "pa_taken", b, pa_n[0])
                    pa_n[0] += 1

                def use_pb():
                    wait_n(pe, "pb_taken", b, pb_n[0])
                    pb_n[0] += 1

                def head_rows(kind, h):
                    if kind in ("self", "cross"):
                        return slice(DH * (h % 2), DH * (h % 2) + DH)
                    return slice(PADH * (h % 4), PADH * (h % 4) + DH2)

                def scores(u):
                    kind, h = UNITS[u]
                    r = head_rows(kind, h)
                    wait_n(pe, "exp_done", b, u - 1)
                    if kind == "self":
                        wait_n(pe, "pa_taken", b, 3 + h // 2)
                        qs, ks = qk[r, h // 2, 0, :], qk[r, h // 2, 1, :]
                    elif kind == "cross":
                        wait_n(pe, "pa_taken", b, 2 + PAIRS + CHUNKS + h // 4 + 1)
                        qs, ks = qk[r, h // 2, 0, :], qk[r, h // 2, 1, :]
                    elif kind == "ca":
                        wait_n(pe, "pb_taken", b, pb_n[0])
                        qs, ks = cq1T[r, h // 4, :], x3T[r, h // 4, :]
                    else:
                        wait_n(pe, "pa_taken", b, 2 + PAIRS + 2 * CHUNKS + FT + 1)
                        qs, ks = q2T[r, h // 4, :], k2T[r, h // 4, 0:KEYS2]
                    k = unit_keys(kind)
                    bank_ = s_bank[u % 2]
                    if kind == "ca":
                        last = pe.matmul(bank_[0:CTX, 0:k], qs, ks, start=True, stop=True)
                    else:
                        for t in range(TT):
                            last = pe.matmul(bank_[:, t * TOK:t * TOK + k], qs[:, t * P:(t + 1) * P], ks,
                                             start=True, stop=True)
                    last.then_inc(sems["scores_ready"], 1)

                def transposes(u):
                    kind, _ = UNITS[u]
                    q, k = unit_queries(kind), unit_keys(kind)
                    wait_n(pe, "norm_ready", b, u + 1)
                    wait_n(pe, "pT_ready", b, u - 1)
                    tb = t_bank[u % 2]
                    for c in range(2):
                        kk = min(P, k - c * P)
                        for t in range(1 if kind == "ca" else TT):
                            qq = min(q, P)
                            last = pe.transpose(tb[0:kk, c * q + t * P:c * q + t * P + qq],
                                                prob[0:qq, u % RING, t * k + c * P:t * k + c * P + kk],
                                                ident[0:qq, 0:qq])
                    last.then_inc(sems["tr_ready"], 1)

                def values(g):
                    us = groups_units(g)
                    kind = UNITS[us[0]][0]
                    q, k = unit_queries(kind), unit_keys(kind)
                    wait_n(pe, "pT_ready", b, us[-1] + 1)
                    wait_n(pe, "o_ready", b, g)
                    if kind == "self":
                        wait_n(pe, "pb_taken", b, 4 + g // 2 + 1)
                    for c in range(2):
                        kk = min(P, k - c * P)
                        for u in us:
                            h = UNITS[u][1]
                            if kind in ("self", "cross"):
                                v = val[:, c, h * DH:(h + 1) * DH]
                                rows_ = slice(DH * (h % 2), DH * (h % 2) + DH)
                            else:
                                src = x3p if kind == "ca" else v2p
                                v = src[0:kk, c, h * PADH:(h + 1) * PADH]
                                rows_ = slice(PADH * (h % 4), PADH * (h % 4) + PADH)
                            last = pe.matmul(o_bank[rows_, 0:q], v, pT[0:kk, u % RINGT, c, 0:q],
                                             start=(c == 0), stop=(c == 1), skip_group_check=True)
                    last.then_inc(sems["pv_ready"], 1)

                def project(g):
                    a = g // PAIRS
                    wait_n(pe, "o_ready", b, g + 1)
                    if g % PAIRS == 0:
                        wait_n(pe, "y_taken", b, a)
                    for t in range(TT):
                        last = pe.matmul(y_bank[:, t * DIM:(t + 1) * DIM], oT[:, g % 2, t * P:(t + 1) * P], wo[:, g, :],
                                         start=(g % PAIRS == 0 and t == 0), stop=(g % PAIRS == PAIRS - 1),
                                         skip_group_check=True)
                    last.then_inc(sems["wo_done"], 1)

                def attention(first, n, ahead):
                    for s in range(n + LAG_O + 1):
                        if s < n:
                            scores(first + s)
                        if s in ahead:
                            ahead[s]()
                        if LAG_T <= s < n + LAG_T:
                            transposes(first + s - LAG_T)
                        u = first + s - LAG_V
                        if LAG_V <= s < n + LAG_V and groups_units(group_of(u))[-1] == u:
                            values(group_of(u))
                        u = first + s - LAG_O
                        if LAG_O <= s < n + LAG_O and u < 2 * HEADS and groups_units(group_of(u))[-1] == u:
                            project(group_of(u))

                def ln_transposes(k):
                    use_pb()
                    wait_n(pe, "xn_ready", b, k + 1)
                    for t in range(TT):
                        pe.transpose(pb[:, t * P:(t + 1) * P], xn[:, t, 0:P], ident[:])
                        last = pe.transpose(pb[0:STACK, TOK + t * P:TOK + (t + 1) * P], xn[:, t, P:P + STACK], ident[:])
                    last.then_inc(sems["pb_ready"], 1)

                def project_qk(j):
                    use_pa()
                    c = slice(j * P, (j + 1) * P)
                    split_product(pa[:, 0:TOK], W_Q1, c, False)
                    split_product(pa[:, TOK:2 * TOK], W_K1, c, False).then_inc(sems["pa_ready"], 1)

                def project_v(c):
                    use_pb()
                    for t in range(TT):
                        last = split_product(pb[:, t * 256:(t + 1) * 256], W_V1, slice(256 * c, 256 * c + 256), True,
                                             slice(t * P, (t + 1) * P))
                    last.then_inc(sems["pb_ready"], 1)

                def project_q2(c):
                    use_pa()
                    for i in range(2):
                        j = 2 * c + i
                        last = split_product(pa[:, i * TOK:(i + 1) * TOK], W_Q2, slice(j * P, (j + 1) * P), False)
                    last.then_inc(sems["pa_ready"], 1)

                pe.wait_ge(ctx_loaded, 32 * b + 32)
                use_pb()
                for t in range(TT):
                    last = pe.transpose(pb[0:CTX, t * P:(t + 1) * P], ctx_in[:, t, :], ident[:])
                last.then_inc(sems["pb_ready"], 1)
                ln_transposes(0)
                wait_n(pe, "xaff_ready", b, 1)
                if isinstance(b, int):
                    pe.wait_ge(small_loaded, 16 * NSMALL)
                    pe.wait_ge(l1_scaled, 2)
                use_pa()
                for g in range(QUADS):
                    last = pe.matmul(pa[:, g * TOK:(g + 1) * TOK], wk2p[:, g * P:(g + 1) * P], cT[:], start=True, stop=True)
                last.then_inc(sems["pa_ready"], 1)
                use_pa()
                for g in range(QUADS):
                    last = pe.matmul(pa[:, g * CTX:(g + 1) * CTX], wqca[:, g * P:(g + 1) * P], ca_in[:], start=True, stop=True)
                last.then_inc(sems["pa_ready"], 1)
                use_pb()
                for t in range(TT):
                    last = pe.matmul(pb[:, t * PADW:(t + 1) * PADW], cT[:, t * P:(t + 1) * P], wv2p[:], start=True, stop=True)
                last.then_inc(sems["pb_ready"], 1)
                use_pb()
                for g in range(QUADS):
                    pe.matmul(pb[:, g * NCA:(g + 1) * NCA], wkca[:, g * P:(g + 1) * P], cT[:, KEYS2:TOK], start=True, stop=True)
                last = pe.matmul(pb[0:HEADS2 * NCA, 64:64 + PADW],
                                 ca_rep[:].rearrange("p h c -> p (h c)"),
                                 wvca[:], start=True, stop=True)
                last.then_inc(sems["pb_ready"], 1)
                if isinstance(b, int):
                    pe.wait_ge(w_lo_ready, 2 * NW + 1)
                wait_n(pe, "lo_ready", b, 2)
                project_qk(0)
                attention(0, HEADS,
                          {**{2 * j: (lambda j=j: project_qk(j + 1)) for j in range(PAIRS - 1)},
                           **{4 * c + 1: (lambda c=c: project_v(c)) for c in range(CHUNKS)}})
                for c in range(CHUNKS):
                    use_pa()
                    for i in range(2):
                        j = 2 * c + i
                        last = split_ctx(pa[:, i * TOK:(i + 1) * TOK], 0, slice(j * P, (j + 1) * P), False)
                    last.then_inc(sems["pa_ready"], 1)
                    use_pb()
                    for t in range(TT):
                        last = split_ctx(pb[:, t * 256:(t + 1) * 256], 1, slice(256 * c, 256 * c + 256), True,
                                         slice(t * P, (t + 1) * P))
                    last.then_inc(sems["pb_ready"], 1)
                ln_transposes(1)
                wait_n(pe, "lo_ready", b, 3)
                project_q2(0)
                attention(HEADS, HEADS, {4 * c: (lambda c=c: project_q2(c + 1)) for c in range(CHUNKS - 1)})
                ln_transposes(2)
                wait_n(pe, "lo_ready", b, 4)
                for j in range(FT):
                    use_pa()
                    split_product(pa[:, 0:TOK], W_F1, slice(DFF + j * P, DFF + (j + 1) * P), False)\
                        .then_inc(sems["pa_ready"], 1)
                    use_pb()
                    split_product(pb[:, 0:TOK], W_F1, slice(j * P, (j + 1) * P), False).then_inc(sems["pb_ready"], 1)
                wait_n(pe, "y_taken", b, 2)
                for j in range(FT):
                    wait_n(pe, "ff_h", b, j + 1)
                    for t in range(TT):
                        last = pe.matmul(y_bank[:, t * DIM:(t + 1) * DIM], f_a[:, j, t * P:(t + 1) * P], wf2[:, j, :],
                                         start=(j == 0 and t == 0), stop=(j == FT - 1), skip_group_check=True)
                last.then_inc(sems["y_ready"], 1)
                wait_n(pe, "y_taken", b, 3)
                use_pb()
                for g in range(QUADS):
                    for t in range(TT):
                        last = pe.transpose(pb[:, g * TOK + t * P:g * TOK + (t + 1) * P], x3p[:, t, g * P:(g + 1) * P], ident[:])
                last.then_inc(sems["pb_ready"], 1)
                use_pa()
                wait_n(pe, "pb_taken", b, pb_n[0])
                for m in range(QUADS):
                    for g in range(QUADS):
                        last = pe.matmul(pa[:, m * TOK:(m + 1) * TOK], wq2p[:, g, m * P:(m + 1) * P], x3T[:, g, :],
                                         start=(g == 0), stop=(g == QUADS - 1))
                last.then_inc(sems["pa_ready"], 1)

                def chain_cq2():
                    wait_n(pe, "o_ready", b, 2 * PAIRS + QUADS)
                    use_pa()
                    for m in range(QUADS):
                        for g in range(QUADS):
                            last = pe.matmul(pa[:, m * CTX:(m + 1) * CTX], wq2p[:, g, m * P:(m + 1) * P], hs1T[:, g, :],
                                             start=(g == 0), stop=(g == QUADS - 1))
                    last.then_inc(sems["pa_ready"], 1)

                def chain_s2():
                    wait_n(pe, "pa_taken", b, pa_n[0])
                    for g in range(QUADS):
                        last = pe.matmul(y_bank[0:CTX, g * 16:(g + 1) * 16], cq2T[:, g, :],
                                         k2bd[:, g, :, :].rearrange("p a c -> p (a c)"), start=True, stop=True)
                    last.then_inc(sems["k2v2"], 1)

                def chain_p2T():
                    wait_n(pe, "k2v2", b, 2)
                    use_pa()
                    pe.transpose(pa[0:HEADS2 * NCA, 0:CTX], s2[:].rearrange("p h c -> p (h c)"), ident[0:CTX, 0:CTX])\
                      .then_inc(sems["pa_ready"], 1)

                def chain_c2T():
                    use_pa()
                    for g in range(QUADS):
                        last = pe.matmul(pa[:, g * CTX:(g + 1) * CTX], v2bd[:, g * P:(g + 1) * P], p2T[:], start=True, stop=True)
                    last.then_inc(sems["pa_ready"], 1)

                def chain_c2w():
                    use_pa()
                    for g in range(QUADS):
                        last = pe.matmul(pa[0:CTX, 0:DIM], c2T[:, g, :], woutp[:, g, :], start=(g == 0), stop=(g == QUADS - 1))
                    last.then_inc(sems["pa_ready"], 1)
                attention(2 * HEADS, 2 * HEADS2, {12: chain_cq2, 13: chain_s2, 14: chain_p2T, 15: chain_c2T, 16: chain_c2w})
                wait_n(pe, "o_ready", b, 2 * PAIRS + 2 * QUADS)
                wait_n(pe, "pa_taken", b, pa_n[0])
                for t in range(TT):
                    y = y_bank[:, t * DIM:(t + 1) * DIM]
                    for g in range(QUADS):
                        pe.matmul(y, hsT[:, g, t * P:(t + 1) * P], woutp[:, g, :], start=(g == 0), stop=False)
                    last = pe.matmul(y, ex[:, t * P:(t + 1) * P], c2w, start=False, stop=True)
                last.then_inc(sems["y_ready"], 1)
                assert pa_n[0] == PER["pa_ready"], pa_n
                assert pb_n[0] == PER["pb_ready"], pb_n
            batches(pe, one)


_OUTS = [((BATCH, TOK, DIM), "float32")]


def kernel(**inputs):
    import concourse.bacc as _bacc
    from concourse.bass_utils import run_bass_kernel_spmd as _run

    a = {k: np.ascontiguousarray(v) for k, v in inputs.items()}

    def l0(n):
        return a["L0_xattn_" + n]

    def l1(n):
        return a["L1_xattn_" + n]

    def pad_cols(w):
        out = np.zeros((w.shape[0], HEADS2, PADH), w.dtype)
        out[:, :, :DH2] = w.reshape(w.shape[0], HEADS2, DH2)
        return out.reshape(w.shape[0], PADW)

    def pad_rows(w):
        out = np.zeros((HEADS2, PADH, w.shape[1]), w.dtype)
        out[:, :DH2] = w.reshape(HEADS2, DH2, w.shape[1])
        return out.reshape(QUADS, P, w.shape[1]).transpose(1, 0, 2)

    ws = [l0("wq1"), l0("wk1"), l0("wv1"), l0("wq2"), l0("w_ff1")]
    cols = []
    for k in (1, 2, 3):
        g, be = l0(f"g{k}"), l0(f"be{k}")
        z = np.zeros((REM,), g.dtype)
        cols += [g[:P], be[:P], np.concatenate([g[P:]] * 3 + [z]), np.concatenate([be[P:]] * 3 + [z])]
    cols += list(l0("b_ff1").reshape(2 * FT, P))
    index = np.linspace(0, CTX - 1, TOK).astype(np.int64)
    expand = np.zeros((CTX, TOK), np.float32)
    expand[index, np.arange(TOK)] = 1.0
    mask_k = np.zeros((P, 4, NCA), np.float32)
    mask_v = np.zeros((HEADS2 * NCA, HEADS2, PADH), np.float32)
    for h in range(4):
        mask_k[PADH * h:PADH * (h + 1), h] = 1.0
    for h in range(HEADS2):
        mask_v[NCA * h:NCA * (h + 1), h] = 1.0
    arrays = dict(
        x=a["x"], ctx=a["ctx_768"],
        w_main=np.stack([w[:P] for w in ws]),
        w_rem=np.stack([np.concatenate([w[P:]] * 3) for w in ws]),
        w_ctx=np.stack([l0("wk2"), l0("wv2")]),
        w_o=np.stack([l0("wo1"), l0("wo2")]),
        w_f2=l0("w_ff2"),
        wq_p=pad_rows(pad_cols(l1("Wq"))), wk_p=pad_cols(l1("Wk")), wv_p=pad_cols(l1("Wv")),
        wqca_p=pad_cols(l1("Wq_ca")), wkca_p=pad_cols(l1("Wk_ca")), wvca_p=pad_cols(l1("Wv_ca")),
        wout_p=pad_rows(l1("Wout")),
        cols=np.stack(cols, axis=1),
        rows=np.stack([l0("bo1"), l0("bo2"), l0("b_ff2"), l1("b_out")])[None],
        expand=expand, mask_k=mask_k, mask_v=mask_v.reshape(HEADS2 * NCA, PADW))
    nc = _bacc.Bacc("TRN2", target_bir_lowering=False, num_devices=1)
    aps, feed = {}, {}
    for name, v in arrays.items():
        v = np.ascontiguousarray(v)
        feed[f"in_{name}"] = v
        aps[name] = nc.dram_tensor(f"in_{name}", v.shape, mybir.dt.from_np(v.dtype), kind="ExternalInput").ap()
    out = nc.dram_tensor("out_0", _OUTS[0][0], F32, kind="ExternalOutput").ap()
    build(nc, out=out, **aps)
    r = _run(nc, [feed], core_ids=[0])
    return r.results[0]["out_0"]
```

```python
from contextlib import ExitStack

import numpy as np

import concourse.bass as bass
from concourse import mybir

ALU = mybir.AluOpType
ACT = mybir.ActivationFunctionType
AX = mybir.AxisListType
F32 = mybir.dt.float32
F32R = mybir.dt.float32r

BATCH, TOK, DIM, CTX = 8, 256, 160, 96
HEADS, DH = 20, 64
INNER = HEADS * DH
DFF = 640
HEADS2, DH2, NCA = 8, 20, 4
P = 128
REM = DIM - P
STACK = 3 * REM
TT = TOK // P
PAIRS = HEADS // 2
CHUNKS = INNER // 256
FT = DFF // P
PADH = 32
QUADS = HEADS2 // 4
PADW = HEADS2 * PADH
KEYS2 = TOK - NCA
EPS = 1e-5
GELU_C = 0.7978845608028654
GELU_A = 0.044715

UNITS = ([("self", h) for h in range(HEADS)] + [("cross", h) for h in range(HEADS)]
         + [("ca", h) for h in range(HEADS2)] + [("enc", h) for h in range(HEADS2)])
NU = len(UNITS)
GROUPS = 2 * PAIRS + 2 * QUADS
FIRST = {"self": 0, "cross": HEADS, "ca": 2 * HEADS, "enc": 2 * HEADS + HEADS2}
RING = 4
RINGT = 8
LAG_T = 2
LAG_V = 3
LAG_O = 4

PA_N = PAIRS + 2 * CHUNKS + 3
PB_N = 2 * CHUNKS + 7

PER = dict(scores_ready=NU, exp_done=NU, max_ready=NU, recip_ready=NU, norm_ready=NU, tr_ready=NU,
           pT_ready=NU, pv_ready=2 * PAIRS + 2 * QUADS, o_ready=2 * PAIRS + 2 * QUADS,
           wo_done=2 * PAIRS, y_ready=2, y_taken=4,
           pa_ready=PA_N, pa_taken=PA_N, pb_ready=PB_N, pb_taken=PB_N,
           hi_ready=7, lo_ready=7, xn_ready=6, res_ready=4, xaff_ready=7, ln_step=6,
           stats_ready=3, rstd_ready=3,
           ff_g_ready=FT, ff_a_ready=FT, ff_g_taken=FT, ff_a_taken=FT,
           ff_cube=FT, ff_u=FT, ff_tanh=FT, ff_h=FT,
           chain_ready=5, chain_taken=5, chain_step=3, s2_exp=1, s2_norm=1)


def unit_queries(kind):
    return CTX if kind == "ca" else TOK


def unit_keys(kind):
    return KEYS2 if kind == "enc" else TOK


def group_of(u):
    if u < 0:
        return group_of(u + NU) - GROUPS
    if u < 2 * HEADS:
        return u // 2
    return 2 * PAIRS + (u - 2 * HEADS) // 4


def groups_units(g):
    if g < 0:
        return [u - NU for u in groups_units(g + GROUPS)]
    if g < 2 * PAIRS:
        return [2 * g, 2 * g + 1]
    first = 2 * HEADS + 4 * (g - 2 * PAIRS)
    return list(range(first, first + 4))


def build(nc, x, ctx, w_main, w_rem, w_ctx, w_o, w_f2, wq_p, wk_p, wv_p, wqca_p, wkca_p, wvca_p,
          wout_p, cols, rows, expand, mask_k, mask_v, out):
    es = ExitStack()
    with es:
        def sb(name, shape, dt=F32):
            return es.enter_context(nc.sbuf_tensor(name, shape, dt))

        sems = {}

        def sem(name):
            sems[name] = es.enter_context(nc.semaphore(name))
            return sems[name]

        NW = 5
        W_Q1, W_K1, W_V1, W_Q2, W_F1 = range(NW)
        w_hi = sb("w_hi", [P, NW, INNER], F32R)
        w_lo = sb("w_lo", [P, NW, INNER], F32R)
        w_st = sb("w_st", [STACK, NW, INNER], F32R)
        wc_hi = sb("wc_hi", [CTX, 2, INNER], F32R)
        wc_lo = sb("wc_lo", [CTX, 2, INNER], F32R)
        wo = sb("wo", [P, 2 * PAIRS, DIM])
        wf2 = sb("wf2", [P, FT, DIM])
        wq2p = sb("wq2p", [P, QUADS, PADW])
        wk2p = sb("wk2p", [CTX, PADW])
        wv2p = sb("wv2p", [CTX, PADW])
        wqca = sb("wqca", [NCA, PADW])
        wkca = sb("wkca", [CTX, PADW])
        wvca = sb("wvca", [CTX, PADW])
        woutp = sb("woutp", [P, QUADS, DIM])
        col = sb("col", [P, 12 + 2 * FT])
        row = sb("row", [P, 4, DIM])
        ex = sb("ex", [CTX, TOK])
        mk = sb("mk", [P, 4, NCA])
        mv = sb("mv", [HEADS2 * NCA, PADW])
        ident = sb("ident", [P, P])
        half_c = sb("half_c", [P, TT])

        x_in = sb("x_in", [P, TT, DIM])
        ctx_in = sb("ctx_in", [P, TT, CTX])
        ca_in = sb("ca_in", [NCA, CTX])
        x_cur = sb("x_cur", [P, TT, DIM])
        x_res = sb("x_res", [P, TT, DIM])
        stats = sb("stats", [P, TT, 6])
        mv_ln = sb("mv_ln", [P, TT, 2])
        wait_pad = sb("wait_pad", [P, 1])
        var_e = sb("var_e", [P, TT])
        rstd = sb("rstd", [P, TT])
        xn = sb("xn", [P, TT, P + STACK])
        xaff = sb("xaff", [P, 2, TOK])
        x_hi = sb("x_hi", [P, TOK], F32R)
        x_lo = sb("x_lo", [P, TOK], F32R)
        x_st = sb("x_st", [STACK, TOK], F32R)
        cT = sb("cT", [CTX, TOK])
        ca_rep = sb("ca_rep", [CTX, HEADS2, NCA])
        cT_hi = sb("cT_hi", [CTX, TOK], F32R)
        cT_lo = sb("cT_lo", [CTX, TOK], F32R)
        qk_buf = sb("qk_buf", [P, PAIRS * 2 * TOK])
        val_buf = sb("val_buf", [P, TT * INNER])
        qk = qk_buf[:].rearrange("p (j s t) -> p j s t", j=PAIRS, s=2)
        val = val_buf[:].rearrange("p (t n) -> p t n", t=TT)
        prob = sb("prob", [P, RING, 2 * TOK])
        pT = sb("pT", [P, RINGT, TT, TOK])
        nmax = sb("nmax", [P, RINGT, TT])
        rsum = sb("rsum", [P, RINGT, TT])
        rinv = sb("rinv", [P, RINGT, TT])
        oT = sb("oT", [P, 2, TOK])
        f_g, f_w, f_h = (qk_buf[:, n * DFF * TT:(n + 1) * DFF * TT].rearrange("p (j t) -> p j t", j=FT) for n in range(3))
        over_at = [PAIRS * TOK]

        def over_qk(parts, groups, width):
            at = over_at[0]
            over_at[0] += groups * width
            assert over_at[0] <= PAIRS * 2 * TOK
            return qk_buf[0:parts, at:at + groups * width].rearrange("p (g t) -> p g t", g=groups)

        x3T, q2T, hsT = (over_qk(P, QUADS, TOK) for _ in range(3))
        hs1T, cq2T, c2T = (over_qk(P, QUADS, CTX) for _ in range(3))
        c2w = over_qk(CTX, 1, DIM)[:, 0, :]
        x3p = sb("x3p", [P, TT, PADW])
        k2T = sb("k2T", [P, QUADS, TOK])
        v2p = sb("v2p", [P, TT, PADW])
        cq1T = sb("cq1T", [P, QUADS, CTX])
        k2bd = sb("k2bd", [P, QUADS, 4, NCA])
        v2bd = sb("v2bd", [HEADS2 * NCA, PADW])
        s2 = sb("s2", [CTX, HEADS2, NCA])
        s2m = sb("s2m", [CTX, HEADS2])
        s2s = sb("s2s", [CTX, HEADS2])
        s2r = sb("s2r", [CTX, HEADS2])
        p2T = sb("p2T", [HEADS2 * NCA, CTX])
        o_sb = sb("o_sb", [P, TT, DIM])
        stage_m = [qk_buf[:, n * INNER:(n + 1) * INNER] for n in range(2)]
        stage_r = [qk_buf[0:STACK, 2 * INNER:3 * INNER], val_buf[0:STACK, 0:INNER]]

        def bank(name):
            return es.enter_context(nc.psum_tensor(name, [P, 512], F32))

        s_bank = [bank("s_bank0"), bank("s_bank1")]
        t_bank = [bank("t_bank0"), bank("t_bank1")]
        o_bank, y_bank, pa, pb = bank("o_bank"), bank("y_bank"), bank("pa"), bank("pb")
        ff_g_bank = [t_bank[0], t_bank[1], o_bank, pa, pb]
        ff_a_bank = [s_bank[0], s_bank[1]]

        for name in PER:
            sem(name)
        w_loaded = [[es.enter_context(nc.semaphore(f"w_loaded{i}")) for i in range(2)]][0]
        wc_loaded = sem("wc_loaded")
        small_loaded = sem("small_loaded")
        w_hi_ready, w_lo_ready = sem("w_hi_ready"), sem("w_lo_ready")
        x_loaded, ctx_loaded, out_stored = sem("x_loaded"), sem("ctx_loaded"), sem("out_stored")
        ident_ready, l1_scaled = sem("ident_ready"), sem("l1_scaled")

        NSMALL = 14

        def count(name, b, n):
            return b * PER[name] + n

        def wait_n(eng, name, b, n):
            if not isinstance(b, int) or count(name, b, n) > 0:
                eng.wait_ge(sems[name], count(name, b, n))

        def batches(eng, one):
            one(0, False)
            with eng.Fori(1, BATCH - 1) as b:
                one(b, False)
            one(BATCH - 1, True)

        block = es.enter_context(nc.Block())

        @block.sync
        def _(sp):
            with nc.allow_non_contiguous_dma(reason="vectors and padded heads"):
                for dst, src in ((col[:], cols), (row[:], rows.to_broadcast([P, 4, DIM])),
                                 (wf2[:], w_f2.rearrange("(j p) e -> p j e", p=P)),
                                 (wq2p[:], wq_p), (wk2p[:], wk_p), (wv2p[:], wv_p), (wqca[:], wqca_p),
                                 (wkca[:], wkca_p), (wvca[:], wvca_p), (woutp[:], wout_p), (ex[:], expand),
                                 (mk[:], mask_k), (mv[:], mask_v)):
                    sp.dma_start(dst, src).then_inc(small_loaded, 16)
                sp.dma_start(wo[:], w_o.rearrange("a (j p) e -> p (a j) e", p=P)).then_inc(small_loaded, 16)

            def load(b, ahead):
                if ahead:
                    sp.wait_ge(sems["xn_ready"], count("xn_ready", b, 2))
                    sp.wait_ge(sems["res_ready"], count("res_ready", b, 1))
                sp.dma_start(x_in[:], x[b + ahead].rearrange("(t p) e -> p t e", p=P)).then_inc(x_loaded, 16)
                if ahead:
                    sp.wait_ge(sems["pa_ready"], count("pa_ready", b, PA_N - 1))
                sp.dma_start(ctx_in[:], ctx[b + ahead].rearrange("(t p) e -> p t e", p=P)).then_inc(ctx_loaded, 16)
                sp.dma_start(ca_in[:], ctx[b + ahead, KEYS2:TOK, :]).then_inc(ctx_loaded, 16)

            def one(b, last):
                if not last:
                    load(b, 1)
                sp.wait_ge(sems["y_taken"], count("y_taken", b, 4))
                sp.dma_start(out[b].rearrange("(t p) e -> p t e", p=P), o_sb[:]).then_inc(out_stored, 16)
            sp.sem_inc(out_stored, 16)
            load(0, 0)
            batches(sp, one)
            sp.wait_ge(out_stored, 16 * BATCH + 16)

        @block.gpsimd
        def _(pool):
            pool.memset(ident[:], 0.0).then_inc(ident_ready, 1)
            pool.memset(half_c[:], -0.5).then_inc(ident_ready, 1)
            pool.memset(x3p[:], 0.0).then_inc(ident_ready, 1)
            pool.wait_ge(ident_ready, 3)
            pool.affine_select(out=ident[:], in_=ident[:], compare_op=ALU.not_equal, fill=1.0, base=0,
                               pattern=[[-1, P]], channel_multiplier=1).then_inc(ident_ready, 1)
            pool.wait_ge(small_loaded, 16 * NSMALL)

            def normalise(b, u):
                kind, _ = UNITS[u]
                q, k = unit_queries(kind), unit_keys(kind)
                pool.wait_ge(sems["recip_ready"], count("recip_ready", b, u + 1))
                if kind == "ca":
                    p = prob[0:q, u % RING, 0:k]
                    r = rinv[0:q, u % RINGT, 0:1].to_broadcast([q, k])
                else:
                    p = prob[:, u % RING, 0:2 * k].rearrange("p (t k) -> p t k", t=2)
                    r = rinv[:, u % RINGT, :].rearrange("p (t o) -> p t o", o=1).to_broadcast([P, 2, k])
                pool.tensor_tensor(p, p, r, ALU.mult).then_inc(sems["norm_ready"], 1)

            def rstd_of(b, n, k):
                pool.wait_ge(sems["stats_ready"], count("stats_ready", b, 3 * n + k + 1))
                pool.tensor_tensor(rstd[:], var_e[:], half_c[:], ALU.pow).then_inc(sems["rstd_ready"], 1)

            def residual(b, k):
                if k == 0:
                    pool.wait_ge(x_loaded, 16 * b + 16)
                    wait_n(pool, "y_taken", b, 0)
                    pool.tensor_tensor(x_res[:], x_in[:], row[:, 0, :].rearrange("p (o e) -> p o e", o=1).to_broadcast([P, TT, DIM]),
                                       ALU.add).then_inc(sems["res_ready"], 1)
                elif k < 3:
                    pool.wait_ge(sems["y_taken"], count("y_taken", b, k))
                    pool.tensor_tensor(x_res[:], x_cur[:], row[:, k, :].rearrange("p (o e) -> p o e", o=1).to_broadcast([P, TT, DIM]),
                                       ALU.add).then_inc(sems["res_ready"], 1)
                else:
                    pool.wait_ge(sems["y_taken"], count("y_taken", b, 3))
                    for t in range(TT):
                        ins = pool.tensor_tensor(
                            x_res[:, t, :].rearrange("p (h d) -> p h d", d=DH2),
                            x3p[:, t, :].rearrange("p (h d) -> p h d", d=PADH)[:, :, 0:DH2],
                            row[:, 3, :].rearrange("p (h d) -> p h d", d=DH2), ALU.add)
                    ins.then_inc(sems["res_ready"], 1)

            def one(b, last):
                for u in range(0, HEADS):
                    normalise(b, u)
                    if u == 5:
                        residual(b, 0)
                rstd_of(b, 0, 1)
                residual(b, 1)
                for u in range(HEADS, 2 * HEADS):
                    normalise(b, u)
                rstd_of(b, 0, 2)
                residual(b, 2)
                for j in range(FT):
                    pool.wait_ge(sems["ff_g_taken"], count("ff_g_taken", b, j + 1))
                    pool.tensor_tensor(f_w[:, j, :], f_w[:, j, :], f_g[:, j, :], ALU.mult).then_inc(sems["ff_cube"], 1)
                residual(b, 3)
                for u in range(2 * HEADS, NU):
                    normalise(b, u)
                    if u == 2 * HEADS + 3 and not last:
                        rstd_of(b, 1, 0)
            rstd_of(0, 0, 0)
            batches(pool, one)

        @block.scalar
        def _(act):
            def load_w(i):
                if i >= 2:
                    act.wait_ge(w_lo_ready, 2 * (i - 1))
                act.dma_start(stage_m[i % 2], w_main[i]).then_inc(w_loaded[i % 2], 16)
                act.dma_start(stage_r[i % 2], w_rem[i]).then_inc(w_loaded[i % 2], 16)

            load_w(0)
            load_w(1)
            act.dma_start(pT[0:CTX, :, :, :].rearrange("p r t k -> p (r t k)")[:, 0:INNER], w_ctx[0]).then_inc(wc_loaded, 16)
            act.dma_start(pT[0:CTX, :, :, :].rearrange("p r t k -> p (r t k)")[:, INNER:2 * INNER], w_ctx[1]).then_inc(wc_loaded, 16)
            for i in range(NW):
                act.wait_ge(w_loaded[i % 2], 32 * (i // 2 + 1))
                sc = DH ** -0.5 if i in (W_Q1, W_Q2) else 1.0
                act.activation(w_hi[:, i, :], stage_m[i % 2], ACT.Copy, scale=sc).then_inc(w_hi_ready, 1)
                act.activation(w_st[:, i, :], stage_r[i % 2], ACT.Copy, scale=sc).then_inc(w_hi_ready, 1)
                if i + 2 < NW:
                    load_w(i + 2)
            act.wait_ge(wc_loaded, 32)
            act.activation(wc_hi[:].rearrange("p a n -> p (a n)"),
                           pT[0:CTX, :, :, :].rearrange("p r t k -> p (r t k)")[:, 0:2 * INNER], ACT.Copy).then_inc(w_hi_ready, 1)
            act.wait_ge(small_loaded, 16 * NSMALL)
            act.activation(wq2p[:], wq2p[:], ACT.Copy, scale=DH2 ** -0.5).then_inc(l1_scaled, 1)
            act.activation(wqca[:], wqca[:], ACT.Copy, scale=DH2 ** -0.5).then_inc(l1_scaled, 1)
            act.wait_ge(w_lo_ready, 2 * NW + 1)

            def exps(b, u):
                kind, _ = UNITS[u]
                q, k = unit_queries(kind), unit_keys(kind)
                act.wait_ge(sems["max_ready"], count("max_ready", b, u + 1))
                wait_n(act, "tr_ready", b, u + 1 - RING)
                tiles = 1 if kind == "ca" else 2
                for t in range(tiles):
                    last = act.activation(prob[0:min(q, P), u % RING, t * k:t * k + k],
                                          s_bank[u % 2][0:min(q, P), t * TOK:t * TOK + k], ACT.Exp,
                                          bias=nmax[0:min(q, P), u % RINGT, t:t + 1],
                                          accum_out=rsum[0:min(q, P), u % RINGT, t:t + 1])
                last.then_inc(sems["exp_done"], 1)

            def take_pT(b, u):
                kind, _ = UNITS[u]
                q, k = unit_queries(kind), unit_keys(kind)
                act.wait_ge(sems["tr_ready"], count("tr_ready", b, u + 1))
                prev = u - RINGT
                wait_n(act, "pv_ready", b, group_of(prev) + 1)
                src = t_bank[u % 2][:, 0:2 * q].rearrange("p (t q) -> p t q", t=2)
                if k == TOK:
                    act.activation(pT[:, u % RINGT, :, 0:q], src, ACT.Copy).then_inc(sems["pT_ready"], 1)
                else:
                    act.activation(pT[:, u % RINGT, 0, 0:q], src[:, 0, :], ACT.Copy)
                    act.activation(pT[0:k - P, u % RINGT, 1, 0:q], src[0:k - P, 1, :], ACT.Copy)\
                       .then_inc(sems["pT_ready"], 1)

            def take_pa(b, n, dst, src):
                act.wait_ge(sems["pa_ready"], count("pa_ready", b, n + 1))
                act.activation(dst, src, ACT.Copy).then_inc(sems["pa_taken"], 1)

            def high_halves(b, n, k):
                act.wait_ge(sems["xaff_ready"], count("xaff_ready", b, 7 * n + 2 * k + 2))
                act.activation(x_hi[:], xaff[:, 0, :], ACT.Copy).then_inc(sems["hi_ready"], 1)
                act.wait_ge(sems["xaff_ready"], count("xaff_ready", b, 7 * n + 2 * k + 3))
                act.activation(x_st[:], xaff[0:STACK, 1, :], ACT.Copy).then_inc(sems["hi_ready"], 1)

            def attention(b, first, n, between, behind=0, tail=True):
                for s in range(n + (LAG_T if tail else 0)):
                    if s < n:
                        exps(b, first + s)
                    if first - behind <= first + s - LAG_T < first + n:
                        take_pT(b, first + s - LAG_T)
                    between(s)

            flat = pa[:, :]
            pairs_of = [flat.rearrange("p (j t) -> p j t", j=2), pb[:, :].rearrange("p (j t) -> p j t", j=2)]
            qk_flat = [qk[:, j, :, :].rearrange("p s t -> p (s t)") for j in range(PAIRS)]

            def chain(b, n, dst, src):
                act.wait_ge(sems["chain_ready"], count("chain_ready", b, n + 1))
                act.activation(dst, src, ACT.Copy).then_inc(sems["chain_taken"], 1)

            def context_high(b, n):
                act.wait_ge(sems["xaff_ready"], count("xaff_ready", b, 7 * n + 1))
                act.activation(cT_hi[:], cT[:], ACT.Copy).then_inc(sems["hi_ready"], 1)

            def first_pair(b, n):
                act.wait_ge(sems["pa_ready"], count("pa_ready", b, PA_N * n + 1))
                act.activation(qk_flat[0], flat, ACT.Copy).then_inc(sems["pa_taken"], 1)

            def chain_c2T(b):
                chain(b, 3 - 5, c2T.rearrange("p g t -> p (g t)"), y_bank[:, 0:QUADS * CTX])

            def chain_c2w(b):
                chain(b, 4 - 5, c2w, y_bank[0:CTX, 0:DIM])

            def one(b, last):
                pa_n = [1]
                pb_n = [2 + CHUNKS]

                def take(dst, src, in_pb=False):
                    n, name = (pb_n, "pb") if in_pb else (pa_n, "pa")
                    act.wait_ge(sems[name + "_ready"], count(name + "_ready", b, n[0] + 1))
                    act.activation(dst, src, ACT.Copy).then_inc(sems[name + "_taken"], 1)
                    n[0] += 1

                first = isinstance(b, int) and b == 0
                def self_between(s):
                    if not first and s == 1:
                        chain_c2T(b)
                    if not first and s == 2:
                        chain_c2w(b)
                    if s < HEADS and s % 2 == 0 and s // 2 + 1 < PAIRS:
                        take(qk_flat[s // 2 + 1], flat)
                    if s >= HEADS:
                        c = s - HEADS
                        take(qk[:, 2 * c:2 * c + 2, 1, :], pairs_of[0])

                def cross_between(s):
                    if s < HEADS and s % 4 == 0 and s // 4 + 1 < CHUNKS:
                        c = s // 4 + 1
                        take(qk[:, 2 * c:2 * c + 2, 0, :], pairs_of[0])

                def second_between(s):
                    if s == 11:
                        chain(b, 0, cq2T.rearrange("p g t -> p (g t)"), y_bank[:, 0:QUADS * CTX])
                    if s == 13:
                        act.wait_ge(sems["chain_taken"], count("chain_taken", b, 2))
                        act.activation(s2[:], s2[:], ACT.Exp).then_inc(sems["s2_exp"], 1)
                    if s == 15:
                        chain(b, 2, p2T[:], y_bank[0:HEADS2 * NCA, 0:CTX])
                    if not last and s == 4:
                        context_high(b, 1)
                    if not last and s == 8:
                        high_halves(b, 1, 0)
                    if not last and s == 14:
                        first_pair(b, 1)

                attention(b, 0, HEADS, self_between, behind=0 if first else LAG_T)
                for c in range(LAG_T, CHUNKS):
                    take(qk[:, 2 * c:2 * c + 2, 1, :], pairs_of[0])
                for c in range(CHUNKS):
                    take(val[:, :, 256 * c:256 * c + 256], pairs_of[1], True)
                high_halves(b, 0, 1)
                take(qk[:, 0:2, 0, :], pairs_of[0])
                attention(b, HEADS, HEADS, cross_between)
                take(k2T[:].rearrange("p g t -> p (g t)"), flat)
                pb_n[0] += 2
                take(v2p[:].rearrange("p t n -> p (t n)"), pb[:, :], True)
                take(cq1T[:].rearrange("p g t -> p (g t)"), flat[:, 0:QUADS * CTX])
                high_halves(b, 0, 2)
                for j in range(FT + 2):
                    if j < FT:
                        act.wait_ge(sems["ff_g_ready"], count("ff_g_ready", b, j + 1))
                        bias = col[:, 12 + FT + j:13 + FT + j]
                        act.activation(f_w[:, j, :], ff_g_bank[j][:, 0:TOK], ACT.Square, bias=bias)
                        act.activation(f_g[:, j, :], ff_g_bank[j][:, 0:TOK], ACT.Identity, bias=bias)\
                           .then_inc(sems["ff_g_taken"], 1)
                    if j >= 2:
                        i = j - 2
                        act.wait_ge(sems["ff_u"], count("ff_u", b, i + 1))
                        act.activation(f_w[:, i, :], f_w[:, i, :], ACT.Tanh, scale=GELU_C).then_inc(sems["ff_tanh"], 1)
                take(q2T.rearrange("p g t -> p (g t)"), flat)
                assert pa_n[0] == PA_N, pa_n

                attention(b, 2 * HEADS, 2 * HEADS2, second_between, tail=False)

            context_high(0, 0)
            high_halves(0, 0, 0)
            first_pair(0, 0)
            batches(act, one)

            def end_between(s):
                if s == 1:
                    chain_c2T(BATCH)
            attention(BATCH, 0, 0, end_between, behind=LAG_T)
            chain_c2w(BATCH)

        @block.vector
        def _(dve):
            for i in range(NW):
                sc = DH ** -0.5 if i in (W_Q1, W_Q2) else 1.0
                dve.wait_ge(w_hi_ready, 2 * i + 2)
                dve.scalar_tensor_tensor(out=w_lo[:, i, :], in0=stage_m[i % 2], scalar=sc,
                                         in1=w_hi[:, i, :].bitcast(F32), op0=ALU.mult, op1=ALU.subtract)\
                   .then_inc(w_lo_ready, 1)
                lo = slice(REM, 2 * REM)
                dve.scalar_tensor_tensor(out=w_st[lo, i, :], in0=stage_r[i % 2][lo], scalar=sc,
                                         in1=w_st[lo, i, :].bitcast(F32), op0=ALU.mult, op1=ALU.subtract)\
                   .then_inc(w_lo_ready, 1)
            dve.wait_ge(w_hi_ready, 2 * NW + 1)
            dve.tensor_tensor(wc_lo[:].rearrange("p a n -> p (a n)"),
                              pT[0:CTX, :, :, :].rearrange("p r t k -> p (r t k)")[:, 0:2 * INNER],
                              wc_hi[:].rearrange("p a n -> p (a n)").bitcast(F32), ALU.subtract).then_inc(w_lo_ready, 1)
            dve.wait_ge(small_loaded, 16 * NSMALL)
            dve.wait_ge(ident_ready, 4)

            def own(name, b, n, ins):
                ins.then_inc(sems[name], 1)
                dve.wait_ge(sems[name], count(name, b, n))

            def maxima(b, u):
                kind, _ = UNITS[u]
                q, k = unit_queries(kind), unit_keys(kind)
                dve.wait_ge(sems["scores_ready"], count("scores_ready", b, u + 1))
                if kind == "ca":
                    dve.tensor_reduce(nmax[0:q, u % RINGT, 0:1], s_bank[u % 2][0:q, 0:k], AX.X, ALU.max,
                                      negate=True).then_inc(sems["max_ready"], 1)
                else:
                    dve.tensor_reduce(nmax[:, u % RINGT, :],
                                      s_bank[u % 2][:, :].rearrange("p (t k) -> p t k", t=2)[:, :, 0:k],
                                      AX.X, ALU.max, negate=True).then_inc(sems["max_ready"], 1)

            def inverse(b, u):
                q = min(unit_queries(UNITS[u][0]), P)
                t = 1 if UNITS[u][0] == "ca" else TT
                dve.wait_ge(sems["exp_done"], count("exp_done", b, u + 1))
                dve.reciprocal(rinv[0:q, u % RINGT, 0:t], rsum[0:q, u % RINGT, 0:t]).then_inc(sems["recip_ready"], 1)

            def take_o(b, g):
                kind = UNITS[groups_units(g)[0]][0]
                dve.wait_ge(sems["pv_ready"], count("pv_ready", b, g + 1))
                if kind in ("self", "cross"):
                    wait_n(dve, "wo_done", b, g - 1)
                    dve.tensor_copy(oT[:, g % 2, :], o_bank[:, 0:TOK]).then_inc(sems["o_ready"], 1)
                elif kind == "ca":
                    dve.tensor_copy(hs1T[:, (g - 2 * PAIRS) % QUADS, :], o_bank[:, 0:CTX]).then_inc(sems["o_ready"], 1)
                else:
                    dve.tensor_copy(hsT[:, (g - 2 * PAIRS) % QUADS, :], o_bank[:, 0:TOK]).then_inc(sems["o_ready"], 1)

            def layer_norm(b, n, k, src):
                at = 6 * n + 2 * k
                for t in range(TT):
                    last = dve.bn_stats(stats[:, t, :], src[:, t, :])
                own("ln_step", b, at + 1, last)
                dve.memset(wait_pad[:], 0.0)
                for t in range(TT):
                    last = dve.bn_aggr(mv_ln[:, t, :], stats[:, t, :])
                own("ln_step", b, at + 2, last)
                dve.tensor_scalar(var_e[:], mv_ln[:, :, 1], EPS, None, ALU.add).then_inc(sems["stats_ready"], 1)
                dve.wait_ge(sems["rstd_ready"], count("rstd_ready", b, 3 * n + k + 1))
                for t in range(TT):
                    dve.tensor_scalar(xn[:, t, 0:P], src[:, t, 0:P], mv_ln[:, t, 0:1], rstd[:, t:t + 1],
                                      ALU.subtract, ALU.mult)
                    dve.tensor_scalar(
                        xn[:, t, P:P + STACK].rearrange("p (c r) -> p c r", c=3),
                        src[:, t, P:DIM].rearrange("p (o r) -> p o r", o=1).to_broadcast([P, 3, REM]),
                        mv_ln[:, t, 0:1], rstd[:, t:t + 1], ALU.subtract, ALU.mult).then_inc(sems["xn_ready"], 1)

            def affine_and_low(b, n, k, n_pb):
                dve.wait_ge(sems["pb_ready"], count("pb_ready", b, n * PB_N + n_pb + 1))
                dve.tensor_scalar(xaff[:, 0, :], pb[:, 0:TOK], col[:, 4 * k:4 * k + 1], col[:, 4 * k + 1:4 * k + 2],
                                  ALU.mult, ALU.add).then_inc(sems["xaff_ready"], 1)
                dve.tensor_scalar(xaff[0:STACK, 1, :], pb[0:STACK, TOK:2 * TOK], col[0:STACK, 4 * k + 2:4 * k + 3],
                                  col[0:STACK, 4 * k + 3:4 * k + 4], ALU.mult, ALU.add).then_inc(sems["xaff_ready"], 1)
                dve.wait_ge(sems["hi_ready"], count("hi_ready", b, 7 * n + 2 * k + 2))
                dve.tensor_tensor(x_lo[:], xaff[:, 0, :], x_hi[:].bitcast(F32), ALU.subtract).then_inc(sems["lo_ready"], 1)
                lo = slice(2 * REM, 3 * REM)
                dve.wait_ge(sems["hi_ready"], count("hi_ready", b, 7 * n + 2 * k + 3))
                dve.tensor_tensor(x_st[lo, :], xaff[lo, 1, :], x_st[lo, :].bitcast(F32), ALU.subtract)\
                   .then_inc(sems["lo_ready"], 1)
                dve.sem_inc(sems["pb_taken"], 1)

            def attention(b, first, n, between, behind=0, tail=True):
                for s in range(n + (LAG_V if tail else 0)):
                    if s < n:
                        maxima(b, first + s)
                    between(s)
                    if first - behind <= first + s - 1 < first + n:
                        inverse(b, first + s - 1)
                    last = first + s - LAG_V
                    if first - behind <= last < first + n and groups_units(group_of(last))[-1] == last:
                        take_o(b, group_of(last))

            def take_y(b, n):
                if n < 2:
                    dve.wait_ge(sems["wo_done"], count("wo_done", b, PAIRS * (n + 1)))
                else:
                    dve.wait_ge(sems["y_ready"], count("y_ready", b, n - 1))
                dve.wait_ge(sems["res_ready"], count("res_ready", b, n + 1))

            def context_rows(b, n):
                dve.wait_ge(sems["pb_ready"], count("pb_ready", b, n * PB_N + 1))
                dve.tensor_copy(ca_rep[:], pb[0:CTX, KEYS2:TOK].rearrange("p (o c) -> p o c", o=1)
                                .to_broadcast([CTX, HEADS2, NCA]))
                dve.tensor_copy(cT[:], pb[0:CTX, 0:TOK]).then_inc(sems["xaff_ready"], 1)
                dve.wait_ge(sems["hi_ready"], count("hi_ready", b, 7 * n + 1))
                dve.tensor_tensor(cT_lo[:], cT[:], cT_hi[:].bitcast(F32), ALU.subtract).then_inc(sems["lo_ready"], 1)
                dve.sem_inc(sems["pb_taken"], 1)

            def x_rows(b, n):
                dve.wait_ge(x_loaded, 16 * (b + n) + 16)
                layer_norm(b, n, 0, x_in)

            def sum_y(b, n, dst):
                take_y(b, n)
                dve.tensor_tensor(dst[:].rearrange("p t e -> p (t e)"), y_bank[:, 0:TT * DIM],
                                  x_res[:].rearrange("p t e -> p (t e)"), ALU.add).then_inc(sems["y_taken"], 1)

            def result(b):
                dve.wait_ge(sems["y_ready"], count("y_ready", b, 0))
                dve.wait_ge(sems["res_ready"], count("res_ready", b, 0))
                dve.wait_ge(out_stored, 16 * b)
                dve.tensor_tensor(o_sb[:].rearrange("p t e -> p (t e)"), y_bank[:, 0:TT * DIM],
                                  x_res[:].rearrange("p t e -> p (t e)"), ALU.add).then_inc(sems["y_taken"], 1)

            def one(b, last):
                pb_n = [2]
                first = isinstance(b, int) and b == 0

                def take(dst, src):
                    dve.wait_ge(sems["pb_ready"], count("pb_ready", b, pb_n[0] + 1))
                    dve.tensor_copy(dst, src).then_inc(sems["pb_taken"], 1)
                    pb_n[0] += 1

                def self_between(s):
                    if not first and s == 3:
                        result(b)
                    if s % 4 == 1 and s // 4 < CHUNKS:
                        c = s // 4
                        take(val[:, :, 256 * c:256 * c + 256], pb[:, :].rearrange("p (t n) -> p t n", t=2))
                attention(b, 0, HEADS, self_between, behind=0 if first else LAG_V)
                pb_n[0] += CHUNKS
                sum_y(b, 0, x_cur)
                dve.wait_ge(sems["y_taken"], count("y_taken", b, 1))
                layer_norm(b, 0, 1, x_cur)
                affine_and_low(b, 0, 1, pb_n[0])
                pb_n[0] += 1

                def blocks():
                    dve.wait_ge(sems["pb_ready"], count("pb_ready", b, pb_n[0] + 1))
                    for g in range(QUADS):
                        dve.tensor_tensor(k2bd[:, g, :, :],
                                          pb[:, g * NCA:(g + 1) * NCA].rearrange("p (o c) -> p o c", o=1)
                                          .to_broadcast([P, 4, NCA]), mk[:], ALU.mult)
                    dve.tensor_tensor(v2bd[:], pb[0:HEADS2 * NCA, 64:64 + PADW], mv[:], ALU.mult)\
                       .then_inc(sems["pb_taken"], 1)
                    pb_n[0] += 1

                def cross_between(s):
                    if s == 17:
                        blocks()
                attention(b, HEADS, HEADS, cross_between)
                pb_n[0] += 1
                sum_y(b, 1, x_cur)
                dve.wait_ge(sems["y_taken"], count("y_taken", b, 2))
                layer_norm(b, 0, 2, x_cur)
                affine_and_low(b, 0, 2, pb_n[0])
                pb_n[0] += 1

                for j in range(FT + 3):
                    if j < FT:
                        dve.wait_ge(sems["ff_a_ready"], count("ff_a_ready", b, j + 1))
                        dve.wait_ge(sems["ff_g_taken"], count("ff_g_taken", b, j + 1))
                        dve.scalar_tensor_tensor(out=f_h[:, j, :], in0=ff_a_bank[j % 2][:, 0:TOK],
                                                 scalar=col[:, 12 + j:13 + j], in1=f_g[:, j, :],
                                                 op0=ALU.add, op1=ALU.mult).then_inc(sems["ff_a_taken"], 1)
                    if 1 <= j <= FT:
                        i = j - 1
                        dve.wait_ge(sems["ff_cube"], count("ff_cube", b, i + 1))
                        dve.scalar_tensor_tensor(out=f_w[:, i, :], in0=f_w[:, i, :], scalar=GELU_A, in1=f_g[:, i, :],
                                                 op0=ALU.mult, op1=ALU.add).then_inc(sems["ff_u"], 1)
                    if j >= 3:
                        i = j - 3
                        dve.wait_ge(sems["ff_tanh"], count("ff_tanh", b, i + 1))
                        dve.scalar_tensor_tensor(out=f_h[:, i, :], in0=f_w[:, i, :], scalar=1.0, in1=f_h[:, i, :],
                                                 op0=ALU.add, op1=ALU.mult).then_inc(sems["ff_h"], 1)
                take_y(b, 2)
                for t in range(TT):
                    ins = dve.scalar_tensor_tensor(
                        out=x3p[:, t, :].rearrange("p (h d) -> p h d", d=PADH)[:, :, 0:DH2],
                        in0=y_bank[:, t * DIM:(t + 1) * DIM].rearrange("p (h d) -> p h d", d=DH2), scalar=0.5,
                        in1=x_res[:, t, :].rearrange("p (h d) -> p h d", d=DH2), op0=ALU.mult, op1=ALU.add)
                ins.then_inc(sems["y_taken"], 1)
                take(x3T.rearrange("p g t -> p (g t)"), pb[:, :])
                assert pb_n[0] == PB_N, pb_n

                def chain_softmax():
                    dve.wait_ge(sems["chain_ready"], count("chain_ready", b, 2))
                    s3 = y_bank[0:CTX, 0:HEADS2 * NCA].rearrange("p (h c) -> p h c", c=NCA)
                    own("chain_step", b, 1, dve.tensor_reduce(s2m[:], s3, AX.X, ALU.max))
                    dve.tensor_tensor(s2[:], s3, s2m[:].rearrange("p (h o) -> p h o", o=1).to_broadcast([CTX, HEADS2, NCA]),
                                      ALU.subtract).then_inc(sems["chain_taken"], 1)

                def chain_norm():
                    dve.wait_ge(sems["s2_exp"], count("s2_exp", b, 1))
                    own("chain_step", b, 2, dve.tensor_reduce(s2s[:], s2[:], AX.X, ALU.add))
                    own("chain_step", b, 3, dve.reciprocal(s2r[:], s2s[:]))
                    dve.tensor_tensor(s2[:], s2[:], s2r[:].rearrange("p (h o) -> p h o", o=1).to_broadcast([CTX, HEADS2, NCA]),
                                      ALU.mult).then_inc(sems["s2_norm"], 1)

                def second_between(s):
                    if s == 13:
                        chain_softmax()
                    if s == 14:
                        chain_norm()
                    if not last and s == 4:
                        context_rows(b, 1)
                    if not last and s == 5:
                        x_rows(b, 1)
                    if not last and s == 8:
                        affine_and_low(b, 1, 0, 1)
                attention(b, 2 * HEADS, 2 * HEADS2, second_between, tail=False)
            context_rows(0, 0)
            x_rows(0, 0)
            affine_and_low(0, 0, 0, 1)
            batches(dve, one)
            attention(BATCH, 0, 0, lambda s: None, behind=LAG_V)
            result(BATCH)

        @block.tensor
        def _(pe):
            pe.wait_ge(ident_ready, 4)

            def split_product(out_ap, w_i, wcols, x_is_weight, tok=slice(0, TOK)):
                pairs = [(w_hi[:, w_i, wcols], x_hi[:, tok]), (w_lo[:, w_i, wcols], x_hi[:, tok]),
                         (w_hi[:, w_i, wcols], x_lo[:, tok]), (w_st[:, w_i, wcols], x_st[:, tok])]
                for n, (w, a) in enumerate(pairs):
                    l, r = (a, w) if x_is_weight else (w, a)
                    last = pe.matmul(out_ap, l, r, start=(n == 0), stop=(n == 3))
                return last

            def split_ctx(out_ap, w_i, wcols, x_is_weight, tok=slice(0, TOK)):
                pairs = [(wc_hi[:, w_i, wcols], cT_hi[:, tok]), (wc_lo[:, w_i, wcols], cT_hi[:, tok]),
                         (wc_hi[:, w_i, wcols], cT_lo[:, tok])]
                for n, (w, a) in enumerate(pairs):
                    l, r = (a, w) if x_is_weight else (w, a)
                    last = pe.matmul(out_ap, l, r, start=(n == 0), stop=(n == 2))
                return last

            def ctx_transposes(b, n):
                pe.wait_ge(ctx_loaded, 32 * (b + n) + 32)
                wait_n(pe, "pb_taken", b, n * PB_N)
                for t in range(TT):
                    last = pe.transpose(pb[0:CTX, t * P:(t + 1) * P], ctx_in[:, t, :], ident[:])
                last.then_inc(sems["pb_ready"], 1)

            def ln_transposes(b, n, k, n_pb):
                pe.wait_ge(sems["pb_taken"], count("pb_taken", b, n * PB_N + n_pb))
                for t in range(TT):
                    pe.wait_ge(sems["xn_ready"], count("xn_ready", b, 6 * n + 2 * k + t + 1))
                    pe.transpose(pb[:, t * P:(t + 1) * P], xn[:, t, 0:P], ident[:])
                    last = pe.transpose(pb[0:STACK, TOK + t * P:TOK + (t + 1) * P], xn[:, t, P:P + STACK], ident[:])
                last.then_inc(sems["pb_ready"], 1)

            def project_qk(b, n, j):
                wait_n(pe, "pa_taken", b, n * PA_N + j)
                c = slice(j * P, (j + 1) * P)
                split_product(pa[:, 0:TOK], W_Q1, c, False)
                split_product(pa[:, TOK:2 * TOK], W_K1, c, False).then_inc(sems["pa_ready"], 1)

            def first_pair(b, n):
                pe.wait_ge(sems["lo_ready"], count("lo_ready", b, 7 * n + 3))
                project_qk(b, n, 0)

            def one(b, last_batch):
                pa_n, pb_n = [1], [2]
                first_batch = isinstance(b, int) and b == 0

                def use_pa():
                    pe.wait_ge(sems["pa_taken"], count("pa_taken", b, pa_n[0]))
                    pa_n[0] += 1

                def use_pb():
                    pe.wait_ge(sems["pb_taken"], count("pb_taken", b, pb_n[0]))
                    pb_n[0] += 1

                def head_rows(kind, h):
                    if kind in ("self", "cross"):
                        return slice(DH * (h % 2), DH * (h % 2) + DH)
                    return slice(PADH * (h % 4), PADH * (h % 4) + DH2)

                def scores(u):
                    kind, h = UNITS[u]
                    r = head_rows(kind, h)
                    wait_n(pe, "exp_done", b, u - 1)
                    if kind == "self":
                        pe.wait_ge(sems["pa_taken"], count("pa_taken", b, 1 + h // 2))
                        qs, ks = qk[r, h // 2, 0, :], qk[r, h // 2, 1, :]
                    elif kind == "cross":
                        pe.wait_ge(sems["pa_taken"], count("pa_taken", b, PAIRS + CHUNKS + h // 4 + 1))
                        qs, ks = qk[r, h // 2, 0, :], qk[r, h // 2, 1, :]
                    elif kind == "ca":
                        pe.wait_ge(sems["pb_taken"], count("pb_taken", b, PB_N))
                        qs, ks = cq1T[r, h // 4, :], x3T[r, h // 4, :]
                    else:
                        pe.wait_ge(sems["pa_taken"], count("pa_taken", b, PA_N))
                        qs, ks = q2T[r, h // 4, :], k2T[r, h // 4, 0:KEYS2]
                    k = unit_keys(kind)
                    bank_ = s_bank[u % 2]
                    if kind == "ca":
                        last = pe.matmul(bank_[0:CTX, 0:k], qs, ks, start=True, stop=True)
                    else:
                        for t in range(TT):
                            last = pe.matmul(bank_[:, t * TOK:t * TOK + k], qs[:, t * P:(t + 1) * P], ks,
                                             start=True, stop=True)
                    last.then_inc(sems["scores_ready"], 1)

                def transposes(u):
                    kind, _ = UNITS[u]
                    q, k = unit_queries(kind), unit_keys(kind)
                    pe.wait_ge(sems["norm_ready"], count("norm_ready", b, u + 1))
                    wait_n(pe, "pT_ready", b, u - 1)
                    tb = t_bank[u % 2]
                    for c in range(2):
                        kk = min(P, k - c * P)
                        for t in range(1 if kind == "ca" else TT):
                            qq = min(q, P)
                            last = pe.transpose(tb[0:kk, c * q + t * P:c * q + t * P + qq],
                                                prob[0:qq, u % RING, t * k + c * P:t * k + c * P + kk],
                                                ident[0:qq, 0:qq])
                    last.then_inc(sems["tr_ready"], 1)

                def values(g):
                    us = groups_units(g)
                    kind = UNITS[us[0]][0]
                    q, k = unit_queries(kind), unit_keys(kind)
                    pe.wait_ge(sems["pT_ready"], count("pT_ready", b, us[-1] + 1))
                    wait_n(pe, "o_ready", b, g)
                    if kind == "self":
                        pe.wait_ge(sems["pb_taken"], count("pb_taken", b, 2 + g // 2 + 1))
                    for c in range(2):
                        kk = min(P, k - c * P)
                        for u in us:
                            h = UNITS[u][1]
                            if kind in ("self", "cross"):
                                v = val[:, c, h * DH:(h + 1) * DH]
                                rows_ = slice(DH * (h % 2), DH * (h % 2) + DH)
                            else:
                                src = x3p if kind == "ca" else v2p
                                v = src[0:kk, c, h * PADH:(h + 1) * PADH]
                                rows_ = slice(PADH * (h % 4), PADH * (h % 4) + PADH)
                            last = pe.matmul(o_bank[rows_, 0:q], v, pT[0:kk, u % RINGT, c, 0:q],
                                             start=(c == 0), stop=(c == 1), skip_group_check=True)
                    last.then_inc(sems["pv_ready"], 1)

                def project(g):
                    a = g // PAIRS
                    pe.wait_ge(sems["o_ready"], count("o_ready", b, g + 1))
                    if g % PAIRS == 0:
                        wait_n(pe, "y_taken", b, a)
                    for t in range(TT):
                        last = pe.matmul(y_bank[:, t * DIM:(t + 1) * DIM], oT[:, g % 2, t * P:(t + 1) * P], wo[:, g, :],
                                         start=(g % PAIRS == 0 and t == 0), stop=(g % PAIRS == PAIRS - 1),
                                         skip_group_check=True)
                    last.then_inc(sems["wo_done"], 1)

                def attention(first, n, between, behind=0, tail=True):
                    for s in range(n + (LAG_O + 1 if tail else 0)):
                        if s < n:
                            scores(first + s)
                        between(s)

                        def ends_group(lag):
                            u = first + s - lag
                            return first - behind <= u < first + n and groups_units(group_of(u))[-1] == u
                        if first - behind <= first + s - LAG_T < first + n:
                            transposes(first + s - LAG_T)
                        if ends_group(LAG_V):
                            values(group_of(first + s - LAG_V))
                        if ends_group(LAG_O) and 0 <= first + s - LAG_O < 2 * HEADS:
                            project(group_of(first + s - LAG_O))

                def project_v(c):
                    use_pb()
                    for t in range(TT):
                        last = split_product(pb[:, t * 256:(t + 1) * 256], W_V1, slice(256 * c, 256 * c + 256), True,
                                             slice(t * P, (t + 1) * P))
                    last.then_inc(sems["pb_ready"], 1)

                def project_k2(c):
                    use_pa()
                    for i in range(2):
                        j = 2 * c + i
                        last = split_ctx(pa[:, i * TOK:(i + 1) * TOK], 0, slice(j * P, (j + 1) * P), False)
                    last.then_inc(sems["pa_ready"], 1)

                def project_v2(c):
                    use_pb()
                    for t in range(TT):
                        last = split_ctx(pb[:, t * 256:(t + 1) * 256], 1, slice(256 * c, 256 * c + 256), True,
                                         slice(t * P, (t + 1) * P))
                    last.then_inc(sems["pb_ready"], 1)

                def project_q2(c):
                    use_pa()
                    for i in range(2):
                        j = 2 * c + i
                        last = split_product(pa[:, i * TOK:(i + 1) * TOK], W_Q2, slice(j * P, (j + 1) * P), False)
                    last.then_inc(sems["pa_ready"], 1)

                def chain_start():
                    pe.wait_ge(sems["o_ready"], count("o_ready", b, 2 * PAIRS + QUADS))
                    pe.wait_ge(sems["y_taken"], count("y_taken", b, 3))
                    for m in range(QUADS):
                        for g in range(QUADS):
                            last = pe.matmul(y_bank[:, m * CTX:(m + 1) * CTX], wq2p[:, g, m * P:(m + 1) * P], hs1T[:, g, :],
                                             start=(g == 0), stop=(g == QUADS - 1))
                    last.then_inc(sems["chain_ready"], 1)

                def chain_s2():
                    pe.wait_ge(sems["chain_taken"], count("chain_taken", b, 1))
                    for g in range(QUADS):
                        last = pe.matmul(y_bank[0:CTX, g * 16:(g + 1) * 16], cq2T[:, g, :],
                                         k2bd[:, g, :, :].rearrange("p a c -> p (a c)"), start=True, stop=True)
                    last.then_inc(sems["chain_ready"], 1)

                def chain_p2T():
                    pe.wait_ge(sems["s2_norm"], count("s2_norm", b, 1))
                    pe.transpose(y_bank[0:HEADS2 * NCA, 0:CTX], s2[:].rearrange("p h c -> p (h c)"), ident[0:CTX, 0:CTX])\
                      .then_inc(sems["chain_ready"], 1)

                def chain_c2T():
                    pe.wait_ge(sems["chain_taken"], count("chain_taken", b, 3 - 5))
                    for g in range(QUADS):
                        last = pe.matmul(y_bank[:, g * CTX:(g + 1) * CTX], v2bd[:, g * P:(g + 1) * P], p2T[:],
                                         start=True, stop=True)
                    last.then_inc(sems["chain_ready"], 1)

                def chain_c2w():
                    pe.wait_ge(sems["chain_taken"], count("chain_taken", b, 4 - 5))
                    for g in range(QUADS):
                        last = pe.matmul(y_bank[0:CTX, 0:DIM], c2T[:, g, :], woutp[:, g, :], start=(g == 0), stop=(g == QUADS - 1))
                    last.then_inc(sems["chain_ready"], 1)

                def final_projection():
                    pe.wait_ge(sems["o_ready"], count("o_ready", b, 0))
                    pe.wait_ge(sems["chain_taken"], count("chain_taken", b, 0))
                    for t in range(TT):
                        y = y_bank[:, t * DIM:(t + 1) * DIM]
                        for g in range(QUADS):
                            pe.matmul(y, hsT[:, g, t * P:(t + 1) * P], woutp[:, g, :], start=(g == 0), stop=False)
                        last = pe.matmul(y, ex[:, t * P:(t + 1) * P], c2w, start=False, stop=True)
                    last.then_inc(sems["y_ready"], 1)

                def last_batch_ends(s):
                    if s == 1:
                        chain_c2T()
                    if s == 2:
                        chain_c2w()
                    if s == 3:
                        final_projection()

                if last_batch is None:
                    attention(0, 0, last_batch_ends, behind=LAG_O)
                    return

                def self_between(s):
                    if not first_batch:
                        last_batch_ends(s)
                    if s % 2 == 0 and s // 2 + 1 < PAIRS:
                        use_pa()
                        project_qk(b, 0, s // 2 + 1)
                    if s % 4 == 1 and s // 4 < CHUNKS:
                        project_v(s // 4)
                    if s >= HEADS:
                        project_k2(s - HEADS)
                attention(0, HEADS, self_between, behind=0 if first_batch else LAG_O)
                for c in range(CHUNKS):
                    project_v2(c)
                use_pb()
                ln_transposes(b, 0, 1, pb_n[0] - 1)
                pe.wait_ge(sems["lo_ready"], count("lo_ready", b, 5))
                project_q2(0)

                def blocks():
                    use_pb()
                    for g in range(QUADS):
                        pe.matmul(pb[:, g * NCA:(g + 1) * NCA], wkca[:, g * P:(g + 1) * P], cT[:, KEYS2:TOK], start=True, stop=True)
                    pe.matmul(pb[0:HEADS2 * NCA, 64:64 + PADW], ca_rep[:].rearrange("p h c -> p (h c)"),
                              wvca[:], start=True, stop=True).then_inc(sems["pb_ready"], 1)

                def cross_between(s):
                    if s % 4 == 0 and s // 4 + 1 < CHUNKS:
                        project_q2(s // 4 + 1)
                    if s == 17:
                        blocks()
                attention(HEADS, HEADS, cross_between)
                use_pa()
                for g in range(QUADS):
                    last = pe.matmul(pa[:, g * TOK:(g + 1) * TOK], wk2p[:, g * P:(g + 1) * P], cT[:], start=True, stop=True)
                last.then_inc(sems["pa_ready"], 1)
                use_pb()
                for t in range(TT):
                    last = pe.matmul(pb[:, t * PADW:(t + 1) * PADW], cT[:, t * P:(t + 1) * P], wv2p[:], start=True, stop=True)
                last.then_inc(sems["pb_ready"], 1)
                use_pa()
                for g in range(QUADS):
                    last = pe.matmul(pa[:, g * CTX:(g + 1) * CTX], wqca[:, g * P:(g + 1) * P], ca_in[:], start=True, stop=True)
                last.then_inc(sems["pa_ready"], 1)
                use_pb()
                ln_transposes(b, 0, 2, pb_n[0] - 1)
                pe.wait_ge(sems["lo_ready"], count("lo_ready", b, 7))
                for j in range(FT):
                    if ff_g_bank[j] is pa:
                        pe.wait_ge(sems["pa_taken"], count("pa_taken", b, pa_n[0]))
                    if ff_g_bank[j] is pb:
                        pe.wait_ge(sems["pb_taken"], count("pb_taken", b, pb_n[0]))
                    split_product(ff_g_bank[j][:, 0:TOK], W_F1, slice(DFF + j * P, DFF + (j + 1) * P), False)\
                        .then_inc(sems["ff_g_ready"], 1)
                    if j >= 2:
                        pe.wait_ge(sems["ff_a_taken"], count("ff_a_taken", b, j - 1))
                    split_product(ff_a_bank[j % 2][:, 0:TOK], W_F1, slice(j * P, (j + 1) * P), False)\
                        .then_inc(sems["ff_a_ready"], 1)
                pe.wait_ge(sems["y_taken"], count("y_taken", b, 2))
                for j in range(FT):
                    pe.wait_ge(sems["ff_h"], count("ff_h", b, j + 1))
                    for t in range(TT):
                        last = pe.matmul(y_bank[:, t * DIM:(t + 1) * DIM], f_h[:, j, t * P:(t + 1) * P], wf2[:, j, :],
                                         start=(j == 0 and t == 0), stop=(j == FT - 1), skip_group_check=True)
                last.then_inc(sems["y_ready"], 1)
                pe.wait_ge(sems["y_taken"], count("y_taken", b, 3))
                use_pb()
                for g in range(QUADS):
                    for t in range(TT):
                        last = pe.transpose(pb[:, g * TOK + t * P:g * TOK + (t + 1) * P], x3p[:, t, g * P:(g + 1) * P], ident[:])
                last.then_inc(sems["pb_ready"], 1)
                use_pa()
                pe.wait_ge(sems["pb_taken"], count("pb_taken", b, pb_n[0]))
                for m in range(QUADS):
                    for g in range(QUADS):
                        last = pe.matmul(pa[:, m * TOK:(m + 1) * TOK], wq2p[:, g, m * P:(m + 1) * P], x3T[:, g, :],
                                         start=(g == 0), stop=(g == QUADS - 1))
                last.then_inc(sems["pa_ready"], 1)
                assert pa_n[0] == PA_N, pa_n
                assert pb_n[0] == PB_N, pb_n

                def second_between(s):
                    if s == 11:
                        chain_start()
                    if s == 13:
                        chain_s2()
                    if s == 15:
                        chain_p2T()
                    if not last_batch and s == 4:
                        ctx_transposes(b, 1)
                    if not last_batch and s == 7:
                        ln_transposes(b, 1, 0, 1)
                    if not last_batch and s == 14:
                        first_pair(b, 1)
                attention(2 * HEADS, 2 * HEADS2, second_between, tail=False)
            ctx_transposes(0, 0)
            ln_transposes(0, 0, 0, 1)
            pe.wait_ge(w_lo_ready, 2 * NW + 1)
            pe.wait_ge(small_loaded, 16 * NSMALL)
            pe.wait_ge(l1_scaled, 2)
            first_pair(0, 0)
            batches(pe, one)
            one(BATCH, None)



_OUTS = [((BATCH, TOK, DIM), "float32")]


def kernel(**inputs):
    import concourse.bacc as _bacc
    from concourse.bass_utils import run_bass_kernel_spmd as _run

    a = {k: np.ascontiguousarray(v) for k, v in inputs.items()}

    def l0(n):
        return a["L0_xattn_" + n]

    def l1(n):
        return a["L1_xattn_" + n]

    def pad_cols(w):
        out = np.zeros((w.shape[0], HEADS2, PADH), w.dtype)
        out[:, :, :DH2] = w.reshape(w.shape[0], HEADS2, DH2)
        return out.reshape(w.shape[0], PADW)

    def pad_rows(w):
        out = np.zeros((HEADS2, PADH, w.shape[1]), w.dtype)
        out[:, :DH2] = w.reshape(HEADS2, DH2, w.shape[1])
        return out.reshape(QUADS, P, w.shape[1]).transpose(1, 0, 2)

    ws = [l0("wq1"), l0("wk1"), l0("wv1"), l0("wq2"), l0("w_ff1")]
    cols = []
    for k in (1, 2, 3):
        g, be = l0(f"g{k}"), l0(f"be{k}")
        z = np.zeros((REM,), g.dtype)
        cols += [g[:P], be[:P], np.concatenate([g[P:]] * 3 + [z]), np.concatenate([be[P:]] * 3 + [z])]
    cols += list(l0("b_ff1").reshape(2 * FT, P))
    index = np.linspace(0, CTX - 1, TOK).astype(np.int64)
    expand = np.zeros((CTX, TOK), np.float32)
    expand[index, np.arange(TOK)] = 1.0
    mask_k = np.zeros((P, 4, NCA), np.float32)
    mask_v = np.zeros((HEADS2 * NCA, HEADS2, PADH), np.float32)
    for h in range(4):
        mask_k[PADH * h:PADH * (h + 1), h] = 1.0
    for h in range(HEADS2):
        mask_v[NCA * h:NCA * (h + 1), h] = 1.0
    arrays = dict(
        x=a["x"], ctx=a["ctx_768"],
        w_main=np.stack([w[:P] for w in ws]),
        w_rem=np.stack([np.concatenate([w[P:]] * 3) for w in ws]),
        w_ctx=np.stack([l0("wk2"), l0("wv2")]),
        w_o=np.stack([l0("wo1"), l0("wo2")]),
        w_f2=l0("w_ff2"),
        wq_p=pad_rows(pad_cols(l1("Wq"))), wk_p=pad_cols(l1("Wk")), wv_p=pad_cols(l1("Wv")),
        wqca_p=pad_cols(l1("Wq_ca")), wkca_p=pad_cols(l1("Wk_ca")), wvca_p=pad_cols(l1("Wv_ca")),
        wout_p=pad_rows(l1("Wout")),
        cols=np.stack(cols, axis=1),
        rows=np.stack([l0("bo1"), l0("bo2"), l0("b_ff2"), l1("b_out")])[None],
        expand=expand, mask_k=mask_k, mask_v=mask_v.reshape(HEADS2 * NCA, PADW))
    nc = _bacc.Bacc("TRN2", target_bir_lowering=False, num_devices=1)
    aps, feed = {}, {}
    for name, v in arrays.items():
        v = np.ascontiguousarray(v)
        feed[f"in_{name}"] = v
        aps[name] = nc.dram_tensor(f"in_{name}", v.shape, mybir.dt.from_np(v.dtype), kind="ExternalInput").ap()
    out = nc.dram_tensor("out_0", _OUTS[0][0], F32, kind="ExternalOutput").ap()
    build(nc, out=out, **aps)
    r = _run(nc, [feed], core_ids=[0])
    return r.results[0]["out_0"]
```

```python
from contextlib import ExitStack

import numpy as np

import concourse.bass as bass
from concourse import mybir

ALU = mybir.AluOpType
ACT = mybir.ActivationFunctionType
AX = mybir.AxisListType
F32 = mybir.dt.float32
F32R = mybir.dt.float32r

BATCH, TOK, DIM, CTX = 8, 256, 160, 96
HEADS, DH = 20, 64
INNER = HEADS * DH
DFF = 640
HEADS2, DH2, NCA = 8, 20, 4
P = 128
REM = DIM - P
STACK = 3 * REM
TT = TOK // P
PAIRS = HEADS // 2
CHUNKS = INNER // 256
FT = DFF // P
PADH = 32
QUADS = HEADS2 // 4
PADW = HEADS2 * PADH
KEYS2 = TOK - NCA
EPS = 1e-5
GELU_C = 0.7978845608028654
GELU_A = 0.044715

SELF = [("self", h) for h in range(HEADS)]
CROSS = [("cross", h) for h in range(HEADS)]
CA = [("ca", h) for h in range(HEADS2)]
ENC = [("enc", h) for h in range(HEADS2)]
RING = 4
RINGT = 8
LN1_AT = 2
LAG_T = 3
LAG_V = LAG_T + 1
LAG_O = LAG_T + 2

CHAIN = ["cq2", "s2", "p2T", "c2T", "c2w"]


class Plan:

    def __init__(self, first=False, last=False, end=False):
        self.first, self.end = first, end
        self.early = ([] if end else SELF) + ([] if first else CA)
        self.late = ([] if end else CROSS) + ([] if first else ENC)
        self.units = self.early + self.late
        self.pa = ["qk2", "qk3", "qk4", "qk5", "qk6", "qk7", "qk8", "qk9", "k2_0", "k2_1", "q2_0", "q2_1", "q2_2",
                   "q2_3", "q2_4", "keyT", "cq1T", "next_qk0"]
        chain = [] if first else CHAIN
        self.pb = (["v0", "v1", "v2", "ctx", "v3", "v4", "v2_0", "v2_1", "v2_2", "v2_3", "v2_4"] + chain[0:2]
                   + ["k2_2"] + chain[2:3] + ["k2_3"] + chain[3:4] + ["k2_4"] + chain[4:5] + ["next_ln0", "blocks", "q2T"])
        if last:
            self.pa.remove("next_qk0")
            self.pb.remove("next_ln0")
        if end:
            self.pa, self.pb = [], chain
        self.qk = self.pa[0:12] + ["q2_2", "k2_2", "q2_3", "k2_3", "q2_4", "k2_4"] + ["next_qk0", "next_qk1"] * (not last)
        self.groups, self.group = [], []
        for i, (kind, h) in enumerate(self.units):
            size = 2 if kind in ("self", "cross") else 4
            if h % size == 0:
                self.groups.append((kind, list(range(i, i + size))))
            self.group.append(len(self.groups) - 1)

    def ends_group(self, i):
        g = self.group[i]
        return g if self.groups[g][1][-1] == i else None

    def per(self):
        n, g = len(self.units), len(self.groups)
        old, l1 = int(not self.end), int(not self.first)
        return dict(scores_ready=n, exp_done=n, max_ready=n, recip_ready=n, norm_ready=n, tr_ready=n, pT_ready=n,
                    pv_ready=g, o_ready=g, wo_done=2 * PAIRS * old, y_ready=old + l1, y_taken=3 * old + l1,
                    pa_ready=len(self.pa), pa_taken=len(self.pa), pb_ready=len(self.pb), pb_taken=len(self.pb),
                    qk_hi_ready=len(self.qk) * old, v2p_ready=old, v2p_taken=old, po_ready=old, po_taken=old, xT_ready=2 * old, xaff_ready=7 * old, hi_ready=7 * old, lo_ready=7 * old, xn_ready=6 * old, ln_step=6 * old,
                    stats_ready=3 * old, rstd_ready=3 * old, res_ready=3 * old, out_res_ready=l1,
                    ff_g_ready=FT * old, ff_a_ready=FT * old, ff_g_taken=FT * old, ff_a_taken=FT * old,
                    ff_cube=FT * old, ff_u=FT * old, ff_tanh=FT * old, ff_h=FT * old, x3_ready=old, x3_taken=old,
                    chain_step=3 * l1, s2_exp=l1, s2_norm=l1)


STEADY, FIRST, LAST, END = Plan(), Plan(first=True), Plan(last=True), Plan(end=True)
BEFORE = dict(pa_ready=1, pa_taken=1, qk_hi_ready=2, po_ready=1, po_taken=1, pb_ready=1, pb_taken=1, xaff_ready=2, hi_ready=2, lo_ready=2, xn_ready=2,
              ln_step=2, stats_ready=1, rstd_ready=1)
PER, PER_FIRST = STEADY.per(), FIRST.per()


def unit_queries(kind):
    return CTX if kind == "ca" else TOK


def unit_keys(kind):
    return KEYS2 if kind == "enc" else TOK


def build(nc, x, ctx, w_main, w_rem, w_ctx, w_o, w_f2, wq_p, wk_p, wv_p, wqca_p, wkca_p, wvca_p,
          wout_p, cols, rows, expand, mask_k, mask_v, out):
    es = ExitStack()
    with es:
        def sb(name, shape, dt=F32):
            return es.enter_context(nc.sbuf_tensor(name, shape, dt))

        sems = {}

        def sem(name):
            sems[name] = es.enter_context(nc.semaphore(name))
            return sems[name]

        NW = 5
        W_Q1, W_K1, W_V1, W_Q2, W_F1 = range(NW)
        w_hi = sb("w_hi", [P, NW, INNER], F32R)
        w_lo = sb("w_lo", [P, NW, INNER], F32R)
        w_st = sb("w_st", [STACK, NW, INNER], F32R)
        wc_hi = sb("wc_hi", [CTX, 2, INNER], F32R)
        wc_lo = sb("wc_lo", [CTX, 2, INNER], F32R)
        wo = sb("wo", [P, 2 * PAIRS, DIM])
        wf2 = sb("wf2", [P, FT, DIM])
        wq2p = sb("wq2p", [P, QUADS, PADW])
        BELOW = slice(CTX, CTX + HEADS2 * NCA)
        BELOW4 = slice(CTX, CTX + NCA)
        wk2p_t, wv2p_t, wkca_t, wvca_t = (sb(n, [P, PADW]) for n in ("wk2p_t", "wv2p_t", "wkca_t", "wvca_t"))
        wk2p, wqca = wk2p_t[0:CTX], wk2p_t[BELOW4]
        wv2p, mv = wv2p_t[0:CTX], wv2p_t[BELOW]
        wkca, v2bd = wkca_t[0:CTX], wkca_t[BELOW]
        wvca, p2T = wvca_t[0:CTX], wvca_t[BELOW, 0:CTX]
        woutp = sb("woutp", [P, QUADS, DIM])
        col = sb("col", [P, 12 + 2 * FT])
        row = sb("row", [P, 4, DIM])
        ex_t = sb("ex_t", [P, TOK])
        ex, ca_in = ex_t[0:CTX], ex_t[BELOW4, 0:CTX]
        mk = sb("mk", [P, 4, NCA])
        ident = sb("ident", [P, P])
        half_c = sb("half_c", [P, TT])

        x_in = sb("x_in", [P, TT, DIM])
        ctx_in = sb("ctx_in", [P, TT, CTX])
        x_cur = sb("x_cur", [P, TT, DIM])
        x_res = sb("x_res", [P, TT, DIM])
        stats = sb("stats", [P, TT, 6])
        mv_ln = sb("mv_ln", [P, 2, TT, 2])
        wait_pad = sb("wait_pad", [P, 1])
        var_e = sb("var_e", [P, 2, TT])
        rstd = sb("rstd", [P, 2, TT])
        xn = sb("xn", [P, TT, P + STACK])
        xaff = sb("xaff", [P, 2, TOK])
        x_hi = sb("x_hi", [P, TOK], F32R)
        x_lo = sb("x_lo", [P, TOK], F32R)
        x_st = sb("x_st", [STACK, TOK], F32R)
        cT = sb("cT", [CTX, TOK])
        ca_rep = sb("ca_rep", [CTX, HEADS2, NCA])
        cT_hi = sb("cT_hi", [CTX, TOK], F32R)
        cT_lo = sb("cT_lo", [CTX, TOK], F32R)
        QRING = 4
        qk_hi = sb("qk_hi", [P, QRING, 2, TOK], F32R)
        qk_lo = sb("qk_lo", [P, QRING, 2, TOK], F32R)
        val_buf = sb("val_buf", [P, TT * INNER])
        val = val_buf[:].rearrange("p (t n) -> p t n", t=TT)
        prob = sb("prob", [P, RING, 2 * TOK])
        pT = sb("pT", [P, RINGT, TT, TOK])
        nmax = sb("nmax", [P, RINGT, TT])
        rsum = sb("rsum", [P, RINGT, TT])
        rinv = sb("rinv", [P, RINGT, TT])
        oT = sb("oT", [P, 2, TOK])
        f_g, f_w = (val_buf[:, n * DFF * TT:(n + 1) * DFF * TT].rearrange("p (j t) -> p j t", j=FT) for n in range(2))
        second_buf = sb("second_buf", [P, 2 * INNER])
        second_at = [0]

        def second(parts, groups, width):
            at = second_at[0]
            second_at[0] += groups * width
            return second_buf[0:parts, at:at + groups * width].rearrange("p (g t) -> p g t", g=groups)

        x3T, q2T, hsT = (second(P, QUADS, TOK) for _ in range(3))
        hs1T, cq2T, c2T = (second(P, QUADS, CTX) for _ in range(3))
        c2w = second(CTX, 1, DIM)[:, 0, :]
        x3p = sb("x3p", [P, TT, PADW])
        k2T = sb("k2T", [P, QUADS, TOK])
        v2p = sb("v2p", [P, TT, PADW])
        cq1T = sb("cq1T", [P, QUADS, CTX])
        k2bd = sb("k2bd", [P, QUADS, 4, NCA])
        s2 = sb("s2", [CTX, HEADS2, NCA])
        s2m = sb("s2m", [CTX, HEADS2])
        s2s = sb("s2s", [CTX, HEADS2])
        s2r = sb("s2r", [CTX, HEADS2])
        o_sb = sb("o_sb", [P, TT, DIM])
        pT_flat = pT[:].rearrange("p r t k -> p (r t k)")
        prob_flat = prob[:].rearrange("p r k -> p (r k)")
        stage = {W_Q1: (val_buf[:, 0:INNER], val_buf[0:STACK, INNER:2 * INNER]),
                 W_K1: (prob_flat[:, 0:INNER], pT_flat[0:STACK, 2 * INNER:3 * INNER]),
                 W_V1: (pT_flat[:, 0:INNER], pT_flat[0:STACK, INNER:2 * INNER])}
        stage[W_Q2] = stage[W_F1] = (second_buf[:, 0:INNER], second_buf[0:STACK, INNER:])
        stage_ctx = second_buf[0:CTX, :]

        def bank(name):
            return es.enter_context(nc.psum_tensor(name, [P, 512], F32))

        s_bank = [bank("s_bank0"), bank("s_bank1")]
        t_bank = [bank("t_bank0"), bank("t_bank1")]
        o_bank, y_bank, pa, pb = bank("o_bank"), bank("y_bank"), bank("pa"), bank("pb")
        ff_g_bank = [t_bank[0], t_bank[1], o_bank]
        ff_a_bank = [s_bank[0], s_bank[1], pa]

        for name in PER:
            sem(name)
        w_loaded = [es.enter_context(nc.semaphore(f"w_loaded{i}")) for i in range(NW + 1)]
        cols_loaded, rows_loaded = sem("cols_loaded"), sem("rows_loaded")
        wo_loaded, small_loaded = sem("wo_loaded"), sem("small_loaded")
        w_hi_ready, w_st_ready, w_lo_ready = sem("w_hi_ready"), sem("w_st_ready"), sem("w_lo_ready")
        x_loaded, ctx_loaded, ca_loaded = sem("x_loaded"), sem("ctx_loaded"), sem("ca_loaded")
        out_stored = sem("out_stored")
        ident_ready, l1_scaled = sem("ident_ready"), sem("l1_scaled")

        NSMALL = 11
        W_CTX = NW
        MAIN = {W_Q1: 1, W_K1: 2, W_V1: 3, W_CTX: 4, W_Q2: 5, W_F1: 6}
        REST = {W_Q1: 1, W_K1: 2, W_V1: 3, W_Q2: 4, W_F1: 5}
        DONE = {W_Q1: 2, W_K1: 4, W_V1: 6, W_CTX: 7, W_Q2: 9, W_F1: 11}

        def qk_bank(name):
            return "pb" if name in ("k2_2", "k2_3", "k2_4") else "po" if name == "next_qk1" else "pa"

        def qk_place(tile, name):
            bank_ = {"pa": pa, "pb": pb, "po": o_bank}[qk_bank(name)]
            if name.startswith("qk") or name.startswith("next"):
                return tile[:, int(name[-1]) % QRING, :, :].rearrange("p s t -> p (s t)"), bank_[:, :]
            j = 2 * int(name[-1]) % QRING
            return tile[:, j:j + 2, int(name[0] == "k"), :], bank_[:, :].rearrange("p (j t) -> p j t", j=2)

        def qk_number(b, name):
            return plan_of(b).qk.index(name) + 1

        def pair_at(s):
            return (s + 3) // 2 if s % 2 == 1 and (s + 3) // 2 < PAIRS else None

        def plan_of(b):
            return {0: FIRST, BATCH - 1: LAST, BATCH: END}[b] if isinstance(b, int) else STEADY

        def count(name, b, n):
            before = BEFORE.get(name, 0)
            if isinstance(b, int) and b == 0:
                return before + n
            if isinstance(b, int) and b == BATCH:
                before = 0
            return b * PER[name] + before + PER_FIRST[name] - PER[name] + n

        def wait_n(eng, name, b, n):
            if not isinstance(b, int) or count(name, b, n) > 0:
                eng.wait_ge(sems[name], count(name, b, n))

        def batches(eng, one):
            one(0, False)
            with eng.Fori(1, BATCH - 1) as b:
                one(b, False)
            one(BATCH - 1, True)

        def filled(b, bank_name, name):
            return 1 if bank_name == "po" else order_of(b, bank_name).index(name) + 1

        def order_of(b, bank_name):
            return plan_of(b).pa if bank_name == "pa" else plan_of(b).pb

        block = es.enter_context(nc.Block())

        @block.sync
        def _(sp):
            def load_x(b):
                sp.dma_start(x_in[:], x[b].rearrange("(t p) e -> p t e", p=P)).then_inc(x_loaded, 16)

            def load_ctx(b):
                sp.dma_start(ctx_in[:], ctx[b].rearrange("(t p) e -> p t e", p=P)).then_inc(ctx_loaded, 16)

            def load_ca(b):
                sp.dma_start(ca_in, ctx[b, KEYS2:TOK, :]).then_inc(ca_loaded, 16)

            def store(b):
                sp.dma_start(out[b].rearrange("(t p) e -> p t e", p=P), o_sb[:]).then_inc(out_stored, 16)

            sp.sem_inc(out_stored, 16)
            load_x(0)
            with nc.allow_non_contiguous_dma(reason="vectors and padded heads"):
                sp.dma_start(col[:], cols).then_inc(cols_loaded, 16)
                sp.dma_start(row[:], rows.to_broadcast([P, 4, DIM])).then_inc(rows_loaded, 16)
                load_ctx(0)
                load_ca(0)
                for dst, src in ((wf2[:], w_f2.rearrange("(j p) e -> p j e", p=P)),
                                 (wq2p[:], wq_p), (wk2p, wk_p), (wv2p, wv_p), (wqca, wqca_p),
                                 (wkca, wkca_p), (wvca, wvca_p), (woutp[:], wout_p), (ex, expand),
                                 (mk[:], mask_k), (mv, mask_v)):
                    sp.dma_start(dst, src).then_inc(small_loaded, 16)

            def one(b, last):
                if not last:
                    sp.wait_ge(sems["xn_ready"], count("xn_ready", b, 0))
                    sp.wait_ge(sems["res_ready"], count("res_ready", b, 1))
                    load_x(b + 1)
                    sp.wait_ge(sems["pb_ready"], count("pb_ready", b, filled(b, "pb", "ctx")))
                    load_ctx(b + 1)
                    sp.wait_ge(sems["pa_ready"], count("pa_ready", b, filled(b, "pa", "cq1T")))
                    load_ca(b + 1)
                if plan_of(b) is not FIRST:
                    sp.wait_ge(sems["y_taken"], count("y_taken", b, 4))
                    store(b - 1)
            batches(sp, one)
            sp.wait_ge(sems["y_taken"], count("y_taken", BATCH, 1))
            store(BATCH - 1)
            sp.wait_ge(out_stored, 16 * BATCH + 16)

        @block.gpsimd
        def _(pool):
            pool.memset(ident[:], 0.0).then_inc(ident_ready, 1)
            pool.memset(half_c[:], -0.5).then_inc(ident_ready, 1)
            pool.memset(x3p[:], 0.0).then_inc(ident_ready, 1)
            pool.wait_ge(ident_ready, 3)
            pool.affine_select(out=ident[:], in_=ident[:], compare_op=ALU.not_equal, fill=1.0, base=0,
                               pattern=[[-1, P]], channel_multiplier=1).then_inc(ident_ready, 1)

            def normalise(b, i):
                kind, _ = plan_of(b).units[i]
                q, k = unit_queries(kind), unit_keys(kind)
                pool.wait_ge(sems["recip_ready"], count("recip_ready", b, i + 1))
                if kind == "ca":
                    p = prob[0:q, i % RING, 0:k]
                    r = rinv[0:q, i % RINGT, 0:1].to_broadcast([q, k])
                else:
                    p = prob[:, i % RING, 0:2 * k].rearrange("p (t k) -> p t k", t=2)
                    r = rinv[:, i % RINGT, :].rearrange("p (t o) -> p t o", o=1).to_broadcast([P, 2, k])
                pool.tensor_tensor(p, p, r, ALU.mult).then_inc(sems["norm_ready"], 1)

            def rstd_of(b, n, slot):
                pool.wait_ge(sems["stats_ready"], count("stats_ready", b, n))
                pool.tensor_tensor(rstd[:, slot, :], var_e[:, slot, :], half_c[:], ALU.pow).then_inc(sems["rstd_ready"], 1)

            def residual(b, k):
                wait_n(pool, "y_taken", b, k)
                src = x_in if k == 0 else x_cur
                if k == 0:
                    pool.wait_ge(x_loaded, 16 * b + 16)
                pool.tensor_tensor(x_res[:], src[:], row[:, k, :].rearrange("p (o e) -> p o e", o=1).to_broadcast([P, TT, DIM]),
                                   ALU.add).then_inc(sems["res_ready"], 1)

            def out_residual(b):
                pool.wait_ge(out_stored, 16 * b)
                pool.wait_ge(sems["y_taken"], count("y_taken", b, 0))
                for t in range(TT):
                    ins = pool.tensor_tensor(
                        o_sb[:, t, :].rearrange("p (h d) -> p h d", d=DH2),
                        x3p[:, t, :].rearrange("p (h d) -> p h d", d=PADH)[:, :, 0:DH2],
                        row[:, 3, :].rearrange("p (h d) -> p h d", d=DH2), ALU.add)
                ins.then_inc(sems["out_res_ready"], 1)

            def one(b, last):
                plan = plan_of(b)
                for i, (kind, h) in enumerate(plan.units):
                    if (kind, h) == CROSS[0]:
                        residual(b, 1)
                    normalise(b, i)
                    if i == min(HEADS + LAG_O, len(plan.early) - 1):
                        rstd_of(b, 1, 1)
                    if i == len(plan.early) + min(HEADS + LAG_O, len(plan.late) - 1):
                        rstd_of(b, 2 if last else 3, 1)
                    if (kind, h) == ("self", 4):
                        residual(b, 0)
                    if (kind, h) == ("self", 8) and plan is not FIRST:
                        out_residual(b)
                    if (kind, h) == ("cross", 10) and not last:
                        rstd_of(b, 2, 0)
                residual(b, 2)
                for j in range(FT):
                    pool.wait_ge(sems["ff_g_taken"], count("ff_g_taken", b, j + 1))
                    pool.tensor_tensor(f_w[:, j, :], f_w[:, j, :], f_g[:, j, :], ALU.mult).then_inc(sems["ff_cube"], 1)
            rstd_of(0, 0, 0)
            for i in (W_Q1, W_K1, W_V1):
                pool.wait_ge(w_loaded[i], 32)
                pool.tensor_scalar(w_st[:, i, :], stage[i][1], DH ** -0.5 if i == W_Q1 else 1.0, None, ALU.mult)\
                    .then_inc(w_st_ready, 1)
            pool.wait_ge(rows_loaded, 16)
            batches(pool, one)
            out_residual(BATCH)
            for i in range(len(END.units)):
                normalise(BATCH, i)

        @block.scalar
        def _(act):
            def load_w(i):
                act.dma_start(stage[i][0], w_main[i]).then_inc(w_loaded[i], 16)
                act.dma_start(stage[i][1], w_rem[i]).then_inc(w_loaded[i], 16)

            for i in (W_Q1, W_K1, W_V1):
                load_w(i)
            act.dma_start(stage_ctx.rearrange("p (a n) -> p a n", a=2), w_ctx.rearrange("a p n -> p a n"))\
               .then_inc(w_loaded[W_CTX], 16)
            act.dma_start(wo[:], w_o.rearrange("a (j p) e -> p (a j) e", p=P)).then_inc(wo_loaded, 16)

            def split_high(i):
                if i == W_CTX:
                    act.wait_ge(w_loaded[i], 16)
                    act.activation(wc_hi[:].rearrange("p a n -> p (a n)"), stage_ctx, ACT.Copy).then_inc(w_hi_ready, 1)
                    return
                act.wait_ge(w_loaded[i], 32)
                sc = DH ** -0.5 if i in (W_Q1, W_Q2) else 1.0
                act.activation(w_hi[:, i, :], stage[i][0], ACT.Copy, scale=sc).then_inc(w_hi_ready, 1)
                if i in (W_Q2, W_F1):
                    act.activation(w_st[:, i, :], stage[i][1], ACT.Copy, scale=sc).then_inc(w_st_ready, 1)

            def exps(b, i):
                kind, _ = plan_of(b).units[i]
                q, k = unit_queries(kind), unit_keys(kind)
                act.wait_ge(sems["max_ready"], count("max_ready", b, i + 1))
                wait_n(act, "tr_ready", b, i + 1 - RING)
                tiles = 1 if kind == "ca" else 2
                for t in range(tiles):
                    last = act.activation(prob[0:min(q, P), i % RING, t * k:t * k + k],
                                          s_bank[i % 2][0:min(q, P), t * TOK:t * TOK + k], ACT.Exp,
                                          bias=nmax[0:min(q, P), i % RINGT, t:t + 1],
                                          accum_out=rsum[0:min(q, P), i % RINGT, t:t + 1])
                last.then_inc(sems["exp_done"], 1)

            def take_pT(b, i):
                plan = plan_of(b)
                kind, _ = plan.units[i]
                q, k = unit_queries(kind), unit_keys(kind)
                act.wait_ge(sems["tr_ready"], count("tr_ready", b, i + 1))
                wait_n(act, "pv_ready", b, plan.group[i - RINGT] + 1 if i >= RINGT else 0)
                src = t_bank[i % 2][:, 0:2 * q].rearrange("p (t q) -> p t q", t=2)
                if k == TOK:
                    act.activation(pT[:, i % RINGT, :, 0:q], src, ACT.Copy).then_inc(sems["pT_ready"], 1)
                else:
                    act.activation(pT[:, i % RINGT, 0, 0:q], src[:, 0, :], ACT.Copy)
                    act.activation(pT[0:k - P, i % RINGT, 1, 0:q], src[0:k - P, 1, :], ACT.Copy)\
                       .then_inc(sems["pT_ready"], 1)

            def high_halves(b, n):
                act.wait_ge(sems["xaff_ready"], count("xaff_ready", b, n))
                act.activation(x_hi[:], xaff[:, 0, :], ACT.Copy).then_inc(sems["hi_ready"], 1)
                act.wait_ge(sems["xaff_ready"], count("xaff_ready", b, n + 1))
                act.activation(x_st[:], xaff[0:STACK, 1, :], ACT.Copy).then_inc(sems["hi_ready"], 1)

            def stream(b, first, n, between):
                for s in range(n + LAG_T):
                    if s < n:
                        exps(b, first + s)
                    if s >= LAG_T:
                        take_pT(b, first + s - LAG_T)
                    between(s)

            flat = pa[:, :]
            flat_b = pb[:, :]

            def take_pa(b, name, dst, src):
                act.wait_ge(sems["pa_ready"], count("pa_ready", b, filled(b, "pa", name)))
                act.activation(dst, src, ACT.Copy).then_inc(sems["pa_taken"], 1)

            def take_pb(b, name, dst, src):
                act.wait_ge(sems["pb_ready"], count("pb_ready", b, filled(b, "pb", name)))
                act.activation(dst, src, ACT.Copy).then_inc(sems["pb_taken"], 1)

            def take_high(b, name):
                dst, src = qk_place(qk_hi, name)
                ready = qk_bank(name) + "_ready"
                act.wait_ge(sems[ready], count(ready, b, filled(b, qk_bank(name), name)))
                act.activation(dst, src, ACT.Copy).then_inc(sems["qk_hi_ready"], 1)

            def take_v2(b, c):
                take_pb(b, f"v2_{c}", val[:, :, 256 * c:256 * c + 256], flat_b.rearrange("p (j t) -> p j t", j=2))

            def chain(b, s):
                if s == 1:
                    take_pb(b, "cq2", cq2T.rearrange("p g t -> p (g t)"), flat_b[:, 0:QUADS * CTX])
                if s == 4:
                    act.wait_ge(sems["pb_taken"], count("pb_taken", b, filled(b, "pb", "s2")))
                    act.activation(s2[:], s2[:], ACT.Exp).then_inc(sems["s2_exp"], 1)
                if s == 7:
                    take_pb(b, "p2T", p2T, pb[BELOW, 0:CTX])
                if s == 11:
                    take_pb(b, "c2T", c2T.rearrange("p g t -> p (g t)"), flat_b[:, 0:QUADS * CTX])
                if s == 15:
                    take_pb(b, "c2w", c2w, pb[0:CTX, 0:DIM])

            def one(b, last):
                plan = plan_of(b)

                def fill_end(s):
                    if s == HEADS + 1:
                        take_high(b, "k2_0")
                    if s == HEADS + 3:
                        take_v2(b, 0)
                    if s == HEADS + 4:
                        take_v2(b, 1)
                    if s == HEADS + 5:
                        take_high(b, "k2_1")
                    if s == HEADS + 8:
                        take_v2(b, 2)

                def early_between(s):
                    if pair_at(s) is not None:
                        take_high(b, f"qk{pair_at(s)}")
                    fill_end(s)
                    if plan is not FIRST and s == len(plan.early) + LN1_AT:
                        high_halves(b, 2)
                    if s == 12:
                        act.wait_ge(sems["xaff_ready"], count("xaff_ready", b, 1))
                        act.activation(cT_hi[:], cT[:], ACT.Copy).then_inc(sems["hi_ready"], 1)
                    if plan is FIRST:
                        if s == 3:
                            split_high(W_CTX)
                        if s == 5:
                            act.wait_ge(w_lo_ready, DONE[W_CTX])
                            load_w(W_Q2)
                        if s == 9:
                            split_high(W_Q2)
                        if s == 11:
                            act.wait_ge(w_lo_ready, DONE[W_Q2])
                            load_w(W_F1)
                        if s == 15:
                            split_high(W_F1)
                        if s == 17:
                            act.wait_ge(small_loaded, 16 * NSMALL)
                            act.activation(wq2p[:], wq2p[:], ACT.Copy, scale=DH2 ** -0.5).then_inc(l1_scaled, 1)
                            act.activation(wqca, wqca, ACT.Copy, scale=DH2 ** -0.5).then_inc(l1_scaled, 1)

                def late_between(s):
                    c = s // 4
                    if s % 4 == 0 and c + 1 < CHUNKS:
                        take_high(b, f"q2_{c + 1}")
                    if s % 4 == 1 and 2 <= c + 1 < CHUNKS:
                        take_high(b, f"k2_{c + 1}")
                    if plan is not FIRST and s == len(plan.late) + 1:
                        high_halves(b, 4)
                    if plan is not FIRST:
                        chain(b, s)
                stream(b, 0, len(plan.early), early_between)
                for s in range(len(plan.early) + LAG_T, HEADS + 10):
                    fill_end(s)
                if plan is FIRST:
                    high_halves(b, 2)
                take_v2(b, 3)
                take_high(b, "q2_0")
                take_v2(b, 4)
                stream(b, len(plan.early), len(plan.late), late_between)
                if plan is FIRST:
                    high_halves(b, 4)
                for j in range(FT + 2):
                    if j < FT:
                        act.wait_ge(sems["ff_g_ready"], count("ff_g_ready", b, j + 1))
                        bias = col[:, 12 + FT + j:13 + FT + j]
                        act.activation(f_w[:, j, :], ff_g_bank[j % 3][:, 0:TOK], ACT.Square, bias=bias)
                        act.activation(f_g[:, j, :], ff_g_bank[j % 3][:, 0:TOK], ACT.Identity, bias=bias)\
                           .then_inc(sems["ff_g_taken"], 1)
                    if j == FT:
                        take_pa(b, "keyT", k2T[:].rearrange("p g t -> p (g t)"), flat)
                    if j == FT + 1:
                        act.wait_ge(sems["v2p_ready"], count("v2p_ready", b, 1))
                        act.activation(v2p[:].rearrange("p t n -> p (t n)"), o_bank[:, :], ACT.Copy)\
                           .then_inc(sems["v2p_taken"], 1)
                    if j >= 2:
                        i = j - 2
                        act.wait_ge(sems["ff_u"], count("ff_u", b, i + 1))
                        act.activation(f_w[:, i, :], f_w[:, i, :], ACT.Tanh, scale=GELU_C).then_inc(sems["ff_tanh"], 1)
                if not last:
                    high_halves(b, 6)
                take_pa(b, "cq1T", cq1T[:].rearrange("p g t -> p (g t)"), flat[:, 0:QUADS * CTX])
                if not last:
                    take_high(b, "next_qk0")
                    take_high(b, "next_qk1")
                take_pb(b, "q2T", q2T.rearrange("p g t -> p (g t)"), flat_b)

            for i in (W_Q1, W_K1, W_V1):
                split_high(i)
                if i == W_Q1:
                    high_halves(0, -1)
            act.wait_ge(sems["pa_ready"], 1)
            dst, src = qk_place(qk_hi, "next_qk0")
            act.activation(dst, src, ACT.Copy).then_inc(sems["qk_hi_ready"], 1)
            act.wait_ge(sems["po_ready"], 1)
            dst, src = qk_place(qk_hi, "next_qk1")
            act.activation(dst, src, ACT.Copy).then_inc(sems["qk_hi_ready"], 1)
            batches(act, one)
            stream(BATCH, 0, len(CA), lambda s: None)
            chain(BATCH, 1)
            stream(BATCH, len(CA), len(ENC), lambda s: chain(BATCH, {1: 4, 3: 7, 5: 11, 7: 15}.get(s, 0)))

        @block.vector
        def _(dve):
            def split_low(i):
                dve.wait_ge(w_hi_ready, MAIN[i])
                if i == W_CTX:
                    dve.tensor_tensor(wc_lo[:].rearrange("p a n -> p (a n)"), stage_ctx,
                                      wc_hi[:].rearrange("p a n -> p (a n)").bitcast(F32), ALU.subtract).then_inc(w_lo_ready, 1)
                    return
                sc = DH ** -0.5 if i in (W_Q1, W_Q2) else 1.0
                dve.scalar_tensor_tensor(out=w_lo[:, i, :], in0=stage[i][0], scalar=sc,
                                         in1=w_hi[:, i, :].bitcast(F32), op0=ALU.mult, op1=ALU.subtract)\
                   .then_inc(w_lo_ready, 1)
                lo = slice(REM, 2 * REM)
                dve.wait_ge(w_st_ready, REST[i])
                dve.scalar_tensor_tensor(out=w_st[lo, i, :], in0=stage[i][1][lo], scalar=sc,
                                         in1=w_st[lo, i, :].bitcast(F32), op0=ALU.mult, op1=ALU.subtract)\
                   .then_inc(w_lo_ready, 1)

            def own(name, b, n, ins):
                ins.then_inc(sems[name], 1)
                dve.wait_ge(sems[name], count(name, b, n))

            def maxima(b, i):
                kind, _ = plan_of(b).units[i]
                q, k = unit_queries(kind), unit_keys(kind)
                dve.wait_ge(sems["scores_ready"], count("scores_ready", b, i + 1))
                if kind == "ca":
                    dve.tensor_reduce(nmax[0:q, i % RINGT, 0:1], s_bank[i % 2][0:q, 0:k], AX.X, ALU.max,
                                      negate=True).then_inc(sems["max_ready"], 1)
                else:
                    dve.tensor_reduce(nmax[:, i % RINGT, :],
                                      s_bank[i % 2][:, :].rearrange("p (t k) -> p t k", t=2)[:, :, 0:k],
                                      AX.X, ALU.max, negate=True).then_inc(sems["max_ready"], 1)

            def inverse(b, i):
                kind, _ = plan_of(b).units[i]
                q, t = min(unit_queries(kind), P), 1 if kind == "ca" else TT
                dve.wait_ge(sems["exp_done"], count("exp_done", b, i + 1))
                dve.reciprocal(rinv[0:q, i % RINGT, 0:t], rsum[0:q, i % RINGT, 0:t]).then_inc(sems["recip_ready"], 1)

            def take_o(b, g):
                kind, members = plan_of(b).groups[g]
                h = plan_of(b).units[members[0]][1]
                dve.wait_ge(sems["pv_ready"], count("pv_ready", b, g + 1))
                if kind in ("self", "cross"):
                    pair = h // 2 + (PAIRS if kind == "cross" else 0)
                    wait_n(dve, "wo_done", b, pair - 1)
                    dve.tensor_copy(oT[:, pair % 2, :], o_bank[:, 0:TOK]).then_inc(sems["o_ready"], 1)
                elif kind == "ca":
                    dve.tensor_copy(hs1T[:, h // 4, :], o_bank[:, 0:CTX]).then_inc(sems["o_ready"], 1)
                else:
                    dve.tensor_copy(hsT[:, h // 4, :], o_bank[:, 0:TOK]).then_inc(sems["o_ready"], 1)

            def ln_sums(b, n, slot, src):
                for t in range(TT):
                    last = dve.bn_stats(stats[:, t, :], src[:, t, :])
                own("ln_step", b, 2 * n - 1, last)

            def ln_variance(b, n, slot):
                dve.memset(wait_pad[:], 0.0)
                for t in range(TT):
                    last = dve.bn_aggr(mv_ln[:, slot, t, :], stats[:, t, :])
                own("ln_step", b, 2 * n, last)
                dve.tensor_scalar(var_e[:, slot, :], mv_ln[:, slot, :, 1], EPS, None, ALU.add).then_inc(sems["stats_ready"], 1)

            def ln_rows(b, n, slot, src):
                dve.wait_ge(sems["rstd_ready"], count("rstd_ready", b, n))
                for t in range(TT):
                    mean, r = mv_ln[:, slot, t, 0:1], rstd[:, slot, t:t + 1]
                    dve.tensor_scalar(xn[:, t, 0:P], src[:, t, 0:P], mean, r, ALU.subtract, ALU.mult)
                    dve.tensor_scalar(
                        xn[:, t, P:P + STACK].rearrange("p (c r) -> p c r", c=3),
                        src[:, t, P:DIM].rearrange("p (o r) -> p o r", o=1).to_broadcast([P, 3, REM]),
                        mean, r, ALU.subtract, ALU.mult).then_inc(sems["xn_ready"], 1)

            def affine_and_low(b, bank_, k, n):
                dve.tensor_scalar(xaff[:, 0, :], bank_[:, 0:TOK], col[:, 4 * k:4 * k + 1], col[:, 4 * k + 1:4 * k + 2],
                                  ALU.mult, ALU.add).then_inc(sems["xaff_ready"], 1)
                dve.tensor_scalar(xaff[0:STACK, 1, :], bank_[0:STACK, TOK:2 * TOK], col[0:STACK, 4 * k + 2:4 * k + 3],
                                  col[0:STACK, 4 * k + 3:4 * k + 4], ALU.mult, ALU.add).then_inc(sems["xaff_ready"], 1)
                dve.wait_ge(sems["hi_ready"], count("hi_ready", b, n))
                dve.tensor_tensor(x_lo[:], xaff[:, 0, :], x_hi[:].bitcast(F32), ALU.subtract).then_inc(sems["lo_ready"], 1)
                lo = slice(2 * REM, 3 * REM)
                dve.wait_ge(sems["hi_ready"], count("hi_ready", b, n + 1))
                dve.tensor_tensor(x_st[lo, :], xaff[lo, 1, :], x_st[lo, :].bitcast(F32), ALU.subtract)\
                   .then_inc(sems["lo_ready"], 1)
                if bank_ is pb:
                    dve.sem_inc(sems["pb_taken"], 1)

            def take_low(b, name):
                dve.wait_ge(sems["qk_hi_ready"], count("qk_hi_ready", b, qk_number(b, name)))
                dst, src = qk_place(qk_lo, name)
                dve.tensor_tensor(dst, src, qk_place(qk_hi, name)[0].bitcast(F32), ALU.subtract)\
                   .then_inc(sems[qk_bank(name) + "_taken"], 1)

            def stream(b, first, n, between):
                plan = plan_of(b)
                for s in range(n + LAG_V):
                    if s < n:
                        maxima(b, first + s)
                    if 1 <= s <= n:
                        inverse(b, first + s - 1)
                    between(s)
                    if s >= LAG_V and plan.ends_group(first + s - LAG_V) is not None:
                        take_o(b, plan.ends_group(first + s - LAG_V))

            def sum_y(b, n):
                dve.wait_ge(sems["wo_done"], count("wo_done", b, PAIRS * (n + 1)))
                dve.wait_ge(sems["res_ready"], count("res_ready", b, n + 1))
                dve.tensor_tensor(x_cur[:].rearrange("p t e -> p (t e)"), y_bank[:, 0:TT * DIM],
                                  x_res[:].rearrange("p t e -> p (t e)"), ALU.add).then_inc(sems["y_taken"], 1)
                dve.wait_ge(sems["y_taken"], count("y_taken", b, n + 1))

            def result(b, ready, taken):
                dve.wait_ge(sems["y_ready"], count("y_ready", b, ready))
                dve.wait_ge(sems["out_res_ready"], count("out_res_ready", b, 1))
                dve.tensor_tensor(o_sb[:].rearrange("p t e -> p (t e)"), y_bank[:, 0:TT * DIM],
                                  o_sb[:].rearrange("p t e -> p (t e)"), ALU.add).then_inc(sems["y_taken"], 1)

            def take_pb(b, name, dst, src):
                dve.wait_ge(sems["pb_ready"], count("pb_ready", b, filled(b, "pb", name)))
                dve.tensor_copy(dst, src).then_inc(sems["pb_taken"], 1)

            def context_rows(b):
                dve.wait_ge(sems["pb_ready"], count("pb_ready", b, filled(b, "pb", "ctx")))
                dve.tensor_copy(ca_rep[:], pb[0:CTX, KEYS2:TOK].rearrange("p (o c) -> p o c", o=1)
                                .to_broadcast([CTX, HEADS2, NCA]))
                dve.tensor_copy(cT[:], pb[0:CTX, 0:TOK]).then_inc(sems["xaff_ready"], 1)

            def context_low(b):
                dve.wait_ge(sems["hi_ready"], count("hi_ready", b, 1))
                dve.tensor_tensor(cT_lo[:], cT[:], cT_hi[:].bitcast(F32), ALU.subtract).then_inc(sems["lo_ready"], 1)
                dve.sem_inc(sems["pb_taken"], 1)

            def blocks(b):
                dve.wait_ge(sems["pb_ready"], count("pb_ready", b, filled(b, "pb", "blocks")))
                for g in range(QUADS):
                    dve.tensor_tensor(k2bd[:, g, :, :],
                                      pb[:, g * NCA:(g + 1) * NCA].rearrange("p (o c) -> p o c", o=1)
                                      .to_broadcast([P, 4, NCA]), mk[:], ALU.mult)
                dve.tensor_tensor(v2bd, pb[BELOW, 64:64 + PADW], mv, ALU.mult)\
                   .then_inc(sems["pb_taken"], 1)

            def chain(b, s):
                if s == 3:
                    dve.wait_ge(sems["pb_ready"], count("pb_ready", b, filled(b, "pb", "s2")))
                    s3 = pb[0:CTX, 0:HEADS2 * NCA].rearrange("p (h c) -> p h c", c=NCA)
                    own("chain_step", b, 1, dve.tensor_reduce(s2m[:], s3, AX.X, ALU.max))
                    dve.tensor_tensor(s2[:], s3, s2m[:].rearrange("p (h o) -> p h o", o=1).to_broadcast([CTX, HEADS2, NCA]),
                                      ALU.subtract).then_inc(sems["pb_taken"], 1)
                if s == 5:
                    dve.wait_ge(sems["s2_exp"], count("s2_exp", b, 1))
                    own("chain_step", b, 2, dve.tensor_reduce(s2s[:], s2[:], AX.X, ALU.add))
                    own("chain_step", b, 3, dve.reciprocal(s2r[:], s2s[:]))
                    dve.tensor_tensor(s2[:], s2[:], s2r[:].rearrange("p (h o) -> p h o", o=1).to_broadcast([CTX, HEADS2, NCA]),
                                      ALU.mult).then_inc(sems["s2_norm"], 1)

            def one(b, last):
                plan = plan_of(b)
                ln2 = 2 if last else 3

                def norm_steps(s, n, y):
                    if s == HEADS + LAG_O:
                        sum_y(b, y)
                        ln_sums(b, n, 1, x_cur)
                    if s == HEADS + LAG_O + 1:
                        ln_variance(b, n, 1)
                    if s == HEADS + LAG_O + 2:
                        ln_rows(b, n, 1, x_cur)

                def early_between(s):
                    if s % 4 == 2 and s // 4 < CHUNKS:
                        c = s // 4
                        take_pb(b, f"v{c}", val[:, :, 256 * c:256 * c + 256], pb[:, :].rearrange("p (t n) -> p t n", t=2))
                    if s > 0 and pair_at(s - 1) is not None:
                        take_low(b, f"qk{pair_at(s - 1)}")
                    if s == HEADS + 2:
                        take_low(b, "k2_0")
                    if s == HEADS + 6:
                        take_low(b, "k2_1")
                    if s == 12:
                        context_rows(b)
                    if s == 13:
                        context_low(b)
                    if plan is FIRST:
                        if s == 4:
                            split_low(W_CTX)
                        if s == 10:
                            split_low(W_Q2)
                        if s == 16:
                            split_low(W_F1)
                    norm_steps(s, 1, 0)
                    if plan is not FIRST and s == len(plan.early) + LN1_AT:
                        normalised_early()

                def normalised_early():
                    dve.wait_ge(sems["xT_ready"], count("xT_ready", b, 1))
                    affine_and_low(b, y_bank, 1, 2)

                def normalised_late():
                    dve.wait_ge(sems["xT_ready"], count("xT_ready", b, 2))
                    affine_and_low(b, y_bank, 2, 4)

                def late_between(s):
                    if not last and s == 9:
                        dve.wait_ge(x_loaded, 16 * (b + 1) + 16)
                        ln_sums(b, 2, 0, x_in)
                    if not last and s == 11:
                        ln_variance(b, 2, 0)
                    if s % 4 == 1 and s // 4 + 1 < CHUNKS:
                        take_low(b, f"q2_{s // 4 + 1}")
                    if s % 4 == 2 and 2 <= s // 4 + 1 < CHUNKS:
                        take_low(b, f"k2_{s // 4 + 1}")
                    if plan is not FIRST:
                        chain(b, s)
                    norm_steps(s, ln2, 1)
                    if plan is not FIRST and s == len(plan.late) + 1:
                        normalised_late()
                stream(b, 0, len(plan.early), early_between)
                if plan is FIRST:
                    take_low(b, "k2_1")
                for s in range(len(plan.early) + LAG_V, HEADS + LAG_O + 3):
                    norm_steps(s, 1, 0)
                if plan is FIRST:
                    normalised_early()
                    dve.wait_ge(small_loaded, 16 * NSMALL)
                take_low(b, "q2_0")
                stream(b, len(plan.early), len(plan.late), late_between)
                for s in range(len(plan.late) + LAG_V, HEADS + LAG_O + 3):
                    norm_steps(s, ln2, 1)
                if plan is FIRST:
                    normalised_late()

                for j in range(FT + 3):
                    if not last and j == 1:
                        ln_rows(b, 2, 0, x_in)
                    if 1 <= j <= FT:
                        i = j - 1
                        dve.wait_ge(sems["ff_cube"], count("ff_cube", b, i + 1))
                        dve.scalar_tensor_tensor(out=f_w[:, i, :], in0=f_w[:, i, :], scalar=GELU_A, in1=f_g[:, i, :],
                                                 op0=ALU.mult, op1=ALU.add).then_inc(sems["ff_u"], 1)
                        dve.wait_ge(sems["ff_a_ready"], count("ff_a_ready", b, i + 1))
                        dve.scalar_tensor_tensor(out=f_g[:, i, :], in0=ff_a_bank[i % 3][:, 0:TOK],
                                                 scalar=col[:, 12 + i:13 + i], in1=f_g[:, i, :],
                                                 op0=ALU.add, op1=ALU.mult).then_inc(sems["ff_a_taken"], 1)
                    if j >= 3:
                        i = j - 3
                        dve.wait_ge(sems["ff_tanh"], count("ff_tanh", b, i + 1))
                        dve.wait_ge(sems["ff_a_taken"], count("ff_a_taken", b, i + 1))
                        dve.scalar_tensor_tensor(out=f_g[:, i, :], in0=f_w[:, i, :], scalar=1.0, in1=f_g[:, i, :],
                                                 op0=ALU.add, op1=ALU.mult).then_inc(sems["ff_h"], 1)
                if not last:
                    dve.wait_ge(sems["pb_ready"], count("pb_ready", b, filled(b, "pb", "next_ln0")))
                    affine_and_low(b, pb, 0, 6)
                dve.wait_ge(sems["y_ready"], count("y_ready", b, 1))
                dve.wait_ge(sems["res_ready"], count("res_ready", b, 3))
                if plan is not FIRST:
                    dve.wait_ge(sems["out_res_ready"], count("out_res_ready", b, 1))
                for t in range(TT):
                    ins = dve.scalar_tensor_tensor(
                        out=x3p[:, t, :].rearrange("p (h d) -> p h d", d=PADH)[:, :, 0:DH2],
                        in0=y_bank[:, t * DIM:(t + 1) * DIM].rearrange("p (h d) -> p h d", d=DH2), scalar=0.5,
                        in1=x_res[:, t, :].rearrange("p (h d) -> p h d", d=DH2), op0=ALU.mult, op1=ALU.add)
                ins.then_inc(sems["y_taken"], 1)
                blocks(b)
                dve.wait_ge(sems["x3_ready"], count("x3_ready", b, 1))
                dve.tensor_copy(x3T.rearrange("p g t -> p (g t)"), t_bank[0][:, :]).then_inc(sems["x3_taken"], 1)
                if plan is not FIRST:
                    result(b, 2, 4)
                if not last:
                    take_low(b, "next_qk0")
                    take_low(b, "next_qk1")
            dve.wait_ge(x_loaded, 16)
            ln_sums(0, 0, 0, x_in)
            ln_variance(0, 0, 0)
            dve.wait_ge(ident_ready, 4)
            ln_rows(0, 0, 0, x_in)
            dve.wait_ge(cols_loaded, 16)
            dve.wait_ge(sems["pb_ready"], 1)
            affine_and_low(0, pb, 0, -1)
            split_low(W_Q1)
            split_low(W_K1)
            split_low(W_V1)
            dve.wait_ge(sems["qk_hi_ready"], 1)
            dst, src = qk_place(qk_lo, "next_qk0")
            dve.tensor_tensor(dst, src, qk_place(qk_hi, "next_qk0")[0].bitcast(F32), ALU.subtract)\
               .then_inc(sems["pa_taken"], 1)
            dve.wait_ge(sems["qk_hi_ready"], 2)
            dst, src = qk_place(qk_lo, "next_qk1")
            dve.tensor_tensor(dst, src, qk_place(qk_hi, "next_qk1")[0].bitcast(F32), ALU.subtract)\
               .then_inc(sems["po_taken"], 1)
            batches(dve, one)
            stream(BATCH, 0, len(CA), lambda s: None)
            stream(BATCH, len(CA), len(ENC), lambda s: chain(BATCH, {0: 3, 2: 5}.get(s, 0)))
            result(BATCH, 1, 1)

        @block.tensor
        def _(pe):
            pe.wait_ge(ident_ready, 4)

            def split_product(out_ap, w_i, wcols, x_is_weight, tok=slice(0, TOK)):
                pairs = [(w_hi[:, w_i, wcols], x_hi[:, tok]), (w_lo[:, w_i, wcols], x_hi[:, tok]),
                         (w_hi[:, w_i, wcols], x_lo[:, tok]), (w_st[:, w_i, wcols], x_st[:, tok])]
                for n, (w, a) in enumerate(pairs):
                    l, r = (a, w) if x_is_weight else (w, a)
                    last = pe.matmul(out_ap, l, r, start=(n == 0), stop=(n == 3))
                return last

            def split_ctx(out_ap, w_i, wcols, x_is_weight, tok=slice(0, TOK)):
                pairs = [(wc_hi[:, w_i, wcols], cT_hi[:, tok]), (wc_lo[:, w_i, wcols], cT_hi[:, tok]),
                         (wc_hi[:, w_i, wcols], cT_lo[:, tok])]
                for n, (w, a) in enumerate(pairs):
                    l, r = (a, w) if x_is_weight else (w, a)
                    last = pe.matmul(out_ap, l, r, start=(n == 0), stop=(n == 2))
                return last

            def use_pa(b, name):
                wait_n(pe, "pa_taken", b, filled(b, "pa", name) - 1)

            def use_pb(b, name):
                wait_n(pe, "pb_taken", b, filled(b, "pb", name) - 1)

            def ln_transposes(b, n, bank_, done):
                for t in range(TT):
                    pe.wait_ge(sems["xn_ready"], count("xn_ready", b, n + t))
                    pe.transpose(bank_[:, t * P:(t + 1) * P], xn[:, t, 0:P], ident[:])
                    last = pe.transpose(bank_[0:STACK, TOK + t * P:TOK + (t + 1) * P], xn[:, t, P:P + STACK], ident[:])
                last.then_inc(sems[done], 1)

            def project_qk(j, bank_=pa, ready="pa_ready"):
                c = slice(j * P, (j + 1) * P)
                split_product(bank_[:, 0:TOK], W_Q1, c, False)
                split_product(bank_[:, TOK:2 * TOK], W_K1, c, False).then_inc(sems[ready], 1)

            def scores(b, i):
                kind, h = plan_of(b).units[i]
                wait_n(pe, "exp_done", b, i - 1)
                bank_ = s_bank[i % 2]
                k = unit_keys(kind)
                if kind in ("self", "cross"):
                    r = slice(DH * (h % 2), DH * (h % 2) + DH)
                    if kind == "self":
                        pe.wait_ge(sems["po_taken"], count("po_taken", b, 0))
                        pe.wait_ge(sems["pa_taken"], count("pa_taken", b, max(0, h // 2 - 1)))
                    else:
                        c = h // 4
                        pe.wait_ge(sems["pa_taken"], count("pa_taken", b, filled(b, "pa", f"q2_{c}")))
                        if c >= 2:
                            pe.wait_ge(sems["pb_taken"], count("pb_taken", b, filled(b, "pb", f"k2_{c}")))
                    halves = [(part_q[r, h // 2 % QRING, 0, :], part_k[r, h // 2 % QRING, 1, :])
                              for part_q, part_k in ((qk_hi, qk_hi), (qk_lo, qk_hi), (qk_hi, qk_lo))]
                else:
                    r = slice(PADH * (h % 4), PADH * (h % 4) + DH2)
                    if kind == "ca":
                        pe.wait_ge(sems["x3_taken"], count("x3_taken", b, 0))
                        pe.wait_ge(sems["pa_taken"], count("pa_taken", b, 0))
                        halves = [(cq1T[r, h // 4, :], x3T[r, h // 4, :])]
                    else:
                        pe.wait_ge(sems["pb_taken"], count("pb_taken", b, 0))
                        halves = [(q2T[r, h // 4, :], k2T[r, h // 4, 0:KEYS2])]
                for t in range(1 if kind == "ca" else TT):
                    for n, (qs, ks) in enumerate(halves):
                        q = qs if kind == "ca" else qs[:, t * P:(t + 1) * P]
                        last = pe.matmul(bank_[0:CTX if kind == "ca" else P, t * TOK:t * TOK + k], q, ks,
                                         start=(n == 0), stop=(n == len(halves) - 1))
                last.then_inc(sems["scores_ready"], 1)

            def transposes(b, i):
                kind, _ = plan_of(b).units[i]
                q, k = unit_queries(kind), unit_keys(kind)
                pe.wait_ge(sems["norm_ready"], count("norm_ready", b, i + 1))
                wait_n(pe, "pT_ready", b, i - 1)
                tb = t_bank[i % 2]
                for c in range(2):
                    kk = min(P, k - c * P)
                    for t in range(1 if kind == "ca" else TT):
                        qq = min(q, P)
                        last = pe.transpose(tb[0:kk, c * q + t * P:c * q + t * P + qq],
                                            prob[0:qq, i % RING, t * k + c * P:t * k + c * P + kk],
                                            ident[0:qq, 0:qq])
                last.then_inc(sems["tr_ready"], 1)

            def values(b, g):
                kind, members = plan_of(b).groups[g]
                q, k = unit_queries(kind), unit_keys(kind)
                pe.wait_ge(sems["pT_ready"], count("pT_ready", b, members[-1] + 1))
                wait_n(pe, "o_ready", b, g)
                if kind in ("self", "cross"):
                    c = plan_of(b).units[members[0]][1] // 4
                    name = f"v{c}" if kind == "self" else f"v2_{c}"
                    pe.wait_ge(sems["pb_taken"], count("pb_taken", b, filled(b, "pb", name)))
                for c in range(2):
                    kk = min(P, k - c * P)
                    for i in members:
                        h = plan_of(b).units[i][1]
                        if kind in ("self", "cross"):
                            v = val[:, c, h * DH:(h + 1) * DH]
                            rows_ = slice(DH * (h % 2), DH * (h % 2) + DH)
                        else:
                            src = x3p if kind == "ca" else v2p
                            v = src[0:kk, c, h * PADH:(h + 1) * PADH]
                            rows_ = slice(PADH * (h % 4), PADH * (h % 4) + PADH)
                        last = pe.matmul(o_bank[rows_, 0:q], v, pT[0:kk, i % RINGT, c, 0:q],
                                         start=(c == 0), stop=(c == 1), skip_group_check=True)
                last.then_inc(sems["pv_ready"], 1)

            def project(b, g):
                kind, members = plan_of(b).groups[g]
                if kind not in ("self", "cross"):
                    return
                pair = plan_of(b).units[members[0]][1] // 2
                a = 0 if kind == "self" else 1
                pe.wait_ge(sems["o_ready"], count("o_ready", b, g + 1))
                if pair == 0:
                    wait_n(pe, "y_taken", b, a)
                for t in range(TT):
                    last = pe.matmul(y_bank[:, t * DIM:(t + 1) * DIM], oT[:, pair % 2, t * P:(t + 1) * P],
                                     wo[:, a * PAIRS + pair, :], start=(pair == 0 and t == 0), stop=(pair == PAIRS - 1),
                                     skip_group_check=True)
                last.then_inc(sems["wo_done"], 1)

            def stream(b, first, n, between):
                plan = plan_of(b)
                for s in range(n + LAG_O + 1):
                    if s < n:
                        scores(b, first + s)
                    if LAG_T <= s < n + LAG_T:
                        transposes(b, first + s - LAG_T)
                    between(s)
                    if LAG_V <= s < n + LAG_V and plan.ends_group(first + s - LAG_V) is not None:
                        values(b, plan.ends_group(first + s - LAG_V))
                    if LAG_O <= s < n + LAG_O and plan.ends_group(first + s - LAG_O) is not None:
                        project(b, plan.ends_group(first + s - LAG_O))

            def project_v(b, c):
                use_pb(b, f"v{c}")
                for t in range(TT):
                    last = split_product(pb[:, t * 256:(t + 1) * 256], W_V1, slice(256 * c, 256 * c + 256), True,
                                         slice(t * P, (t + 1) * P))
                last.then_inc(sems["pb_ready"], 1)

            def project_k2(b, c):
                name = qk_bank(f"k2_{c}")
                bank_, use, ready = (pa, use_pa, "pa_ready") if name == "pa" else (pb, use_pb, "pb_ready")
                use(b, f"k2_{c}")
                for i in range(2):
                    j = 2 * c + i
                    last = split_ctx(bank_[:, i * TOK:(i + 1) * TOK], 0, slice(j * P, (j + 1) * P), False)
                last.then_inc(sems[ready], 1)

            def project_v2(b, c):
                use_pb(b, f"v2_{c}")
                for t in range(TT):
                    last = split_ctx(pb[:, t * 256:(t + 1) * 256], 1, slice(256 * c, 256 * c + 256), True,
                                     slice(t * P, (t + 1) * P))
                last.then_inc(sems["pb_ready"], 1)

            def project_q2(b, c):
                use_pa(b, f"q2_{c}")
                for i in range(2):
                    j = 2 * c + i
                    last = split_product(pa[:, i * TOK:(i + 1) * TOK], W_Q2, slice(j * P, (j + 1) * P), False)
                last.then_inc(sems["pa_ready"], 1)

            def chain(b, s):
                if s == 1:
                    plan = plan_of(b)
                    pe.wait_ge(sems["o_ready"], count("o_ready", b, plan.group[len(plan.early) - 1] + 1))
                    use_pb(b, "cq2")
                    for m in range(QUADS):
                        for g in range(QUADS):
                            last = pe.matmul(pb[:, m * CTX:(m + 1) * CTX], wq2p[:, g, m * P:(m + 1) * P], hs1T[:, g, :],
                                             start=(g == 0), stop=(g == QUADS - 1))
                    last.then_inc(sems["pb_ready"], 1)
                if s == 3:
                    use_pb(b, "s2")
                    for g in range(QUADS):
                        last = pe.matmul(pb[0:CTX, g * 16:(g + 1) * 16], cq2T[:, g, :],
                                         k2bd[:, g, :, :].rearrange("p a c -> p (a c)"), start=True, stop=True)
                    last.then_inc(sems["pb_ready"], 1)
                if s == 7:
                    pe.wait_ge(sems["s2_norm"], count("s2_norm", b, 1))
                    use_pb(b, "p2T")
                    pe.matmul(pb[BELOW, 0:CTX], s2[:].rearrange("p h c -> p (h c)"), ident[0:CTX, 0:CTX],
                              start=True, stop=True)\
                      .then_inc(sems["pb_ready"], 1)
                if s == 11:
                    use_pb(b, "c2T")
                    for g in range(QUADS):
                        last = pe.matmul(pb[:, g * CTX:(g + 1) * CTX], v2bd[:, g * P:(g + 1) * P], p2T,
                                         start=True, stop=True)
                    last.then_inc(sems["pb_ready"], 1)
                if s == 15:
                    use_pb(b, "c2w")
                    for g in range(QUADS):
                        last = pe.matmul(pb[0:CTX, 0:DIM], c2T[:, g, :], woutp[:, g, :], start=(g == 0), stop=(g == QUADS - 1))
                    last.then_inc(sems["pb_ready"], 1)

            def final_projection(b):
                pe.wait_ge(sems["o_ready"], count("o_ready", b, len(plan_of(b).groups)))
                pe.wait_ge(sems["pb_taken"], count("pb_taken", b, filled(b, "pb", "c2w")))
                for t in range(TT):
                    y = y_bank[:, t * DIM:(t + 1) * DIM]
                    for g in range(QUADS):
                        pe.matmul(y, hsT[:, g, t * P:(t + 1) * P], woutp[:, g, :], start=(g == 0), stop=False)
                    last = pe.matmul(y, ex[:, t * P:(t + 1) * P], c2w, start=False, stop=True)
                last.then_inc(sems["y_ready"], 1)

            def one(b, last_one):
                plan = plan_of(b)

                def fill_end(s):
                    if s == HEADS + 1:
                        project_k2(b, 0)
                    if s == HEADS + 3:
                        project_v2(b, 0)
                    if s == HEADS + 4:
                        project_v2(b, 1)
                    if s == HEADS + 5:
                        project_k2(b, 1)
                    if s == HEADS + 8:
                        project_v2(b, 2)

                def early_between(s):
                    if pair_at(s) is not None:
                        use_pa(b, f"qk{pair_at(s)}")
                        project_qk(pair_at(s))
                    if plan is FIRST and s == 2:
                        pe.wait_ge(w_lo_ready, DONE[W_V1])
                    if plan is FIRST and s == 4:
                        pe.wait_ge(wo_loaded, 16)
                    if s % 4 == 2 and s // 4 < CHUNKS:
                        project_v(b, s // 4)
                    if s == 12:
                        pe.wait_ge(ctx_loaded, 16 * b + 16)
                        use_pb(b, "ctx")
                        for t in range(TT):
                            last = pe.transpose(pb[0:CTX, t * P:(t + 1) * P], ctx_in[:, t, :], ident[:])
                        last.then_inc(sems["pb_ready"], 1)
                    if plan is FIRST and s == HEADS:
                        pe.wait_ge(w_lo_ready, DONE[W_CTX])
                    fill_end(s)
                    if plan is not FIRST and s == len(plan.early) + LN1_AT:
                        ln_transposes(b, 1, y_bank, "xT_ready")

                def late_between(s):
                    c = s // 4
                    if s % 4 == 0 and c + 1 < CHUNKS:
                        project_q2(b, c + 1)
                    if s % 4 == 1 and 2 <= c + 1 < CHUNKS:
                        project_k2(b, c + 1)
                    if plan is not FIRST:
                        chain(b, s)
                    if plan is not FIRST and s == len(plan.late) + 1:
                        ln_transposes(b, 3, y_bank, "xT_ready")
                stream(b, 0, len(plan.early), early_between)
                for s in range(len(plan.early) + LAG_O + 1, HEADS + 10):
                    fill_end(s)
                if plan is FIRST:
                    ln_transposes(b, 1, y_bank, "xT_ready")
                project_v2(b, 3)
                if plan is FIRST:
                    pe.wait_ge(w_lo_ready, DONE[W_Q2])
                    pe.wait_ge(w_lo_ready, DONE[W_F1])
                    pe.wait_ge(small_loaded, 16 * NSMALL)
                    pe.wait_ge(l1_scaled, 2)
                pe.wait_ge(sems["lo_ready"], count("lo_ready", b, 3))
                project_q2(b, 0)
                project_v2(b, 4)
                stream(b, len(plan.early), len(plan.late), late_between)
                if plan is FIRST:
                    ln_transposes(b, 3, y_bank, "xT_ready")
                pe.wait_ge(sems["lo_ready"], count("lo_ready", b, 5))
                for j in range(FT):
                    if j == 2:
                        pe.wait_ge(sems["o_ready"], count("o_ready", b, len(plan.groups)))
                    if j >= 3:
                        pe.wait_ge(sems["ff_g_taken"], count("ff_g_taken", b, j - 2))
                    split_product(ff_g_bank[j % 3][:, 0:TOK], W_F1, slice(DFF + j * P, DFF + (j + 1) * P), False)\
                        .then_inc(sems["ff_g_ready"], 1)
                    if ff_a_bank[j % 3] is pa and j < 3:
                        use_pa(b, "keyT")
                    if j >= 3:
                        pe.wait_ge(sems["ff_a_taken"], count("ff_a_taken", b, j - 2))
                    split_product(ff_a_bank[j % 3][:, 0:TOK], W_F1, slice(j * P, (j + 1) * P), False)\
                        .then_inc(sems["ff_a_ready"], 1)
                pe.wait_ge(sems["ff_a_taken"], count("ff_a_taken", b, 3))
                for g in range(QUADS):
                    last = pe.matmul(pa[:, g * TOK:(g + 1) * TOK], wk2p[:, g * P:(g + 1) * P], cT[:], start=True, stop=True)
                last.then_inc(sems["pa_ready"], 1)
                pe.wait_ge(sems["ff_g_taken"], count("ff_g_taken", b, 3))
                for t in range(TT):
                    last = pe.matmul(o_bank[:, t * PADW:(t + 1) * PADW], cT[:, t * P:(t + 1) * P], wv2p, start=True, stop=True)
                last.then_inc(sems["v2p_ready"], 1)
                if not last_one:
                    use_pb(b, "next_ln0")
                    ln_transposes(b, 5, pb, "pb_ready")
                pe.wait_ge(sems["y_taken"], count("y_taken", b, 2))
                for j in range(FT):
                    pe.wait_ge(sems["ff_h"], count("ff_h", b, j + 1))
                    for t in range(TT):
                        last = pe.matmul(y_bank[:, t * DIM:(t + 1) * DIM], f_g[:, j, t * P:(t + 1) * P], wf2[:, j, :],
                                         start=(j == 0 and t == 0), stop=(j == FT - 1), skip_group_check=True)
                last.then_inc(sems["y_ready"], 1)
                pe.wait_ge(ca_loaded, 16 * b + 16)
                use_pa(b, "cq1T")
                for g in range(QUADS):
                    last = pe.matmul(pa[:, g * CTX:(g + 1) * CTX], wqca[:, g * P:(g + 1) * P], ca_in, start=True, stop=True)
                last.then_inc(sems["pa_ready"], 1)
                use_pb(b, "blocks")
                for g in range(QUADS):
                    pe.matmul(pb[:, g * NCA:(g + 1) * NCA], wkca[:, g * P:(g + 1) * P], cT[:, KEYS2:TOK], start=True, stop=True)
                pe.matmul(pb[BELOW, 64:64 + PADW], ca_rep[:].rearrange("p h c -> p (h c)"),
                          wvca, start=True, stop=True).then_inc(sems["pb_ready"], 1)
                pe.wait_ge(sems["y_taken"], count("y_taken", b, 3))
                for g in range(QUADS):
                    for t in range(TT):
                        last = pe.transpose(t_bank[0][:, g * TOK + t * P:g * TOK + (t + 1) * P], x3p[:, t, g * P:(g + 1) * P],
                                            ident[:])
                last.then_inc(sems["x3_ready"], 1)
                if plan is not FIRST:
                    final_projection(b)
                if not last_one:
                    use_pa(b, "next_qk0")
                    pe.wait_ge(sems["lo_ready"], count("lo_ready", b, 7))
                    project_qk(0)
                pe.wait_ge(sems["x3_taken"], count("x3_taken", b, 1))
                pe.wait_ge(sems["v2p_taken"], count("v2p_taken", b, 1))
                if not last_one:
                    project_qk(1, o_bank, "po_ready")
                use_pb(b, "q2T")
                for m in range(QUADS):
                    for g in range(QUADS):
                        last = pe.matmul(pb[:, m * TOK:(m + 1) * TOK], wq2p[:, g, m * P:(m + 1) * P], x3T[:, g, :],
                                         start=(g == 0), stop=(g == QUADS - 1))
                last.then_inc(sems["pb_ready"], 1)
            ln_transposes(0, -1, pb, "pb_ready")
            pe.wait_ge(w_lo_ready, DONE[W_K1])
            pe.wait_ge(sems["lo_ready"], 2)
            project_qk(0)
            project_qk(1, o_bank, "po_ready")
            batches(pe, one)
            stream(BATCH, 0, len(CA), lambda s: None)
            chain(BATCH, 1)
            stream(BATCH, len(CA), len(ENC), lambda s: chain(BATCH, {0: 3, 3: 7, 5: 11, 7: 15}.get(s, 0)))
            final_projection(BATCH)


_OUTS = [((BATCH, TOK, DIM), "float32")]


def kernel(**inputs):
    import concourse.bacc as _bacc
    from concourse.bass_utils import run_bass_kernel_spmd as _run

    a = {k: np.ascontiguousarray(v) for k, v in inputs.items()}

    def l0(n):
        return a["L0_xattn_" + n]

    def l1(n):
        return a["L1_xattn_" + n]

    def pad_cols(w):
        out = np.zeros((w.shape[0], HEADS2, PADH), w.dtype)
        out[:, :, :DH2] = w.reshape(w.shape[0], HEADS2, DH2)
        return out.reshape(w.shape[0], PADW)

    def pad_rows(w):
        out = np.zeros((HEADS2, PADH, w.shape[1]), w.dtype)
        out[:, :DH2] = w.reshape(HEADS2, DH2, w.shape[1])
        return out.reshape(QUADS, P, w.shape[1]).transpose(1, 0, 2)

    ws = [l0("wq1"), l0("wk1"), l0("wv1"), l0("wq2"), l0("w_ff1")]
    cols = []
    for k in (1, 2, 3):
        g, be = l0(f"g{k}"), l0(f"be{k}")
        z = np.zeros((REM,), g.dtype)
        cols += [g[:P], be[:P], np.concatenate([g[P:]] * 3 + [z]), np.concatenate([be[P:]] * 3 + [z])]
    cols += list(l0("b_ff1").reshape(2 * FT, P))
    index = np.linspace(0, CTX - 1, TOK).astype(np.int64)
    expand = np.zeros((CTX, TOK), np.float32)
    expand[index, np.arange(TOK)] = 1.0
    mask_k = np.zeros((P, 4, NCA), np.float32)
    mask_v = np.zeros((HEADS2 * NCA, HEADS2, PADH), np.float32)
    for h in range(4):
        mask_k[PADH * h:PADH * (h + 1), h] = 1.0
    for h in range(HEADS2):
        mask_v[NCA * h:NCA * (h + 1), h] = 1.0
    arrays = dict(
        x=a["x"], ctx=a["ctx_768"],
        w_main=np.stack([w[:P] for w in ws]),
        w_rem=np.stack([np.concatenate([w[P:]] * 3) for w in ws]),
        w_ctx=np.stack([l0("wk2"), l0("wv2")]),
        w_o=np.stack([l0("wo1"), l0("wo2")]),
        w_f2=l0("w_ff2"),
        wq_p=pad_rows(pad_cols(l1("Wq"))), wk_p=pad_cols(l1("Wk")), wv_p=pad_cols(l1("Wv")),
        wqca_p=pad_cols(l1("Wq_ca")), wkca_p=pad_cols(l1("Wk_ca")), wvca_p=pad_cols(l1("Wv_ca")),
        wout_p=pad_rows(l1("Wout")),
        cols=np.stack(cols, axis=1),
        rows=np.stack([l0("bo1"), l0("bo2"), l0("b_ff2"), l1("b_out")])[None],
        expand=expand, mask_k=mask_k, mask_v=mask_v.reshape(HEADS2 * NCA, PADW))
    nc = _bacc.Bacc("TRN2", target_bir_lowering=False, num_devices=1)
    aps, feed = {}, {}
    for name, v in arrays.items():
        v = np.ascontiguousarray(v)
        feed[f"in_{name}"] = v
        aps[name] = nc.dram_tensor(f"in_{name}", v.shape, mybir.dt.from_np(v.dtype), kind="ExternalInput").ap()
    out = nc.dram_tensor("out_0", _OUTS[0][0], F32, kind="ExternalOutput").ap()
    build(nc, out=out, **aps)
    r = _run(nc, [feed], core_ids=[0])
    return r.results[0]["out_0"]
```
